# Optimizing a Trainium2 kernel written in Bass

```python
import numpy as np
import jax
import jax.numpy as jnp

def _softmax(x, axis=-1):
    return jax.nn.softmax(x, axis=axis)

def _gelu(x):
    return jax.nn.gelu(x, approximate=True)

def _silu(x):
    return jax.nn.silu(x)

def _sigmoid(x):
    return jax.nn.sigmoid(x)

def _layernorm(x, axis=-1, eps=1e-05):
    m = jnp.mean(x, axis=axis, keepdims=True)
    v = jnp.var(x, axis=axis, keepdims=True)
    return (x - m) / jnp.sqrt(v + eps)

def _scatter_add(tgt, idx, src, axis=0):
    return tgt.at[idx].add(src)

def _segment_sum(src, seg, n):
    return jax.ops.segment_sum(src, seg, n)
kernel_name = 'mk_prb_d2_jaxref_r8_12018e'

def setup_inputs(seed: int=0):
    np.random.seed(seed)
    _w = jnp.asarray

    def _L0_attn_setup():
        import jax, jax.numpy as jnp
        import numpy as np
        EMBED_DIM = 128
        NUM_HEADS = 16
        HEAD_DIM = EMBED_DIM // NUM_HEADS
        key = jax.random.key(seed)
        k0, k1, k2, k3, k4 = jax.random.split(key, 5)
        B, S = (1, 512)
        scale = 1.0 / np.sqrt(EMBED_DIM)
        x = jax.random.normal(k0, (B, S, EMBED_DIM), dtype=jnp.float32)
        Wqkv = jax.random.normal(k1, (EMBED_DIM, 3 * EMBED_DIM), dtype=jnp.float32) * scale
        bqkv = jax.random.normal(k2, (3 * EMBED_DIM,), dtype=jnp.float32) * 0.02
        Wout = jax.random.normal(k3, (EMBED_DIM, EMBED_DIM), dtype=jnp.float32) * scale
        bout = jax.random.normal(k4, (EMBED_DIM,), dtype=jnp.float32) * 0.02
        return {'x': x, 'Wqkv': Wqkv, 'bqkv': bqkv, 'Wout': Wout, 'bout': bout}
    _L0_attn_in = _L0_attn_setup()

    def _L0_ffn_setup():
        import jax, jax.numpy as jnp
        import numpy as np

        def _bitlinear(x, w_latent):
            scale = jax.lax.stop_gradient(jnp.clip(jnp.mean(jnp.abs(w_latent), axis=1, keepdims=True), 1e-05, None))
            tern = jnp.clip(jnp.round(w_latent / scale), -1.0, 1.0)
            w = w_latent + jax.lax.stop_gradient(tern - w_latent)
            return x @ (w * scale).T
        key = jax.random.key(seed)
        ks = jax.random.split(key, 6)
        dim, hidden, rank = (128, 512, 16)
        B, S = (4, 512)
        x = jax.random.normal(ks[0], (B, S, dim), dtype=jnp.float32)
        w_fc = 0.02 * jax.random.normal(ks[1], (hidden, dim), dtype=jnp.float32)
        w_proj = 0.02 * jax.random.normal(ks[2], (dim, hidden), dtype=jnp.float32)
        u = 0.02 * jax.random.normal(ks[3], (hidden, rank), dtype=jnp.float32)
        v = 0.02 * jax.random.normal(ks[4], (rank, dim), dtype=jnp.float32)
        fast_b = jax.random.normal(ks[5], (rank, rank), dtype=jnp.float32)
        gate = jnp.float32(0.05)
        return {'x': x, 'fast_b': fast_b, 'w_fc': w_fc, 'w_proj': w_proj, 'u': u, 'v': v, 'gate': gate}
    _L0_ffn_in = _L0_ffn_setup()

    def _L1_attn_setup():
        import jax, jax.numpy as jnp
        import numpy as np
        D_MODEL = 128
        N_HEADS = 16
        HEAD_DIM = D_MODEL // N_HEADS
        ROPE_THETA = 10000.0
        EPS = 1e-06
        PAD_VAL = 1.0

        def _rope(x, cos, sin):
            x1 = x[..., 0::2]
            x2 = x[..., 1::2]
            r1 = x1 * cos - x2 * sin
            r2 = x1 * sin + x2 * cos
            return jnp.stack([r1, r2], axis=-1).reshape(x.shape)
        key = jax.random.key(seed)
        ks = jax.random.split(key, 5)
        w_scale = 1.0 / np.sqrt(D_MODEL)
        return {'x': jax.random.normal(ks[0], (4, 512, D_MODEL), jnp.float32), 'Wq': jax.random.normal(ks[1], (D_MODEL, D_MODEL), jnp.float32) * w_scale, 'Wk': jax.random.normal(ks[2], (D_MODEL, D_MODEL), jnp.float32) * w_scale, 'Wv': jax.random.normal(ks[3], (D_MODEL, D_MODEL), jnp.float32) * w_scale, 'Wo': jax.random.normal(ks[4], (D_MODEL, D_MODEL), jnp.float32) * w_scale}
    _L1_attn_in = _L1_attn_setup()

    def _L1_ffn_setup():
        import jax, jax.numpy as jnp
        import numpy as np
        EMBED = 128
        HEADS = 16
        HEAD_DIM = EMBED // HEADS
        NUM_EXPERTS = 8
        TOP_K = 2
        HIDDEN = (int(2 * (4 * EMBED) / 3) + 63) // 64 * 64
        SEQ = 256
        BATCH = 2
        ROPE_BASE = 10000.0
        EPS = 1e-06

        def _rope_tables(seq_len, dim):
            inv_freq = 1.0 / ROPE_BASE ** (np.arange(0, dim, 2, dtype=np.float32) / dim)
            t = np.arange(seq_len, dtype=np.float32)
            freqs = np.einsum('i,j->ij', t, inv_freq)
            emb = np.concatenate([freqs, freqs], axis=-1)
            return (jnp.asarray(np.cos(emb)), jnp.asarray(np.sin(emb)))

        def _rotate_half(x):
            x1, x2 = jnp.split(x, 2, axis=-1)
            return jnp.concatenate([-x2, x1], axis=-1)

        def _rmsnorm(x, w):
            return x * jax.lax.rsqrt(jnp.mean(x * x, axis=-1, keepdims=True) + EPS) * w

        def _attention(x, wq, wk, wv, wo):
            B, S, _ = x.shape
            q = (x @ wq).reshape(B, S, HEADS, HEAD_DIM).transpose(0, 2, 1, 3)
            k = (x @ wk).reshape(B, S, HEADS, HEAD_DIM).transpose(0, 2, 1, 3)
            v = (x @ wv).reshape(B, S, HEADS, HEAD_DIM).transpose(0, 2, 1, 3)
            cos, sin = _rope_tables(S, HEAD_DIM)
            cos = cos[None, None]
            sin = sin[None, None]
            q = q * cos + _rotate_half(q) * sin
            k = k * cos + _rotate_half(k) * sin
            scale = HEAD_DIM ** (-0.5)
            scores = jnp.einsum('bhqd,bhkd->bhqk', q, k) * scale
            causal = jnp.triu(jnp.ones((S, S), bool), k=1)
            scores = jnp.where(causal, -jnp.inf, scores)
            attn = jax.nn.softmax(scores, axis=-1)
            out = jnp.einsum('bhqk,bhkd->bhqd', attn, v)
            out = out.transpose(0, 2, 1, 3).reshape(B, S, EMBED)
            return out @ wo

        def _moe(x, w_router, wg, wu, wd):
            B, S, E = x.shape
            xf = x.reshape(-1, E)
            logits = xf @ w_router
            probs = jax.nn.softmax(logits, axis=-1)
            topw, topi = jax.lax.top_k(probs, TOP_K)
            topw = topw / jnp.sum(topw, axis=-1, keepdims=True)
            combine = jnp.sum(jax.nn.one_hot(topi, NUM_EXPERTS, dtype=xf.dtype) * topw[..., None], axis=1)
            g = jax.nn.silu(jnp.einsum('td,xdh->txh', xf, wg))
            u = jnp.einsum('td,xdh->txh', xf, wu)
            eo = jnp.einsum('txh,xhd->txd', g * u, wd)
            out = jnp.einsum('txd,tx->td', eo, combine)
            return out.reshape(B, S, E)
        key = jax.random.key(seed)
        ks = jax.random.split(key, 12)
        s = 0.02
        return {'x': jax.random.normal(ks[0], (BATCH, SEQ, EMBED), jnp.float32), 'wq': jax.random.normal(ks[1], (EMBED, EMBED), jnp.float32) * s, 'wk': jax.random.normal(ks[2], (EMBED, EMBED), jnp.float32) * s, 'wv': jax.random.normal(ks[3], (EMBED, EMBED), jnp.float32) * s, 'wo': jax.random.normal(ks[4], (EMBED, EMBED), jnp.float32) * s, 'w_router': jax.random.normal(ks[5], (EMBED, NUM_EXPERTS), jnp.float32) * s, 'wg': jax.random.normal(ks[6], (NUM_EXPERTS, EMBED, HIDDEN), jnp.float32) * s, 'wu': jax.random.normal(ks[7], (NUM_EXPERTS, EMBED, HIDDEN), jnp.float32) * s, 'wd': jax.random.normal(ks[8], (NUM_EXPERTS, HIDDEN, EMBED), jnp.float32) * s, 'g1': jnp.ones((EMBED,), jnp.float32), 'g2': jnp.ones((EMBED,), jnp.float32)}
    _L1_ffn_in = _L1_ffn_setup()
    _d = {'L0_attn_x': _L0_attn_in['x'], 'L0_attn_Wqkv': _L0_attn_in['Wqkv'], 'L0_attn_bqkv': _L0_attn_in['bqkv'], 'L0_attn_Wout': _L0_attn_in['Wout'], 'L0_attn_bout': _L0_attn_in['bout'], 'L0_ffn_fast_b': _L0_ffn_in['fast_b'], 'L0_ffn_w_fc': _L0_ffn_in['w_fc'], 'L0_ffn_w_proj': _L0_ffn_in['w_proj'], 'L0_ffn_u': _L0_ffn_in['u'], 'L0_ffn_v': _L0_ffn_in['v'], 'L0_ffn_gate': _L0_ffn_in['gate'], 'L1_attn_Wq': _L1_attn_in['Wq'], 'L1_attn_Wk': _L1_attn_in['Wk'], 'L1_attn_Wv': _L1_attn_in['Wv'], 'L1_attn_Wo': _L1_attn_in['Wo'], 'L1_ffn_wq': _L1_ffn_in['wq'], 'L1_ffn_wk': _L1_ffn_in['wk'], 'L1_ffn_wv': _L1_ffn_in['wv'], 'L1_ffn_wo': _L1_ffn_in['wo'], 'L1_ffn_w_router': _L1_ffn_in['w_router'], 'L1_ffn_wg': _L1_ffn_in['wg'], 'L1_ffn_wu': _L1_ffn_in['wu'], 'L1_ffn_wd': _L1_ffn_in['wd'], 'L1_ffn_g1': _L1_ffn_in['g1'], 'L1_ffn_g2': _L1_ffn_in['g2']}
    _x0 = _d['L0_attn_x']
    _d['L0_attn_x'] = jax.random.normal(jax.random.fold_in(jax.random.key(seed), 1), (1, 2048, 128), dtype=_x0.dtype)
    del _x0
    return _d

def reference(L0_attn_x, L0_attn_Wqkv, L0_attn_bqkv, L0_attn_Wout, L0_attn_bout, L0_ffn_fast_b, L0_ffn_w_fc, L0_ffn_w_proj, L0_ffn_u, L0_ffn_v, L0_ffn_gate, L1_attn_Wq, L1_attn_Wk, L1_attn_Wv, L1_attn_Wo, L1_ffn_wq, L1_ffn_wk, L1_ffn_wv, L1_ffn_wo, L1_ffn_w_router, L1_ffn_wg, L1_ffn_wu, L1_ffn_wd, L1_ffn_g1, L1_ffn_g2):

    def _L0_attn_ref(x, Wqkv, bqkv, Wout, bout):
        import jax, jax.numpy as jnp
        import numpy as np
        EMBED_DIM = 128
        NUM_HEADS = 16
        HEAD_DIM = EMBED_DIM // NUM_HEADS
        B, S, E = x.shape
        H, D = (NUM_HEADS, HEAD_DIM)
        qkv = x @ Wqkv + bqkv
        qkv = qkv.reshape(B, S, 3, H, D)
        q, k, v = (qkv[:, :, 0], qkv[:, :, 1], qkv[:, :, 2])
        softmax_scale = 1.0 / np.sqrt(D)
        scores = jnp.einsum('bthd,bshd->bhts', q, k * softmax_scale)
        causal_mask = jnp.triu(jnp.full((S, S), -10000.0, dtype=scores.dtype), 1)
        scores = scores + causal_mask
        attention = jax.nn.softmax(scores, axis=-1)
        context = jnp.einsum('bhts,bshd->bthd', attention, v)
        out = context.reshape(B, S, E) @ Wout + bout
        return out

    def _L0_ffn_ref(x, fast_b, w_fc, w_proj, u, v, gate):
        import jax, jax.numpy as jnp
        import numpy as np

        def _bitlinear(x, w_latent):
            scale = jax.lax.stop_gradient(jnp.clip(jnp.mean(jnp.abs(w_latent), axis=1, keepdims=True), 1e-05, None))
            tern = jnp.clip(jnp.round(w_latent / scale), -1.0, 1.0)
            w = w_latent + jax.lax.stop_gradient(tern - w_latent)
            return x @ (w * scale).T
        h = _bitlinear(x, w_fc) + gate * (x @ v.T @ fast_b.T @ u.T)
        r = jnp.maximum(h, 0.0)
        return _bitlinear(r * r, w_proj)

    def _L1_attn_ref(x, Wq, Wk, Wv, Wo):
        import jax, jax.numpy as jnp
        import numpy as np
        D_MODEL = 128
        N_HEADS = 16
        HEAD_DIM = D_MODEL // N_HEADS
        ROPE_THETA = 10000.0
        EPS = 1e-06
        PAD_VAL = 1.0

        def _rope(x, cos, sin):
            x1 = x[..., 0::2]
            x2 = x[..., 1::2]
            r1 = x1 * cos - x2 * sin
            r2 = x1 * sin + x2 * cos
            return jnp.stack([r1, r2], axis=-1).reshape(x.shape)
        B, S, D = x.shape

        def split_heads(t):
            return t.reshape(B, S, N_HEADS, HEAD_DIM).transpose(0, 2, 1, 3)
        q = split_heads(x @ Wq)
        k = split_heads(x @ Wk)
        v = split_heads(x @ Wv)
        freqs = 1.0 / ROPE_THETA ** (jnp.arange(0, HEAD_DIM, 2, dtype=jnp.float32) / HEAD_DIM)
        ang = jnp.arange(S, dtype=jnp.float32)[:, None] * freqs[None, :]
        cos = jnp.cos(ang)[None, None]
        sin = jnp.sin(ang)[None, None]
        q = _rope(q, cos, sin)
        k = _rope(k, cos, sin)
        q = jax.nn.relu(q)
        k = jax.nn.relu(k)
        v_pad = jnp.pad(v, ((0, 0), (0, 0), (0, 0), (0, 1)), constant_values=PAD_VAL)
        vk = jnp.einsum('bhke,bhkd->bhed', v_pad, k)
        num = jnp.einsum('bhed,bhld->bhle', vk, q)
        attn = num[..., :-1] / (num[..., -1:] + EPS)
        out = attn.transpose(0, 2, 1, 3).reshape(B, S, D)
        return out @ Wo

    def _L1_ffn_ref(x, wq, wk, wv, wo, w_router, wg, wu, wd, g1, g2):
        import jax, jax.numpy as jnp
        import numpy as np
        EMBED = 128
        HEADS = 16
        HEAD_DIM = EMBED // HEADS
        NUM_EXPERTS = 8
        TOP_K = 2
        HIDDEN = (int(2 * (4 * EMBED) / 3) + 63) // 64 * 64
        SEQ = 256
        BATCH = 2
        ROPE_BASE = 10000.0
        EPS = 1e-06

        def _rope_tables(seq_len, dim):
            inv_freq = 1.0 / ROPE_BASE ** (np.arange(0, dim, 2, dtype=np.float32) / dim)
            t = np.arange(seq_len, dtype=np.float32)
            freqs = np.einsum('i,j->ij', t, inv_freq)
            emb = np.concatenate([freqs, freqs], axis=-1)
            return (jnp.asarray(np.cos(emb)), jnp.asarray(np.sin(emb)))

        def _rotate_half(x):
            x1, x2 = jnp.split(x, 2, axis=-1)
            return jnp.concatenate([-x2, x1], axis=-1)

        def _rmsnorm(x, w):
            return x * jax.lax.rsqrt(jnp.mean(x * x, axis=-1, keepdims=True) + EPS) * w

        def _attention(x, wq, wk, wv, wo):
            B, S, _ = x.shape
            q = (x @ wq).reshape(B, S, HEADS, HEAD_DIM).transpose(0, 2, 1, 3)
            k = (x @ wk).reshape(B, S, HEADS, HEAD_DIM).transpose(0, 2, 1, 3)
            v = (x @ wv).reshape(B, S, HEADS, HEAD_DIM).transpose(0, 2, 1, 3)
            cos, sin = _rope_tables(S, HEAD_DIM)
            cos = cos[None, None]
            sin = sin[None, None]
            q = q * cos + _rotate_half(q) * sin
            k = k * cos + _rotate_half(k) * sin
            scale = HEAD_DIM ** (-0.5)
            scores = jnp.einsum('bhqd,bhkd->bhqk', q, k) * scale
            causal = jnp.triu(jnp.ones((S, S), bool), k=1)
            scores = jnp.where(causal, -jnp.inf, scores)
            attn = jax.nn.softmax(scores, axis=-1)
            out = jnp.einsum('bhqk,bhkd->bhqd', attn, v)
            out = out.transpose(0, 2, 1, 3).reshape(B, S, EMBED)
            return out @ wo

        def _moe(x, w_router, wg, wu, wd):
            B, S, E = x.shape
            xf = x.reshape(-1, E)
            logits = xf @ w_router
            probs = jax.nn.softmax(logits, axis=-1)
            topw, topi = jax.lax.top_k(probs, TOP_K)
            topw = topw / jnp.sum(topw, axis=-1, keepdims=True)
            combine = jnp.sum(jax.nn.one_hot(topi, NUM_EXPERTS, dtype=xf.dtype) * topw[..., None], axis=1)
            g = jax.nn.silu(jnp.einsum('td,xdh->txh', xf, wg))
            u = jnp.einsum('td,xdh->txh', xf, wu)
            eo = jnp.einsum('txh,xhd->txd', g * u, wd)
            out = jnp.einsum('txd,tx->td', eo, combine)
            return out.reshape(B, S, E)
        h = x + _attention(_rmsnorm(x, g1), wq, wk, wv, wo)
        y = h + _moe(_rmsnorm(h, g2), w_router, wg, wu, wd)
        return y
    x = L0_attn_x
    xn = _layernorm(x, axis=-1)
    x = x + _L0_attn_ref(xn, L0_attn_Wqkv, L0_attn_bqkv, L0_attn_Wout, L0_attn_bout) + _L0_ffn_ref(xn, L0_ffn_fast_b, L0_ffn_w_fc, L0_ffn_w_proj, L0_ffn_u, L0_ffn_v, L0_ffn_gate)
    xn = _layernorm(x, axis=-1)
    x = x + _L1_attn_ref(xn, L1_attn_Wq, L1_attn_Wk, L1_attn_Wv, L1_attn_Wo) + _L1_ffn_ref(xn, L1_ffn_wq, L1_ffn_wk, L1_ffn_wv, L1_ffn_wo, L1_ffn_w_router, L1_ffn_wg, L1_ffn_wu, L1_ffn_wd, L1_ffn_g1, L1_ffn_g2)
    return x

_drawn_inputs = setup_inputs


def setup_inputs(seed=0):
    import zlib

    import numpy as np

    out = dict(_drawn_inputs(seed))
    spreads = {'L1_ffn_g1': (1.0, 0.6), 'L1_ffn_g2': (1.0, 0.6)}
    factors = {'L0_ffn_fast_b': 8.0,
     'L0_ffn_w_fc': 4.325,
     'L0_ffn_w_proj': 3.259,
     'L0_ffn_u': 8.0,
     'L0_ffn_v': 8.0,
     'L1_attn_Wq': 3.906,
     'L1_attn_Wk': 3.041,
     'L1_ffn_wq': 8.0,
     'L1_ffn_wk': 8.0,
     'L1_ffn_wv': 8.0,
     'L1_ffn_wo': 8.0,
     'L1_ffn_w_router': 8.0,
     'L1_ffn_wg': 8.0,
     'L1_ffn_wu': 8.0,
     'L1_ffn_wd': 8.0}
    for name, (base, spread) in spreads.items():
        noise = np.random.default_rng([zlib.crc32(name.encode()), seed]).standard_normal(out[name].shape)
        drawn = base * np.exp(spread * noise) if base else spread * noise
        out[name] = jnp.asarray(drawn.astype(out[name].dtype))
    for name, factor in factors.items():
        out[name] = (out[name] * factor).astype(out[name].dtype)
    return out
```

```python
from contextlib import ExitStack

import numpy as np

import concourse.bass as bass
from concourse import mybir

P = 128
S = 2048
T = S // P
H, D = 16, 8
HQ = 4
NQ = H // HQ
CH = 512
NC = S // CH
TC = CH // P
E = 8
HID = 384
HC = HID // P
F0 = 512
RANK = 16
STACK = 8 * D
KROWS = 96
Q_PARTS = (0, 1, 2, 0, 1, 2, 0, 1)
K_PARTS = (0, 0, 0, 1, 1, 1, 2, 2)
SM_SCALE = float(1.0 / np.sqrt(D))

F32 = mybir.dt.float32
BF16 = mybir.dt.bfloat16
ALU = mybir.AluOpType
ACT = mybir.ActivationFunctionType
AX = mybir.AxisListType
FLOOR = -3.0e38
MASKED = -1.0e30

GROUPS = [(c, t) for c in range(NC) for t in range(TC * (c + 1))]
NG = len(GROUPS)
DIAG = [k for k, (c, t) in enumerate(GROUPS) if t >= TC * c]
LAST = [max(k for k, (c, t) in enumerate(GROUPS) if c == cc) for cc in range(NC)]
UNITS = [(g, i, kc) for g in range(HQ) for i in range(T) for kc in range(i // TC + 1)]
NU = len(UNITS) + 2
A_FROM, A_PER = 5, 5
A_TAIL = A_FROM + (len(UNITS) + A_PER - 1) // A_PER + 1
RING = 4
assert A_TAIL < NG and NG % RING == 0 and NU % 2 == 0


def first_pass_share(step, alone):
    if alone:
        return list(range(NU)) if step == 0 else []
    if step == A_TAIL:
        return [NU - 2, NU - 1]
    a = (step - A_FROM) * A_PER
    return [u for u in range(a, a + A_PER) if 0 <= u < len(UNITS)]


class Chain:

    def __init__(self, eng, sem):
        self.eng, self.sem, self.n = eng, sem, 0

    def then(self, ins):
        self.n += 1
        ins.then_inc(self.sem, 1)
        self.eng.wait_ge(self.sem, self.n)


class Core:

    def __init__(self, nc, ctx):
        self.nc, self.ctx = nc, ctx

    def sb(self, name, shape, dt=F32):
        return self.ctx.enter_context(self.nc.sbuf_tensor(name, shape, dt))

    def sem(self, name):
        return self.ctx.enter_context(self.nc.semaphore(name))

    def dram(self, name, shape, dt):
        return self.nc.dram_tensor(name, shape, dt, kind="Internal").ap()


def fresh(eng, value, most):
    if value is None or isinstance(value, int):
        return value
    with eng.register() as reg:
        eng.reg_mov(reg, value)
        return eng.snap(reg, min_val=0, max_val=most)


def wait_apart(eng, sem, value, ticks):
    eng.wait_ge(sem, value)
    eng.sem_inc(ticks, 1)


def load(nc, core, tag, pairs):
    landed = core.sem(f"{tag}_landed")
    with nc.Block() as block:
        @block.sync
        def _(sp):
            for dst, src in pairs[0::2]:
                sp.dma_start(dst, src).then_inc(landed, 16)
            sp.wait_ge(landed, 16 * len(pairs))

        @block.scalar
        def _(act):
            for dst, src in pairs[1::2]:
                act.dma_start(dst, src).then_inc(landed, 16)


def constants(nc, core, c):
    made = core.sem("const_made")
    with nc.Block() as block:
        @block.gpsimd
        def _(pool):
            ch = Chain(pool, made)
            ch.then(pool.memset(c["ident"][:], 0.0))
            ch.then(pool.memset(c["identb"][:], 0.0))
            ch.then(pool.memset(c["future"][:], 0.0))
            ch.then(pool.affine_select(out=c["ident"][:], in_=c["ident"][:], compare_op=ALU.not_equal, fill=1.0,
                                       base=0, pattern=[[-1, P]], channel_multiplier=1))
            ch.then(pool.affine_select(out=c["identb"][:], in_=c["identb"][:], compare_op=ALU.not_equal, fill=1.0,
                                       base=0, pattern=[[-1, P]], channel_multiplier=1))
            ch.then(pool.affine_select(out=c["future"][:], in_=c["future"][:], compare_op=ALU.is_ge, fill=MASKED,
                                       base=0, pattern=[[-1, P]], channel_multiplier=1))


def norm_transpose(nc, core, ps, ident, tag, src, tok, cols, rms_gain=None, eps=1e-5):
    st = core.sb(f"{tag}_st", [P, T, 6])
    mv = core.sb(f"{tag}_mv", [P, T, 2])
    var = core.sb(f"{tag}_var", [P, T])
    root = core.sb(f"{tag}_root", [P, T])
    rstd = core.sb(f"{tag}_rstd", [P, T])
    chain = core.sem(f"{tag}_chain")
    var_ready, root_ready = core.sem(f"{tag}_var"), core.sem(f"{tag}_root")
    tok_ready, transposed, moved = core.sem(f"{tag}_tok"), core.sem(f"{tag}_tr"), core.sem(f"{tag}_moved")
    with nc.Block() as block:
        @block.vector
        def _(dve):
            ch = Chain(dve, chain)
            for t in range(T):
                last = dve.bn_stats(st[:, t, :], src[:, t, :])
            ch.then(last)
            for t in range(T):
                last = dve.bn_aggr(mv[:, t, :], st[:, t, :])
            ch.then(last)
            if rms_gain is None:
                dve.tensor_scalar(var[:], mv[:, :, 1], eps, None, ALU.add).then_inc(var_ready, 1)
            else:
                ch.then(dve.tensor_tensor(var[:], mv[:, :, 0], mv[:, :, 0], ALU.mult))
                dve.scalar_tensor_tensor(out=var[:], in0=mv[:, :, 1], scalar=eps, in1=var[:],
                                         op0=ALU.add, op1=ALU.add).then_inc(var_ready, 1)
            dve.wait_ge(root_ready, 1)
            ch.then(dve.reciprocal(rstd[:], root[:]))
            for t in range(T):
                if rms_gain is None:
                    dve.tensor_scalar(tok[:, t, :], src[:, t, :], mv[:, t, 0:1], rstd[:, t:t + 1],
                                      ALU.subtract, ALU.mult).then_inc(tok_ready, 1)
                else:
                    dve.scalar_tensor_tensor(out=tok[:, t, :], in0=src[:, t, :], scalar=rstd[:, t:t + 1],
                                             in1=rms_gain[:], op0=ALU.mult, op1=ALU.mult).then_inc(tok_ready, 1)

        @block.scalar
        def _(act):
            act.wait_ge(var_ready, 1)
            act.activation(root[:], var[:], ACT.Sqrt).then_inc(root_ready, 1)
            for n in range(NC):
                act.wait_ge(transposed, n + 1)
                act.copy(cols[:, n * CH:(n + 1) * CH], ps[:, n, :]).then_inc(moved, 1)

        @block.tensor
        def _(pe):
            for t in range(T):
                pe.wait_ge(tok_ready, t + 1)
                ins = pe.transpose(ps[:, t // TC, (t % TC) * P:(t % TC + 1) * P], tok[:, t, :], ident[:])
                if t % TC == TC - 1:
                    ins.then_inc(transposed, 1)


def split_parts(dve, ch, src, parts, rest):
    ch.then(dve.tensor_copy(parts[:, 0, :], src))
    ch.then(dve.tensor_tensor(rest, src, parts[:, 0, :], ALU.subtract))
    ch.then(dve.tensor_copy(parts[:, 1, :], rest))
    ch.then(dve.tensor_tensor(rest, rest, parts[:, 1, :], ALU.subtract))
    return dve.tensor_copy(parts[:, 2, :], rest)


def project_values(pe, ps, cols, wv, ready, free, v):
    for n in range(NC):
        for i in range(TC):
            t = n * TC + i
            ins = pe.matmul(ps[:, 4 + n, i * P:(i + 1) * P], cols[:, t * P:(t + 1) * P], wv, start=True, stop=True)
        ins.then_inc(ready, 1)


def qkv_plain(nc, core, ps, tag, cols, wqkv, bias, bias_v, values, parts_dram):
    flat = core.sb(f"{tag}_qk", [P, 2, S])
    rest = core.sb(f"{tag}_rest", [P, S])
    parts = core.sb(f"{tag}_parts", [P, 2, 3, S], BF16)
    biask = core.sb(f"{tag}_biask", [P, 1])
    mm, moved, chain = core.sem(f"{tag}_mm"), core.sem(f"{tag}_moved"), core.sem(f"{tag}_chain")
    vmm, kb, split, stored = core.sem(f"{tag}_vmm"), core.sem(f"{tag}_kb"), core.sem(f"{tag}_split"), core.sem(f"{tag}_stored")
    with nc.Block() as block:
        @block.tensor
        def _(pe):
            for x in range(2):
                for n in range(NC):
                    if x:
                        pe.wait_ge(moved, n + 1)
                    pe.matmul(ps[:, n, :], wqkv[:, x * P:(x + 1) * P], cols[:, n * CH:(n + 1) * CH],
                              start=True, stop=True).then_inc(mm, 1)
            project_values(pe, ps, cols, wqkv[:, 2 * P:3 * P], vmm, None, None)

        @block.scalar
        def _(act):
            act.wait_ge(kb, 1)
            for x in range(2):
                for n in range(NC):
                    act.wait_ge(mm, x * NC + n + 1)
                    act.activation(flat[:, x, n * CH:(n + 1) * CH], ps[:, n, :], ACT.Identity,
                                   bias=(biask[:] if x else bias[:, 0:1]),
                                   scale=(SM_SCALE if x else 1.0)).then_inc(moved, 1)

        @block.vector
        def _(dve):
            ch = Chain(dve, chain)
            dve.tensor_scalar(biask[:], bias[:, 1:2], SM_SCALE, None, ALU.mult).then_inc(kb, 1)
            for x in range(2):
                dve.wait_ge(moved, NC * (x + 1))
                split_parts(dve, ch, flat[:, x, :], parts[:, x], rest[:]).then_inc(split, 1)
            for n in range(NC):
                dve.wait_ge(vmm, n + 1)
                dve.tensor_tensor(values[:, n * TC:(n + 1) * TC, :],
                                  ps[:, 4 + n, :].rearrange("p (a b) -> p a b", a=TC),
                                  bias_v[:].rearrange("p (o b) -> p o b", o=1).to_broadcast([P, TC, P]), ALU.add)

        @block.sync
        def _(sp):
            for x in range(2):
                sp.wait_ge(split, x + 1)
                sp.dma_start(parts_dram[x].rearrange("a p t -> p a t"), parts[:, x]).then_inc(stored, 16)
            sp.wait_ge(stored, 32)


def qkv_rope(nc, core, ps, tag, cols, wq, wqr, wk, wkr, wv, cos, sin, values, finish, k_scale, parts_dram=None,
             out=None):
    flat = out if out is not None else core.sb(f"{tag}_qk", [P, 2, S])
    turn = core.sb(f"{tag}_turn", [P, S])
    mm, used, chain = core.sem(f"{tag}_mm"), core.sem(f"{tag}_used"), core.sem(f"{tag}_chain")
    vmm, split, stored = core.sem(f"{tag}_vmm"), core.sem(f"{tag}_split"), core.sem(f"{tag}_stored")
    vmoved = core.sem(f"{tag}_vmoved")
    parts = core.sb(f"{tag}_parts", [P, 2, 3, S], BF16) if parts_dram is not None else None
    with nc.Block() as block:
        @block.tensor
        def _(pe):
            for x, (w, wr) in enumerate(((wq, wqr), (wk, wkr))):
                for n in range(NC):
                    u = x * NC + n
                    if u >= 2:
                        pe.wait_ge(used, 2 * (u - 1))
                    for y, ww in enumerate((w, wr)):
                        ins = pe.matmul(ps[:, 2 * (u % 2) + y, :], ww, cols[:, n * CH:(n + 1) * CH],
                                        start=True, stop=True)
                    ins.then_inc(mm, 1)
            project_values(pe, ps, cols, wv, vmm, None, None)

        @block.vector
        def _(dve):
            ch = Chain(dve, chain)
            for x in range(2):
                s = k_scale if x else 1.0
                for n in range(NC):
                    u = x * NC + n
                    sl = slice(n * CH, (n + 1) * CH)
                    dve.wait_ge(mm, u + 1)
                    dve.scalar_tensor_tensor(out=flat[:, x, sl], in0=ps[:, 2 * (u % 2), :], scalar=s,
                                             in1=cos[:, sl], op0=ALU.mult, op1=ALU.mult).then_inc(used, 1)
                    dve.scalar_tensor_tensor(out=turn[:, sl], in0=ps[:, 2 * (u % 2) + 1, :], scalar=s,
                                             in1=sin[:, sl], op0=ALU.mult, op1=ALU.mult).then_inc(used, 1)
                dve.wait_ge(used, 2 * NC * (x + 1))
                ch.then(dve.tensor_tensor(flat[:, x, :], flat[:, x, :], turn[:], ALU.add))
                if finish == "relu":
                    ch.then(dve.tensor_scalar(flat[:, x, :], flat[:, x, :], 0.0, None, ALU.max))
                else:
                    split_parts(dve, ch, flat[:, x, :], parts[:, x], turn[:]).then_inc(split, 1)
                    dve.wait_ge(split, x + 1)

        @block.scalar
        def _(act):
            for n in range(NC):
                act.wait_ge(vmm, n + 1)
                act.copy(values[:, n * TC:(n + 1) * TC, :],
                         ps[:, 4 + n, :].rearrange("p (a b) -> p a b", a=TC)).then_inc(vmoved, 1)

        if parts_dram is not None:
            @block.sync
            def _(sp):
                for x in range(2):
                    sp.wait_ge(split, x + 1)
                    sp.dma_start(parts_dram[x].rearrange("a p t -> p a t"), parts[:, x]).then_inc(stored, 16)
                sp.wait_ge(stored, 32)


def attention(nc, core, ps, tag, parts_dram, values, c, ctxu, scratch):
    qs = core.sb(f"{tag}_qs", [P, 2, HQ, S], BF16)
    ks = core.sb(f"{tag}_ks", [P, 2, HQ, S], BF16)
    probs = core.sb(f"{tag}_probs", [P, RING, HQ, CH])
    vq = core.sb(f"{tag}_vq", [P, T, HQ, 32])
    part_max = core.sb(f"{tag}_pmax", [P, HQ * T, NC])
    neg_max = core.sb(f"{tag}_nmax", [P, HQ * T])
    max_parts = core.sb(f"{tag}_mparts", [P, 2, HQ * T], BF16)
    max_rows = core.sb(f"{tag}_mrows", [HQ * T, 2, P], BF16)
    dens = core.sb(f"{tag}_dens", [P, HQ * S // P])
    rdens = core.sb(f"{tag}_rdens", [P, HQ * S // P])
    rrows = core.sb(f"{tag}_rrows", [P, S])
    nothing = core.sb(f"{tag}_nothing", [P, 8])
    qs2 = qs[:].rearrange("p a h t -> p (a h t)")
    ks2 = ks[:].rearrange("p a h t -> p (a h t)")
    ctx2 = ctxu[:].rearrange("p a t -> p (a t)")
    QB = HQ * S
    max_dram, den_dram, rden_dram = scratch

    prepared, ticks, ticks_pool = core.sem(f"{tag}_prepared"), core.sem(f"{tag}_ticks"), core.sem(f"{tag}_ticks_pool")
    with nc.Block() as block:
        @block.gpsimd
        def _(pool):
            pool.memset(qs2[STACK:KROWS, :], 0.0)
            pool.memset(ks2[STACK:KROWS, :], 1.0)

        @block.vector
        def _(dve):
            dve.memset(part_max[:], FLOOR)
            dve.memset(ctxu[:, 0, :], 1.0)
            dve.memset(vq[:], 0.0).then_inc(prepared, 1)
            dve.wait_ge(prepared, 1)
            dve.memset(vq[:, :, :, D:D + 1], 1.0)

    staged = core.sem(f"{tag}_staged")
    v_placed = core.sem(f"{tag}_v_placed")
    a_scored = core.sem(f"{tag}_a_scored")
    a_free = core.sem(f"{tag}_a_free")
    neg_ready = core.sem(f"{tag}_neg_ready")
    chain = core.sem(f"{tag}_chain")
    rows_ready = core.sem(f"{tag}_rows_ready")
    max_stored = core.sem(f"{tag}_max_stored")
    max_loaded = core.sem(f"{tag}_max_loaded")
    b_scored = core.sem(f"{tag}_b_scored")
    exped = core.sem(f"{tag}_exped")
    masked = core.sem(f"{tag}_masked")
    pv_done = core.sem(f"{tag}_pv_done")
    ctx_moved = core.sem(f"{tag}_ctx_moved")
    den_out, den_in = core.sem(f"{tag}_den_out"), core.sem(f"{tag}_den_in")
    rden_made, rden_out = core.sem(f"{tag}_rden_made"), core.sem(f"{tag}_rden_out")
    rden_in, scaled = core.sem(f"{tag}_rden_in"), core.sem(f"{tag}_scaled")
    A0, B0, O0 = 0, 2, 6

    with nc.Block() as block:
        @block.sync
        def _(sp):
            def stage(j, buf):
                for x, (stack, which) in enumerate(((qs2, Q_PARTS), (ks2, K_PARTS))):
                    for r, part in enumerate(which):
                        sp.dma_start(
                            stack[r * D:(r + 1) * D, bass.ds(buf * QB, QB)].rearrange("d (h t) -> d h t", h=HQ),
                            parts_dram[x, part, bass.ds(j * HQ * D, HQ * D), :].rearrange("(h d) t -> d h t", h=HQ)
                        ).then_inc(staged, 16)

            def maxima(j, buf):
                sp.wait_ge(rows_ready, j * 2 + 2)
                sp.dma_start(max_dram[bass.ds(j, 1)].rearrange("o a r q -> (o r) a q"),
                             max_rows[:]).then_inc(max_stored, 16)
                sp.wait_ge(max_stored, j * 16 + 16)
                sp.dma_start(qs2[STACK:STACK + 2, bass.ds(buf * QB, QB)],
                             max_dram[bass.ds(j, 1)].rearrange("o a r q -> (o a) (r q)")).then_inc(max_loaded, 16)

            def normalise(j):
                sp.wait_ge(ctx_moved, j * NC + 2)
                sp.dma_start(den_dram[bass.ds(j, 1)].rearrange("o g t -> (o g) t"),
                             ctx2[D:P:32, bass.ds(j * S, S)]).then_inc(den_out, 16)
                sp.wait_ge(den_out, j * 16 + 16)
                sp.dma_start(dens[:], den_dram[bass.ds(j, 1)].rearrange("o g (a b) -> (o g a) b", b=HQ * S // P)
                             ).then_inc(den_in, 16)
                sp.wait_ge(rden_made, j + 1)
                sp.dma_start(rden_dram[bass.ds(j, 1)].rearrange("o g (a b) -> (o g a) b", b=HQ * S // P),
                             rdens[:]).then_inc(rden_out, 16)
                sp.wait_ge(rden_out, j * 16 + 16)
                sp.wait_ge(scaled, j + 1)
                for g in range(HQ):
                    sp.dma_start(rrows[32 * g:32 * g + 32, :],
                                 rden_dram[bass.ds(j, 1), g, :].to_broadcast([32, S])).then_inc(rden_in, 16)

            stage(0, 0)
            sp.wait_ge(staged, 256)
            stage(1, 1)
            maxima(0, 0)
            with sp.Fori(0, NQ - 2) as j:
                normalise(j)
                maxima(j + 1, (j + 1) % 2)
                sp.wait_ge(pv_done, j * NG + NG + RING)
                sp.wait_ge(staged, j * 256 + 512)
                stage(j + 2, j % 2)
            normalise(NQ - 2)
            maxima(NQ - 1, (NQ - 1) % 2)
            normalise(NQ - 1)
            normalise(NQ)

        @block.tensor
        def _(pe):
            def first_unit(j, buf, u):
                wait_apart(pe, a_free, j * NU + u + 1, ticks)
                bank = A0 + u % 2
                if u >= len(UNITS):
                    wait_apart(pe, neg_ready, j + 1, ticks)
                    pe.transpose(ps[0:HQ * T, bank, 0:P // 2].bitcast(BF16), max_parts[:, u - len(UNITS), :],
                                 c["identb"][:]).then_inc(a_scored, 1)
                    return
                g, i, kc = UNITS[u]
                diagonal = kc == i // TC
                w = P * (i % TC + 1) if diagonal else CH
                ins = pe.matmul(ps[:, bank, 0:w], qs2[0:STACK, bass.ds(buf * QB + g * S + i * P, P)],
                                ks2[0:STACK, bass.ds(buf * QB + g * S + kc * CH, w)], start=True, stop=not diagonal)
                if diagonal:
                    ins = pe.matmul(ps[:, bank, w - P:w], c["identb"][:], c["future"][:], start=False, stop=True)
                ins.then_inc(a_scored, 1)

            def scores(j, buf, k):
                cq, t = GROUPS[k]
                skip = max(0, t - TC * cq) * P
                for g in range(HQ):
                    pe.wait_ge(exped, j * HQ * NG + HQ * k + g + 1)
                    pe.matmul(ps[:, B0 + g, skip:CH], ks2[0:KROWS, bass.ds(buf * QB + g * S + t * P, P)],
                              qs2[0:KROWS, bass.ds(buf * QB + g * S + cq * CH + skip, CH - skip)],
                              start=True, stop=True).then_inc(b_scored, 1)

            def product(j, k):
                cq, t = GROUPS[k]
                skip = max(0, t - TC * cq) * P
                pe.wait_ge(exped, j * HQ * NG + HQ * k + 2 * HQ)
                if k in DIAG:
                    pe.wait_ge(masked, j * len(DIAG) + DIAG.index(k) + 1)
                if t == 0:
                    pe.wait_ge(ctx_moved, j * NC + cq + 1)
                for g in range(HQ):
                    ins = pe.matmul(ps[32 * g:32 * g + 32, O0 + cq % 2, skip:CH], vq[:, t, g, :],
                                    probs[:, k % RING, g, skip:CH], start=(t == 0), stop=(k == LAST[cq]),
                                    skip_group_check=True)
                ins.then_inc(pv_done, 1)

            def body(jb, ja, bufb, bufa):
                if jb is not None:
                    pe.wait_ge(max_loaded, jb * 16 + 16)
                    pe.wait_ge(v_placed, jb + 1)
                for k in range(NG):
                    bufb, bufa = fresh(pe, bufb, 1), fresh(pe, bufa, 1)
                    if jb is not None:
                        scores(jb, bufb, k)
                    if ja is not None:
                        if k == (A_FROM if jb is not None else 0):
                            pe.wait_ge(staged, ja * 256 + 256)
                        for u in first_pass_share(k, jb is None):
                            first_unit(ja, bufa, u)
                    if jb is not None and k:
                        product(jb, k - 1)
                if jb is not None:
                    product(jb, NG - 1)

            body(None, 0, None, 0)
            with pe.Fori(0, NQ - 1) as j:
                body(j, j + 1, j % 2, (j + 1) % 2)
            body(NQ - 1, None, (NQ - 1) % 2, None)

        @block.scalar
        def _(act):
            def body(j):
                for k, (cq, t) in enumerate(GROUPS):
                    skip = max(0, t - TC * cq) * P
                    act.wait_ge(pv_done, j * NG + k + 1)
                    for g in range(HQ):
                        act.wait_ge(b_scored, j * HQ * NG + HQ * k + g + 1)
                        act.activation(probs[:, k % RING, g, skip:CH], ps[:, B0 + g, skip:CH],
                                       ACT.Exp).then_inc(exped, 1)

            with act.Fori(0, NQ) as j:
                body(j)

        @block.gpsimd
        def _(pool):
            def mask(j, n):
                k = DIAG[n]
                cq, t = GROUPS[k]
                skip = (t - TC * cq) * P
                tri = probs[:, k % RING, :, skip:skip + P]
                wait_apart(pool, exped, j * HQ * NG + HQ * k + 2 * HQ, ticks_pool)
                pool.affine_select(out=tri, in_=tri, compare_op=ALU.is_ge, fill=0.0, base=0,
                                   pattern=[[0, HQ], [1, P]], channel_multiplier=-1).then_inc(masked, 1)

            def scale(j):
                pool.wait_ge(rden_in, j * 64 + 64)
                ctx = ctx2[:, bass.ds(j * S, S)]
                pool.tensor_tensor(ctx, ctx, rrows[:], ALU.mult).then_inc(scaled, 1)

            pool.memset(nothing[:, 0:1], 0.0).then_inc(scaled, 1)
            with pool.Fori(0, NQ) as j:
                for n in range(len(DIAG)):
                    mask(j, n)
                    if n == 3 * TC - 1:
                        scale(j)
            scale(NQ)

        @block.vector
        def _(dve):
            def place_values(j):
                dve.tensor_copy(vq[:, :, :, 0:D],
                                values[:].rearrange("p t (q d) -> p q t d", d=HQ * D)[:, bass.ds(j, 1)]
                                .rearrange("p o t (h d) -> p (o t) h d", h=HQ)).then_inc(v_placed, 1)

            def first_unit(j, first, u):
                dve.wait_ge(a_scored, j * NU + u + 1)
                bank = A0 + u % 2
                if u >= len(UNITS):
                    x = u - len(UNITS)
                    if not first and x == 0:
                        dve.wait_ge(max_stored, j * 16)
                    dve.tensor_copy(max_rows[:, x, :], ps[0:HQ * T, bank, 0:P // 2].bitcast(BF16)
                                    ).then_inc(rows_ready, 1)
                    dve.wait_ge(rows_ready, j * 2 + x + 1)
                    dve.memset(nothing[:, 1:2], 0.0).then_inc(a_free, 1)
                    return
                g, i, kc = UNITS[u]
                w = P * (i % TC + 1) if kc == i // TC else CH
                dve.tensor_reduce(part_max[:, g * T + i, kc:kc + 1], ps[:, bank, 0:w], AX.X,
                                  ALU.max).then_inc(a_free, 1)
                if u == len(UNITS) - 1:
                    dve.wait_ge(a_free, j * NU + len(UNITS) + 2)
                    dve.tensor_reduce(neg_max[:], part_max[:], AX.X, ALU.max, negate=True).then_inc(chain, 1)
                    dve.wait_ge(chain, j * 2 + 1)
                    dve.tensor_copy(max_parts[:, 0, :], neg_max[:]).then_inc(chain, 1)
                    dve.wait_ge(chain, j * 2 + 2)
                    dve.tensor_tensor(max_parts[:, 1, :], neg_max[:], max_parts[:, 0, :],
                                      ALU.subtract).then_inc(neg_ready, 1)

            def move_context(j, cq):
                dve.wait_ge(pv_done, j * NG + LAST[cq] + 1 + RING)
                dve.tensor_copy(ctx2[:, bass.ds(j * S + S + cq * CH, CH)], ps[:, O0 + cq % 2, :]
                                ).then_inc(ctx_moved, 1)

            def reciprocals(j):
                dve.wait_ge(den_in, j * 16 + 16)
                dve.reciprocal(rdens[:], dens[:]).then_inc(rden_made, 1)

            def body(jb, ja):
                for k in range(NG):
                    for cq in range(NC - 1):
                        if k == LAST[cq] + 2:
                            move_context(jb, cq)
                    if k == A_FROM + 1:
                        reciprocals(jb)
                    if ja is not None:
                        for u in first_pass_share(k, False):
                            first_unit(ja, False, u)
                move_context(jb, NC - 1)

            dve.memset(nothing[:, 2:3], 0.0).then_inc(a_free, 2)
            dve.memset(nothing[:, 3:4], 0.0).then_inc(exped, HQ)
            dve.memset(nothing[:, 4:5], 0.0).then_inc(pv_done, RING)
            dve.memset(nothing[:, 5:6], 0.0).then_inc(ctx_moved, 2)
            place_values(0)
            for u in first_pass_share(0, True):
                first_unit(0, True, u)
            with dve.Fori(0, NQ - 1) as j:
                body(j, j + 1)
                place_values(j + 1)
            body(NQ - 1, None)
            reciprocals(NQ)


def project_context(nc, core, ps, tag, ctxu, wo, base, out):
    done, chain = core.sem(f"{tag}_done"), core.sem(f"{tag}_read")
    with nc.Block() as block:
        @block.tensor
        def _(pe):
            for n in range(NC):
                for i in range(TC):
                    t = n * TC + i
                    for q in range(NQ):
                        ins = pe.matmul(ps[:, n, i * P:(i + 1) * P], ctxu[:, 1 + q, t * P:(t + 1) * P], wo[:, q, :],
                                        start=(q == 0), stop=(q == NQ - 1))
                ins.then_inc(done, 1)

        @block.vector
        def _(dve):
            for n in range(NC):
                dve.wait_ge(done, n + 1)
                sl = slice(n * TC, (n + 1) * TC)
                dve.tensor_tensor(out[:, sl, :], ps[:, n, :].rearrange("p (a b) -> p a b", a=TC), base[:, sl, :],
                                  ALU.add).then_inc(chain, 1)


def ffn0_weights(nc, core, ps, ident, w_fc, w_proj, fbT, v, uT, gate, fcT, projT):
    G = F0 // P
    sums = core.sb("f0_sums", [P, G + 1])
    scale = core.sb("f0_scale", [P, G + 1])
    half = core.sb("f0_half", [P, 2, G + 1])
    tern = core.sb("f0_tern", [P, 2, F0])
    low = core.sb("f0_low", [P, 2, F0])
    m1 = core.sb("f0_m1", [RANK, P])
    chain, made, small = core.sem("f0_chain"), core.sem("f0_made"), core.sem("f0_small")
    turned, m1_moved, lowrank = core.sem("f0_turned"), core.sem("f0_m1_moved"), core.sem("f0_lowrank")
    wide = [w_fc[:].rearrange("p a b -> p (a b)"), w_proj[:]]
    with nc.Block() as block:
        @block.vector
        def _(dve):
            ch = Chain(dve, chain)
            ch.then(dve.tensor_reduce(sums[:, 0:G], w_fc[:], AX.X, ALU.add, apply_absolute_value=True))
            ch.then(dve.tensor_reduce(sums[:, G:G + 1], w_proj[:], AX.X, ALU.add, apply_absolute_value=True))
            ch.then(dve.tensor_scalar(scale[:, 0:G], sums[:, 0:G], 1.0 / P, 1e-5, ALU.mult, ALU.max))
            ch.then(dve.tensor_scalar(scale[:, G:], sums[:, G:], 1.0 / F0, 1e-5, ALU.mult, ALU.max))
            ch.then(dve.tensor_scalar(half[:, 0, :], scale[:], 0.5, None, ALU.mult))
            ch.then(dve.tensor_scalar(half[:, 1, :], scale[:], -0.5, None, ALU.mult))
            for x in range(2):
                for g in range(G):
                    s = g if x == 0 else G
                    sl = slice(g * P, (g + 1) * P)
                    w = wide[x][:, sl]
                    ch.then(dve.tensor_scalar(tern[:, x, sl], w, half[:, 0, s:s + 1], None, ALU.is_gt))
                    ch.then(dve.tensor_scalar(low[:, x, sl], w, half[:, 1, s:s + 1], None, ALU.is_lt))
                    ch.then(dve.tensor_tensor(tern[:, x, sl], tern[:, x, sl], low[:, x, sl], ALU.subtract))
                    ch.then(dve.tensor_tensor(tern[:, x, sl], tern[:, x, sl], w, ALU.subtract))
                    ch.then(dve.tensor_tensor(tern[:, x, sl], tern[:, x, sl], w, ALU.add))
                    dve.tensor_scalar(tern[:, x, sl], tern[:, x, sl], scale[:, s:s + 1], None,
                                      ALU.mult).then_inc(made, 1)
            dve.wait_ge(small, 1)
            dve.tensor_copy(m1[:], ps[0:RANK, 2, 0:P]).then_inc(m1_moved, 1)
            dve.wait_ge(turned, 1)
            dve.tensor_copy(projT[:].rearrange("p a b -> p (a b)"), ps[:, 1, :])
            ch.then(dve.tensor_copy(fcT[:], ps[:, 0, :]))
            dve.wait_ge(lowrank, 1)
            ch.then(dve.scalar_tensor_tensor(out=fcT[:], in0=ps[:, 3, :], scalar=gate[:, 0:1], in1=fcT[:],
                                             op0=ALU.mult, op1=ALU.add))

        @block.tensor
        def _(pe):
            pe.matmul(ps[0:RANK, 2, 0:P], fbT[:], v[:], start=True, stop=True).then_inc(small, 1)
            for x in range(2):
                for g in range(G):
                    pe.wait_ge(made, x * G + g + 1)
                    ins = pe.transpose(ps[:, x, g * P:(g + 1) * P], tern[:, x, g * P:(g + 1) * P], ident[:])
            ins.then_inc(turned, 1)
            pe.wait_ge(m1_moved, 1)
            pe.matmul(ps[:, 3, :], m1[:], uT[:], start=True, stop=True).then_inc(lowrank, 1)


def ffn0(nc, core, ps, cols, fcT, projT, acc):
    G = F0 // P
    relu = core.sb("ffn0_relu", [P, 2, G, CH])
    up, relued, squared, down, added = (core.sem(f"ffn0_{n}") for n in ("up", "relued", "squared", "down", "added"))
    with nc.Block() as block:
        @block.tensor
        def _(pe):
            for n in range(NC + 1):
                if n < NC:
                    for g in range(G):
                        if n:
                            pe.wait_ge(relued, (n - 1) * G + g + 1)
                        pe.matmul(ps[:, g, :], fcT[:, g * P:(g + 1) * P], cols[:, n * CH:(n + 1) * CH],
                                  start=True, stop=True).then_inc(up, 1)
                if n:
                    m = n - 1
                    pe.wait_ge(squared, n)
                    if m >= 2:
                        pe.wait_ge(added, m - 1)
                    for i in range(TC):
                        for g in range(G):
                            ins = pe.matmul(ps[:, 4 + m % 2, i * P:(i + 1) * P], relu[:, m % 2, g, i * P:(i + 1) * P],
                                            projT[:, g, :], start=(g == 0), stop=(g == G - 1))
                    ins.then_inc(down, 1)

        @block.scalar
        def _(act):
            for n in range(NC):
                if n >= 2:
                    act.wait_ge(down, n - 1)
                for g in range(G):
                    act.wait_ge(up, n * G + g + 1)
                    act.activation(relu[:, n % 2, g, :], ps[:, g, :], ACT.Relu).then_inc(relued, 1)

        @block.vector
        def _(dve):
            for n in range(NC + 1):
                if n < NC:
                    dve.wait_ge(relued, (n + 1) * G)
                    dve.tensor_tensor(relu[:, n % 2], relu[:, n % 2], relu[:, n % 2], ALU.mult).then_inc(squared, 1)
                if n:
                    m = n - 1
                    sl = slice(m * TC, (m + 1) * TC)
                    dve.wait_ge(down, n)
                    dve.tensor_tensor(acc[:, sl, :], ps[:, 4 + m % 2, :].rearrange("p (a b) -> p a b", a=TC),
                                      acc[:, sl, :], ALU.add).then_inc(added, 1)


def linear_attention(nc, core, ps, ident, qk, values, wo, blocks, acc):
    ktok = core.sb("la_ktok", [P, T, P])
    ones = core.sb("la_ones", [P, 1])
    vk = core.sb("la_vk", [P, P])
    kden = core.sb("la_kden", [P, P])
    ksum = core.sb("la_ksum", [P, 1])
    den = core.sb("la_den", [P, S])
    rden = core.sb("la_rden", [P, S])
    att = core.sb("la_att", [P, S])
    names = ("turned", "moved", "summed", "chain", "weights", "applied", "normed", "projected", "ones", "added")
    turned, moved, summed, chain, weights, applied, normed, projected, ones_made, added = (core.sem(f"la_{n}") for n in names)
    with nc.Block() as block:
        @block.tensor
        def _(pe):
            for t in range(T):
                ins = pe.transpose(ps[:, t // TC, (t % TC) * P:(t % TC + 1) * P], qk[:, 1, t * P:(t + 1) * P], ident[:])
                if t % TC == TC - 1:
                    ins.then_inc(turned, 1)
            pe.wait_ge(ones_made, 1)
            pe.wait_ge(moved, NC)
            for t in range(T):
                pe.matmul(ps[:, 4, 0:P], ktok[:, t, :], values[:, t, :], start=(t == 0), stop=(t == T - 1))
            for t in range(T):
                ins = pe.matmul(ps[:, 5, 0:1], ktok[:, t, :], ones[:], start=(t == 0), stop=(t == T - 1))
            ins.then_inc(summed, 1)
            pe.wait_ge(weights, 1)
            for n in range(NC):
                if n >= 1:
                    pe.wait_ge(normed, n)
                pe.matmul(ps[:, 6, :], kden[:], qk[:, 0, n * CH:(n + 1) * CH], start=True, stop=True)
                pe.matmul(ps[:, 7, :], vk[:], qk[:, 0, n * CH:(n + 1) * CH], start=True, stop=True).then_inc(applied, 1)
            for n in range(NC):
                pe.wait_ge(normed, n + 1)
                for i in range(TC):
                    t = n * TC + i
                    ins = pe.matmul(ps[:, n, i * P:(i + 1) * P], att[:, t * P:(t + 1) * P], wo[:], start=True, stop=True)
                ins.then_inc(projected, 1)

        @block.scalar
        def _(act):
            for n in range(NC):
                act.wait_ge(turned, n + 1)
                act.copy(ktok[:, n * TC:(n + 1) * TC, :],
                         ps[:, n, :].rearrange("p (a b) -> p a b", a=TC)).then_inc(moved, 1)

        @block.vector
        def _(dve):
            ch = Chain(dve, chain)
            dve.memset(ones[:], 1.0).then_inc(ones_made, 1)
            dve.wait_ge(summed, 1)
            ch.then(dve.tensor_copy(ksum[:], ps[:, 5, 0:1]))
            ch.then(dve.tensor_tensor(vk[:], ps[:, 4, 0:P], blocks[:], ALU.mult))
            dve.tensor_scalar(kden[:], blocks[:], ksum[:, 0:1], None, ALU.mult).then_inc(weights, 1)
            for n in range(NC):
                sl = slice(n * CH, (n + 1) * CH)
                dve.wait_ge(applied, n + 1)
                ch.then(dve.tensor_scalar(den[:, sl], ps[:, 6, :], 1e-6, None, ALU.add))
                ch.then(dve.reciprocal(rden[:, sl], den[:, sl]))
                dve.tensor_tensor(att[:, sl], ps[:, 7, :], rden[:, sl], ALU.mult).then_inc(normed, 1)
            for n in range(NC):
                sl = slice(n * TC, (n + 1) * TC)
                dve.wait_ge(projected, n + 1)
                dve.tensor_tensor(acc[:, sl, :], ps[:, n, :].rearrange("p (a b) -> p a b", a=TC), acc[:, sl, :],
                                  ALU.add).then_inc(added, 1)


def route(nc, core, ps, cols, w_router, order, combine):
    shape = [P, T, E]
    logits, left, pick, first, second, ex = (core.sb(f"rt_{n}", shape) for n in
                                             ("logits", "left", "pick", "first", "second", "ex"))
    best = core.sb("rt_best", [P, T])
    rank = core.sb("rt_rank", [P, T])
    best2 = core.sb("rt_best2", [P, T])
    tot = core.sb("rt_tot", [P, T])
    scored, chain, shifted, exped = core.sem("rt_scored"), core.sem("rt_chain"), core.sem("rt_shifted"), core.sem("rt_exped")

    def wide(x):
        return x[:].rearrange("p (t o) -> p t o", o=1).to_broadcast(shape)

    with nc.Block() as block:
        @block.tensor
        def _(pe):
            for t in range(T):
                ins = pe.matmul(ps[:, 0, t * E:(t + 1) * E], cols[:, t * P:(t + 1) * P], w_router[:], start=True, stop=True)
            ins.then_inc(scored, 1)

        @block.vector
        def _(dve):
            ch = Chain(dve, chain)

            def one_hot(values, top, out):
                ch.then(dve.tensor_reduce(top[:], values[:], AX.X, ALU.max))
                ch.then(dve.tensor_tensor(pick[:], values[:], wide(top), ALU.is_equal))
                ch.then(dve.tensor_tensor(pick[:], pick[:], order[:], ALU.mult))
                ch.then(dve.tensor_reduce(rank[:], pick[:], AX.X, ALU.max))
                ch.then(dve.tensor_tensor(out[:], order[:], wide(rank), ALU.is_equal))

            dve.wait_ge(scored, 1)
            ch.then(dve.tensor_copy(logits[:], ps[:, 0, 0:T * E].rearrange("p (t e) -> p t e", e=E)))
            one_hot(logits, best, first)
            ch.then(dve.scalar_tensor_tensor(out=left[:], in0=first[:], scalar=FLOOR, in1=logits[:],
                                             op0=ALU.mult, op1=ALU.add))
            one_hot(left, best2, second)
            dve.tensor_tensor(ex[:], logits[:], wide(best), ALU.subtract).then_inc(shifted, 1)
            ch.then(dve.tensor_tensor(first[:], first[:], second[:], ALU.add))
            dve.wait_ge(exped, 1)
            ch.then(dve.tensor_tensor(ex[:], ex[:], first[:], ALU.mult))
            ch.then(dve.tensor_reduce(tot[:], ex[:], AX.X, ALU.add))
            ch.then(dve.reciprocal(tot[:], tot[:]))
            ch.then(dve.tensor_tensor(combine[:], ex[:], wide(tot), ALU.mult))

        @block.scalar
        def _(act):
            act.wait_ge(shifted, 1)
            act.activation(ex[:], ex[:], ACT.Exp).then_inc(exped, 1)


def experts(nc, core, ps, cols, wg, wu, wd, combine, acc):
    silu = core.sb("moe_silu", [P, 2, CH])
    act_ = core.sb("moe_act", [P, 2, HC, CH])
    names = ("gu", "silued", "mixed", "down", "added")
    gu, silued, mixed, down, added = (core.sem(f"moe_{n}") for n in names)
    W_UNIT = NC * HC
    wcur = core.sb("moe_wcur", [P, 2, 2 * HID + HC * P])
    w_placed = [core.sem(f"moe_w_placed{b}") for b in range(2)]
    none = core.sb("moe_none", [P, 8])
    combine_by_expert = core.sb("moe_combine", [P, E, T])
    placed = core.sem("moe_placed")
    with nc.Block() as block:
        def weights(b):
            return wcur[:, b, 0:HID], wcur[:, b, HID:2 * HID], wcur[:, b, 2 * HID:]

        @block.tensor
        def _(pe):
            def expert(e, half):
                wgn, wun, _ = weights(half)
                pe.wait_ge(w_placed[half], e * 24 + 48)
                for n in range(NC):
                    for h in range(HC):
                        u = half * W_UNIT + n * HC + h
                        b = 2 * (u % 2)
                        pe.wait_ge(mixed, e * W_UNIT + u + 1)
                        pe.matmul(ps[:, b, :], wgn[:, h * P:(h + 1) * P], cols[:, n * CH:(n + 1) * CH],
                                  start=True, stop=True)
                        pe.matmul(ps[:, b + 1, :], wun[:, h * P:(h + 1) * P], cols[:, n * CH:(n + 1) * CH],
                                  start=True, stop=True).then_inc(gu, 1)
                    if n:
                        down_product(e, half, n - 1)
                down_product(e, half, NC - 1)

            def down_product(e, half, n):
                d = half * NC + n
                pe.wait_ge(mixed, e * W_UNIT + (d + 1) * HC + 2)
                pe.wait_ge(added, e * NC + d + 1)
                _, _, wdn = weights(half)
                for i in range(TC):
                    for h in range(HC):
                        ins = pe.matmul(ps[:, 4 + n % 2, i * P:(i + 1) * P], act_[:, n % 2, h, i * P:(i + 1) * P],
                                        wdn[:, h * P:(h + 1) * P], start=(h == 0), stop=(h == HC - 1))
                ins.then_inc(down, 1)

            with pe.Fori(0, E // 2) as pair:
                e = pair * 2
                for half in range(2):
                    expert(e, half)

        @block.sync
        def _(sp):
            with sp.Fori(0, E // 2) as pair:
                e = pair * 2
                for half in range(2):
                    sp.wait_ge(down, e * NC + NC * (half + 1))
                    wgn, wun, wdn = weights(half)
                    one = bass.ds(e + half, 1)
                    sp.dma_start(wgn, wg[one].rearrange("o d h -> (o d) h")).then_inc(w_placed[half], 16)
                    sp.dma_start(wun, wu[one].rearrange("o d h -> (o d) h")).then_inc(w_placed[half], 16)
                    sp.dma_start(wdn.rearrange("p (c d) -> p c d", c=HC),
                                 wd[one].rearrange("o (c p) d -> p (o c) d", p=P)).then_inc(w_placed[half], 16)

        @block.scalar
        def _(act):
            with act.Fori(0, E // 2) as pair:
                e = pair * 2
                for u in range(2 * W_UNIT):
                    act.wait_ge(gu, e * W_UNIT + u + 1)
                    act.wait_ge(mixed, e * W_UNIT + u + 1)
                    act.activation(silu[:, u % 2, :], ps[:, 2 * (u % 2), :], ACT.Silu).then_inc(silued, 1)

        @block.vector
        def _(dve):
            def add(e, half, n):
                d = half * NC + n
                dve.wait_ge(down, e * NC + d + 1 + 2 * NC)
                for i in range(TC):
                    t = n * TC + i
                    ins = dve.scalar_tensor_tensor(out=acc[:, t, :], in0=ps[:, 4 + n % 2, i * P:(i + 1) * P],
                                                   scalar=combine2[:, bass.ds(e * T + half * T + t, 1)],
                                                   in1=acc[:, t, :], op0=ALU.mult, op1=ALU.add)
                ins.then_inc(added, 1)

            combine2 = combine_by_expert[:].rearrange("p e t -> p (e t)")
            dve.memset(none[:, 0:1], 0.0).then_inc(mixed, 2)
            dve.memset(none[:, 1:2], 0.0).then_inc(added, 2)
            dve.memset(none[:, 2:3], 0.0).then_inc(down, 2 * NC)
            dve.tensor_copy(combine_by_expert[:], combine[:].rearrange("p t e -> p e t")).then_inc(placed, 1)
            dve.wait_ge(placed, 1)
            with dve.Fori(0, E // 2) as pair:
                e = pair * 2
                for half in range(2):
                    for n in range(NC):
                        for h in range(HC):
                            u = half * W_UNIT + n * HC + h
                            dve.wait_ge(silued, e * W_UNIT + u + 1)
                            if h == 0:
                                dve.wait_ge(down, e * NC + half * NC + n + 1 + 2 * NC - 2)
                            dve.tensor_tensor(act_[:, n % 2, h, :], ps[:, 2 * (u % 2) + 1, :], silu[:, u % 2, :],
                                              ALU.mult).then_inc(mixed, 1)
                        if n:
                            add(e, half, n - 1)
                    add(e, half, NC - 1)



def build(nc, a, out):
    with ExitStack() as outer:
        core = Core(nc, outer)
        ps = outer.enter_context(nc.psum_tensor("psum", [P, 8, CH], F32))
        c = {"ident": core.sb("ident", [P, P]), "identb": core.sb("identb", [P, P], BF16),
             "future": core.sb("future", [P, P], BF16)}
        ident = c["ident"]
        x = core.sb("x", [P, T, P])
        xn = core.sb("xn", [P, T, P])
        cols = core.sb("cols", [P, S])
        values = core.sb("values", [P, T, P])
        parts_dram = core.dram("parts", (2, 3, P, S), BF16)
        scratch = [[core.dram(f"maxima{n}", (NQ, 2, HQ * T, P), BF16), core.dram(f"sums{n}", (NQ + 1, HQ, S), F32),
                    core.dram(f"rsums{n}", (NQ + 1, HQ, S), F32)] for n in range(2)]

        def tokens(ap):
            return ap.rearrange("(t p) d -> p t d", p=P)

        def quad_rows(wo, dst):
            return [(dst[32 * g:32 * g + D, :, :], wo.rearrange("(q g d) n -> g d q n", q=NQ, g=HQ)[g])
                    for g in range(HQ)]

        def zero(tag, tensors):
            z = core.sem(f"{tag}_zero")
            with nc.Block() as block:
                @block.vector
                def _(dve):
                    for t in tensors:
                        dve.memset(t[:], 0.0).then_inc(z, 1)

        with ExitStack() as ctx0:
            w0 = Core(nc, ctx0)
            ctxu = w0.sb("ctx0", [P, NQ + 1, S])
            wo = w0.sb("wo0", [P, NQ, P])
            bout = w0.sb("bout", [P, P])
            zero("z0", [wo])
            constants(nc, core, c)
            with ExitStack() as early:
                e0 = Core(nc, early)
                wqkv, bias, bias_v = e0.sb("wqkv", [P, 3 * P]), e0.sb("bias", [P, 2]), e0.sb("bias_v", [P, P])
                w_fc, w_proj = e0.sb("w_fc", [P, F0 // P, P]), e0.sb("w_proj", [P, F0])
                fbT, v, uT, gate = e0.sb("fbT", [RANK, RANK]), e0.sb("v", [RANK, P]), e0.sb("uT", [RANK, F0]), e0.sb("gate", [P, 1])
                fcT, projT = e0.sb("fcT", [P, F0]), e0.sb("projT", [P, F0 // P, P])
                load(nc, core, "l0", [
                    (x[:], tokens(a["x"])), (wqkv[:], a["Wqkv"]),
                    (bias[:], a["bqk"]), (bias_v[:], a["bv"].partition_broadcast(P)),
                    (bout[:], a["bout"].partition_broadcast(P)),
                    (w_fc[:], a["w_fc"].rearrange("(g p) d -> p g d", p=P)), (w_proj[:], a["w_proj"]),
                    (fbT[:], a["fast_bT"]), (v[:], a["v"]), (uT[:], a["uT"]), (gate[:], a["gate"].partition_broadcast(P)),
                    *quad_rows(a["Wout"], wo)])
                norm_transpose(nc, e0, ps, ident, "n0", x, xn, cols)
                qkv_plain(nc, e0, ps, "p0", cols, wqkv, bias, bias_v, values, parts_dram)
                ffn0_weights(nc, e0, ps, ident, w_fc, w_proj, fbT, v, uT, gate, fcT, projT)
                b = core.sem("bout_added")
                with nc.Block() as block:
                    @block.vector
                    def _(dve):
                        for t in range(T):
                            dve.tensor_tensor(x[:, t, :], x[:, t, :], bout[:], ALU.add).then_inc(b, 1)
                ffn0(nc, e0, ps, cols, fcT, projT, x)
            with ExitStack() as att:
                attention(nc, Core(nc, att), ps, "a0", parts_dram, values, c, ctxu, scratch[0])
            project_context(nc, w0, ps, "o0", ctxu, wo, x, x)

        hid = core.sb("hid", [P, T, P])
        with ExitStack() as ctx1:
            w1 = Core(nc, ctx1)
            ctxu = w1.sb("ctx1", [P, NQ + 1, S])
            wo = w1.sb("wo1", [P, NQ, P])
            zero("z1", [wo])
            with ExitStack() as early:
                e1 = Core(nc, early)
                wl = e1.sb("wl", [P, 6, P])
                wf = e1.sb("wf", [P, 5, P])
                g1 = e1.sb("g1", [P, P])
                cos, sin = e1.sb("cos", [P, S]), e1.sb("sin", [P, S])
                blocks = e1.sb("blocks", [P, P])
                load(nc, w1, "l1", [
                    *[(wl[:, i, :], a[n]) for i, n in enumerate(("Wq", "Wq_turned", "Wk", "Wk_turned", "Wv", "Wo"))],
                    *[(wf[:, i, :], a[n]) for i, n in enumerate(("wq", "wq_turned", "wk", "wk_turned", "wv"))],
                    (g1[:], a["g1"].partition_broadcast(P)), (blocks[:], a["blocks"]),
                    (cos[:], a["cos_pairs"]), (sin[:], a["sin_pairs"]), *quad_rows(a["wo"], wo)])
                norm_transpose(nc, e1, ps, ident, "n1", x, xn, cols)
                with ExitStack() as lin:
                    l1 = Core(nc, lin)
                    qk = l1.sb("la_qk", [P, 2, S])
                    qkv_rope(nc, l1, ps, "pl", cols, *(wl[:, i, :] for i in range(5)), cos, sin, values, "relu", 1.0, out=qk)
                    linear_attention(nc, l1, ps, ident, qk, values, wl[:, 5, :], blocks, x)
                load(nc, w1, "l2", [(cos[:], a["cos_halves"]), (sin[:], a["sin_halves"])])
                norm_transpose(nc, e1, ps, ident, "n2", xn, hid, cols, rms_gain=g1, eps=1e-6)
                qkv_rope(nc, e1, ps, "pf", cols, *(wf[:, i, :] for i in range(5)), cos, sin, values, "split", SM_SCALE,
                         parts_dram=parts_dram)
            with ExitStack() as att:
                attention(nc, Core(nc, att), ps, "a1", parts_dram, values, c, ctxu, scratch[1])
            project_context(nc, w1, ps, "o1", ctxu, wo, xn, hid)

        with ExitStack() as ctx2:
            w2 = Core(nc, ctx2)
            w_router, g2 = w2.sb("w_router", [P, E]), w2.sb("g2", [P, P])
            order, combine = w2.sb("order", [P, T, E]), w2.sb("combine", [P, T, E])
            s = w2.sem("hid_added")
            load(nc, w2, "l3", [
                (w_router[:], a["w_router"]),
                (g2[:], a["g2"].partition_broadcast(P)), (order[:], a["order"].partition_broadcast(P))])
            norm_transpose(nc, w2, ps, ident, "n3", hid, xn, cols, rms_gain=g2, eps=1e-6)
            with nc.Block() as block:
                @block.vector
                def _(dve):
                    dve.tensor_tensor(x[:], x[:], hid[:], ALU.add).then_inc(s, 1)
            route(nc, w2, ps, cols, w_router, order, combine)
            experts(nc, w2, ps, cols, a["wg"], a["wu"], a["wd"], combine, x)
            stored = w2.sem("out_stored")
            with nc.Block() as block:
                @block.sync
                def _(sp):
                    sp.dma_start(tokens(out), x[:]).then_inc(stored, 16)
                    sp.wait_ge(stored, 16)


def shape_tables():
    t = np.arange(S, dtype=np.float32)
    f = (1.0 / 10000.0 ** (np.arange(0, D, 2, dtype=np.float32) / D)).astype(np.float32)
    ang = np.einsum("i,j->ij", t, f)
    cos, sin = np.cos(ang).T, np.sin(ang).T
    head = np.arange(P) % D
    sign_pairs = np.where(head % 2, 1.0, -1.0)[:, None].astype(np.float32)
    sign_halves = np.where(head >= D // 2, 1.0, -1.0)[:, None].astype(np.float32)
    return {"cos_pairs": cos[head // 2], "sin_pairs": sin[head // 2] * sign_pairs,
            "cos_halves": cos[head % (D // 2)], "sin_halves": sin[head % (D // 2)] * sign_halves,
            "blocks": (np.arange(P)[:, None] // D == np.arange(P)[None] // D).astype(np.float32),
            "order": np.tile(E - np.arange(E, dtype=np.float32), (T, 1))}


def kernel(**inputs):
    import concourse.bacc as _bacc
    from concourse.bass_utils import run_bass_kernel_spmd as _run

    i = {k: np.asarray(v) for k, v in inputs.items()}
    head = np.arange(P)
    pairs = head ^ 1
    halves = head ^ (D // 2)
    arrays = {
        "x": i["L0_attn_x"][0], "Wqkv": i["L0_attn_Wqkv"], "bqk": i["L0_attn_bqkv"][:2 * P].reshape(2, P).T,
        "bv": i["L0_attn_bqkv"][2 * P:], "Wout": i["L0_attn_Wout"],
        "bout": i["L0_attn_bout"], "fast_bT": i["L0_ffn_fast_b"].T, "w_fc": i["L0_ffn_w_fc"],
        "w_proj": i["L0_ffn_w_proj"], "uT": i["L0_ffn_u"].T, "v": i["L0_ffn_v"], "gate": i["L0_ffn_gate"].reshape(1),
        "Wq": i["L1_attn_Wq"], "Wq_turned": i["L1_attn_Wq"][:, pairs], "Wk": i["L1_attn_Wk"],
        "Wk_turned": i["L1_attn_Wk"][:, pairs], "Wv": i["L1_attn_Wv"], "Wo": i["L1_attn_Wo"],
        "wq": i["L1_ffn_wq"], "wq_turned": i["L1_ffn_wq"][:, halves], "wk": i["L1_ffn_wk"],
        "wk_turned": i["L1_ffn_wk"][:, halves], "wv": i["L1_ffn_wv"], "wo": i["L1_ffn_wo"],
        "w_router": i["L1_ffn_w_router"], "wg": i["L1_ffn_wg"], "wu": i["L1_ffn_wu"], "wd": i["L1_ffn_wd"],
        "g1": i["L1_ffn_g1"], "g2": i["L1_ffn_g2"], **shape_tables(),
    }
    nc = _bacc.Bacc("TRN2", target_bir_lowering=False, num_devices=1)
    feed, aps = {}, {}
    for name, arr in arrays.items():
        arr = np.ascontiguousarray(arr)
        feed[f"in_{name}"] = arr
        aps[name] = nc.dram_tensor(f"in_{name}", arr.shape, mybir.dt.from_np(arr.dtype), kind="ExternalInput").ap()
    out = nc.dram_tensor("out", (S, P), F32, kind="ExternalOutput").ap()
    build(nc, aps, out)
    r = _run(nc, [feed], core_ids=[0])
    return r.results[0]["out"].reshape(1, S, P)
```

```python
from contextlib import ExitStack

import numpy as np

import concourse.bass as bass
from concourse import mybir

P = 128
S = 2048
T = S // P
H, D = 16, 8
HQ = 4
NQ = H // HQ
CH = 512
NC = S // CH
TC = CH // P
E = 8
HID = 384
HC = HID // P
F0 = 512
RANK = 16
STACK = 8 * D
KROWS = 96
Q_PARTS = (0, 1, 2, 0, 1, 2, 0, 1)
K_PARTS = (0, 0, 0, 1, 1, 1, 2, 2)
SM_SCALE = float(1.0 / np.sqrt(D))

F32 = mybir.dt.float32
BF16 = mybir.dt.bfloat16
ALU = mybir.AluOpType
ACT = mybir.ActivationFunctionType
AX = mybir.AxisListType
PAIR_OF_ONES = float(np.array([0x3F803F80], np.uint32).view(np.float32)[0])
FLOOR = -3.0e38
MASKED = -1.0e30

GROUPS = [(c, t) for c in range(NC) for t in range(TC * (c + 1))]
NG = len(GROUPS)
DIAG = [k for k, (c, t) in enumerate(GROUPS) if t >= TC * c]
LAST = [max(k for k, (c, t) in enumerate(GROUPS) if c == cc) for cc in range(NC)]
ALONE, PAIRED = 6, 3
RING = 4


def first_pass_order():
    order, late = [], []
    for cq in range(NC):
        for n, (g, i, kc) in enumerate((g, i, kc) for g in range(HQ) for i in range(TC) for kc in range(cq + 1)):
            if n == 4:
                order += late
            order.append(("max", cq, g, i, kc))
        late = [("turn", cq)]
    return order + late


UNITS = first_pass_order()
NU = len(UNITS)
LEAD = 60
RATIO = 5.6
READ = 58


def unit_columns(u):
    if UNITS[u][0] == "turn":
        return P + READ
    _, cq, _, i, kc = UNITS[u]
    return (P * (i + 1) if kc == cq else CH) + READ


def group_columns(k):
    cq, t = GROUPS[k]
    return CH - max(0, t - TC * cq) * P


def first_pass_steps():
    steps, owed, k = [[] for _ in range(NG)], 0.0, 0
    for u in range(LEAD, NU - 1):
        while owed >= RATIO * group_columns(k):
            owed -= RATIO * group_columns(k)
            k += 1
        steps[k].append((0, u))
        owed += unit_columns(u)
    k += 1
    steps[k].append((0, NU - 1))
    k += 1
    total = sum(unit_columns(u) for u in range(LEAD))
    left = sum(group_columns(n) for n in range(k, NG - 1))
    done, passed = 0.0, group_columns(k)
    for u in range(LEAD):
        while done > total * passed / left and k < NG - 2:
            k += 1
            passed += group_columns(k)
        steps[k].append((1, u))
        done += unit_columns(u)
    return steps


STEPS = first_pass_steps()
STAGED = 16 * (len(Q_PARTS) + len(K_PARTS) + 1)
assert NG % RING == 0


def first_bank(u, alone):
    return u % (ALONE if alone else PAIRED)


def first_free(u):
    return u + 1 + (1 if u < NU % PAIRED else 0)


class Chain:

    def __init__(self, eng, sem):
        self.eng, self.sem, self.n = eng, sem, 0

    def then(self, ins):
        self.n += 1
        ins.then_inc(self.sem, 1)
        self.eng.wait_ge(self.sem, self.n)


class Core:

    def __init__(self, nc, ctx):
        self.nc, self.ctx = nc, ctx

    def sb(self, name, shape, dt=F32):
        return self.ctx.enter_context(self.nc.sbuf_tensor(name, shape, dt))

    def sem(self, name):
        return self.ctx.enter_context(self.nc.semaphore(name))

    def dram(self, name, shape, dt):
        return self.nc.dram_tensor(name, shape, dt, kind="Internal").ap()


def fresh(eng, value, most):
    if value is None or isinstance(value, int):
        return value
    with eng.register() as reg:
        eng.reg_mov(reg, value)
        return eng.snap(reg, min_val=0, max_val=most)


def wait_apart(eng, sem, value, ticks):
    eng.wait_ge(sem, value)
    eng.sem_inc(ticks, 1)


def load(nc, core, tag, pairs):
    landed = core.sem(f"{tag}_landed")
    with nc.Block() as block:
        @block.sync
        def _(sp):
            for dst, src in pairs[0::2]:
                sp.dma_start(dst, src).then_inc(landed, 16)
            sp.wait_ge(landed, 16 * len(pairs))

        @block.scalar
        def _(act):
            for dst, src in pairs[1::2]:
                act.dma_start(dst, src).then_inc(landed, 16)


def constants(nc, core, c):
    made = core.sem("const_made")
    with nc.Block() as block:
        @block.gpsimd
        def _(pool):
            ch = Chain(pool, made)
            for name, word in (("qs", 0.0), ("ks", PAIR_OF_ONES)):
                ch.then(pool.memset(c[name][STACK:KROWS].rearrange("p a h t -> p (a h t)").bitcast(F32), word))
            ch.then(pool.memset(c["ident"][:], 0.0))
            ch.then(pool.memset(c["identb"][:], 0.0))
            ch.then(pool.memset(c["future"][:], 0.0))
            ch.then(pool.affine_select(out=c["ident"][:], in_=c["ident"][:], compare_op=ALU.not_equal, fill=1.0,
                                       base=0, pattern=[[-1, P]], channel_multiplier=1))
            ch.then(pool.affine_select(out=c["identb"][:], in_=c["identb"][:], compare_op=ALU.not_equal, fill=1.0,
                                       base=0, pattern=[[-1, P]], channel_multiplier=1))
            ch.then(pool.affine_select(out=c["future"][:], in_=c["future"][:], compare_op=ALU.is_ge, fill=MASKED,
                                       base=0, pattern=[[-1, P]], channel_multiplier=1))


def norm_transpose(nc, core, ps, ident, tag, src, tok, cols, rms_gain=None, eps=1e-5):
    st = core.sb(f"{tag}_st", [P, T, 6])
    mv = core.sb(f"{tag}_mv", [P, T, 2])
    var = core.sb(f"{tag}_var", [P, T])
    root = core.sb(f"{tag}_root", [P, T])
    rstd = core.sb(f"{tag}_rstd", [P, T])
    chain = core.sem(f"{tag}_chain")
    var_ready, root_ready = core.sem(f"{tag}_var"), core.sem(f"{tag}_root")
    tok_ready, transposed, moved = core.sem(f"{tag}_tok"), core.sem(f"{tag}_tr"), core.sem(f"{tag}_moved")
    with nc.Block() as block:
        @block.vector
        def _(dve):
            ch = Chain(dve, chain)
            for t in range(T):
                last = dve.bn_stats(st[:, t, :], src[:, t, :])
            ch.then(last)
            for t in range(T):
                last = dve.bn_aggr(mv[:, t, :], st[:, t, :])
            ch.then(last)
            if rms_gain is None:
                dve.tensor_scalar(var[:], mv[:, :, 1], eps, None, ALU.add).then_inc(var_ready, 1)
            else:
                ch.then(dve.tensor_tensor(var[:], mv[:, :, 0], mv[:, :, 0], ALU.mult))
                dve.scalar_tensor_tensor(out=var[:], in0=mv[:, :, 1], scalar=eps, in1=var[:],
                                         op0=ALU.add, op1=ALU.add).then_inc(var_ready, 1)
            dve.wait_ge(root_ready, 1)
            ch.then(dve.reciprocal(rstd[:], root[:]))
            for t in range(T):
                if rms_gain is None:
                    dve.tensor_scalar(tok[:, t, :], src[:, t, :], mv[:, t, 0:1], rstd[:, t:t + 1],
                                      ALU.subtract, ALU.mult).then_inc(tok_ready, 1)
                else:
                    dve.scalar_tensor_tensor(out=tok[:, t, :], in0=src[:, t, :], scalar=rstd[:, t:t + 1],
                                             in1=rms_gain[:], op0=ALU.mult, op1=ALU.mult).then_inc(tok_ready, 1)

        @block.scalar
        def _(act):
            act.wait_ge(var_ready, 1)
            act.activation(root[:], var[:], ACT.Sqrt).then_inc(root_ready, 1)
            for n in range(NC):
                act.wait_ge(transposed, n + 1)
                act.copy(cols[:, n * CH:(n + 1) * CH], ps[:, n, :]).then_inc(moved, 1)

        @block.tensor
        def _(pe):
            for t in range(T):
                pe.wait_ge(tok_ready, t + 1)
                ins = pe.transpose(ps[:, t // TC, (t % TC) * P:(t % TC + 1) * P], tok[:, t, :], ident[:])
                if t % TC == TC - 1:
                    ins.then_inc(transposed, 1)


def split_parts(dve, ch, src, parts, rest):
    ch.then(dve.tensor_copy(parts[:, 0, :], src))
    ch.then(dve.tensor_tensor(rest, src, parts[:, 0, :], ALU.subtract))
    ch.then(dve.tensor_copy(parts[:, 1, :], rest))
    ch.then(dve.tensor_tensor(rest, rest, parts[:, 1, :], ALU.subtract))
    return dve.tensor_copy(parts[:, 2, :], rest)


def project_values(pe, ps, cols, wv, ready, free, v):
    for n in range(NC):
        for i in range(TC):
            t = n * TC + i
            ins = pe.matmul(ps[:, 4 + n, i * P:(i + 1) * P], cols[:, t * P:(t + 1) * P], wv, start=True, stop=True)
        ins.then_inc(ready, 1)


def qkv_plain(nc, core, ps, tag, cols, wqkv, bias, bias_v, values, parts_dram):
    flat = core.sb(f"{tag}_qk", [P, 2, S])
    rest = core.sb(f"{tag}_rest", [P, S])
    parts = core.sb(f"{tag}_parts", [P, 2, 3, S], BF16)
    biask = core.sb(f"{tag}_biask", [P, 1])
    mm, moved, chain = core.sem(f"{tag}_mm"), core.sem(f"{tag}_moved"), core.sem(f"{tag}_chain")
    vmm, kb, split, stored = core.sem(f"{tag}_vmm"), core.sem(f"{tag}_kb"), core.sem(f"{tag}_split"), core.sem(f"{tag}_stored")
    with nc.Block() as block:
        @block.tensor
        def _(pe):
            for x in range(2):
                for n in range(NC):
                    if x:
                        pe.wait_ge(moved, n + 1)
                    pe.matmul(ps[:, n, :], wqkv[:, x * P:(x + 1) * P], cols[:, n * CH:(n + 1) * CH],
                              start=True, stop=True).then_inc(mm, 1)
            project_values(pe, ps, cols, wqkv[:, 2 * P:3 * P], vmm, None, None)

        @block.scalar
        def _(act):
            act.wait_ge(kb, 1)
            for x in range(2):
                for n in range(NC):
                    act.wait_ge(mm, x * NC + n + 1)
                    act.activation(flat[:, x, n * CH:(n + 1) * CH], ps[:, n, :], ACT.Identity,
                                   bias=(biask[:] if x else bias[:, 0:1]),
                                   scale=(SM_SCALE if x else 1.0)).then_inc(moved, 1)

        @block.vector
        def _(dve):
            ch = Chain(dve, chain)
            dve.tensor_scalar(biask[:], bias[:, 1:2], SM_SCALE, None, ALU.mult).then_inc(kb, 1)
            for x in range(2):
                dve.wait_ge(moved, NC * (x + 1))
                split_parts(dve, ch, flat[:, x, :], parts[:, x], rest[:]).then_inc(split, 1)
            for n in range(NC):
                dve.wait_ge(vmm, n + 1)
                dve.tensor_tensor(values[:, n * TC:(n + 1) * TC, :],
                                  ps[:, 4 + n, :].rearrange("p (a b) -> p a b", a=TC),
                                  bias_v[:].rearrange("p (o b) -> p o b", o=1).to_broadcast([P, TC, P]), ALU.add)

        @block.sync
        def _(sp):
            for x in range(2):
                sp.wait_ge(split, x + 1)
                sp.dma_start(parts_dram[x].rearrange("a p t -> p a t"), parts[:, x]).then_inc(stored, 16)
            sp.wait_ge(stored, 32)


def qkv_rope(nc, core, ps, tag, cols, wq, wqr, wk, wkr, wv, cos, sin, values, finish, k_scale, parts_dram=None,
             out=None):
    flat = out if out is not None else core.sb(f"{tag}_qk", [P, 2, S])
    turn = core.sb(f"{tag}_turn", [P, S])
    mm, used, chain = core.sem(f"{tag}_mm"), core.sem(f"{tag}_used"), core.sem(f"{tag}_chain")
    vmm, split, stored = core.sem(f"{tag}_vmm"), core.sem(f"{tag}_split"), core.sem(f"{tag}_stored")
    vmoved = core.sem(f"{tag}_vmoved")
    parts = core.sb(f"{tag}_parts", [P, 2, 3, S], BF16) if parts_dram is not None else None
    with nc.Block() as block:
        @block.tensor
        def _(pe):
            for x, (w, wr) in enumerate(((wq, wqr), (wk, wkr))):
                for n in range(NC):
                    u = x * NC + n
                    if u >= 2:
                        pe.wait_ge(used, 2 * (u - 1))
                    for y, ww in enumerate((w, wr)):
                        ins = pe.matmul(ps[:, 2 * (u % 2) + y, :], ww, cols[:, n * CH:(n + 1) * CH],
                                        start=True, stop=True)
                    ins.then_inc(mm, 1)
            project_values(pe, ps, cols, wv, vmm, None, None)

        @block.vector
        def _(dve):
            ch = Chain(dve, chain)
            for x in range(2):
                s = k_scale if x else 1.0
                for n in range(NC):
                    u = x * NC + n
                    sl = slice(n * CH, (n + 1) * CH)
                    dve.wait_ge(mm, u + 1)
                    dve.scalar_tensor_tensor(out=flat[:, x, sl], in0=ps[:, 2 * (u % 2), :], scalar=s,
                                             in1=cos[:, sl], op0=ALU.mult, op1=ALU.mult).then_inc(used, 1)
                    dve.scalar_tensor_tensor(out=turn[:, sl], in0=ps[:, 2 * (u % 2) + 1, :], scalar=s,
                                             in1=sin[:, sl], op0=ALU.mult, op1=ALU.mult).then_inc(used, 1)
                dve.wait_ge(used, 2 * NC * (x + 1))
                ch.then(dve.tensor_tensor(flat[:, x, :], flat[:, x, :], turn[:], ALU.add))
                if finish == "relu":
                    ch.then(dve.tensor_scalar(flat[:, x, :], flat[:, x, :], 0.0, None, ALU.max))
                else:
                    split_parts(dve, ch, flat[:, x, :], parts[:, x], turn[:]).then_inc(split, 1)
                    dve.wait_ge(split, x + 1)

        @block.scalar
        def _(act):
            for n in range(NC):
                act.wait_ge(vmm, n + 1)
                act.copy(values[:, n * TC:(n + 1) * TC, :],
                         ps[:, 4 + n, :].rearrange("p (a b) -> p a b", a=TC)).then_inc(vmoved, 1)

        if parts_dram is not None:
            @block.sync
            def _(sp):
                for x in range(2):
                    sp.wait_ge(split, x + 1)
                    sp.dma_start(parts_dram[x].rearrange("a p t -> p a t"), parts[:, x]).then_inc(stored, 16)
                sp.wait_ge(stored, 32)


def attention(nc, core, ps, tag, parts_dram, values, c, ctxu, scratch):
    qs, ks = c["qs"], c["ks"]
    probs = core.sb(f"{tag}_probs", [P, RING, HQ, CH])
    vq = core.sb(f"{tag}_vq", [P, T, HQ, 32])
    RC = HQ * TC
    part_max = core.sb(f"{tag}_pmax", [P, NC, RC, NC])
    neg_max = core.sb(f"{tag}_nmax", [P, NC, RC])
    max_parts = core.sb(f"{tag}_mparts", [P, NC, 2, RC], BF16)
    max_rows = core.sb(f"{tag}_mrows", [2 * RC, NC, P], BF16)
    dens = core.sb(f"{tag}_dens", [P, HQ * S // P])
    rdens = core.sb(f"{tag}_rdens", [P, HQ * S // P])
    rrows = core.sb(f"{tag}_rrows", [P, S])
    nothing = core.sb(f"{tag}_nothing", [P, 8])
    qs2 = qs[:].rearrange("p a h t -> p (a h t)")
    ks2 = ks[:].rearrange("p a h t -> p (a h t)")
    ctx2 = ctxu[:].rearrange("p a t -> p (a t)")
    QB = HQ * S
    max_dram, den_dram, rden_dram = scratch

    prepared, ticks, ticks_pool = core.sem(f"{tag}_prepared"), core.sem(f"{tag}_ticks"), core.sem(f"{tag}_ticks_pool")
    with nc.Block() as block:
        @block.vector
        def _(dve):
            dve.memset(part_max[:], FLOOR)
            dve.memset(ctxu[:, 0, :], 1.0)
            dve.memset(vq[:], 0.0).then_inc(prepared, 1)
            dve.wait_ge(prepared, 1)
            dve.memset(vq[:, :, :, D:D + 1], 1.0)

    staged = core.sem(f"{tag}_staged")
    v_placed = core.sem(f"{tag}_v_placed")
    a_scored = core.sem(f"{tag}_a_scored")
    a_free = core.sem(f"{tag}_a_free")
    neg_ready = core.sem(f"{tag}_neg_ready")
    chain = core.sem(f"{tag}_chain")
    rows_ready = core.sem(f"{tag}_rows_ready")
    max_stored = core.sem(f"{tag}_max_stored")
    max_loaded = [core.sem(f"{tag}_max_loaded{n}") for n in range(2)]
    b_scored = core.sem(f"{tag}_b_scored")
    exped = core.sem(f"{tag}_exped")
    masked = core.sem(f"{tag}_masked")
    pv_done = core.sem(f"{tag}_pv_done")
    ctx_moved = core.sem(f"{tag}_ctx_moved")
    den_out, den_in = core.sem(f"{tag}_den_out"), core.sem(f"{tag}_den_in")
    rden_made, rden_out = core.sem(f"{tag}_rden_made"), core.sem(f"{tag}_rden_out")
    rden_in, scaled = core.sem(f"{tag}_rden_in"), core.sem(f"{tag}_scaled")
    B0, O0 = 3, 7

    with nc.Block() as block:
        @block.sync
        def _(sp):
            def stage(j, buf):
                for x, (stack, which) in enumerate(((qs2, Q_PARTS), (ks2, K_PARTS))):
                    for r, part in enumerate(which):
                        sp.dma_start(
                            stack[r * D:(r + 1) * D, bass.ds(buf * QB, QB)].rearrange("d (h t) -> d h t", h=HQ),
                            parts_dram[x, part, bass.ds(j * HQ * D, HQ * D), :].rearrange("(h d) t -> d h t", h=HQ)
                        ).then_inc(staged, 16)

                sp.dma_start(qs2[STACK:STACK + 2, bass.ds(buf * QB, QB)],
                             qs2[STACK + 2:STACK + 4, bass.ds(buf * QB, QB)]).then_inc(staged, 16)

            def maxima(j, buf, cq):
                sp.wait_ge(rows_ready, j * NC + cq + 1)
                sp.dma_start(max_dram[bass.ds(j, 1), cq].rearrange("o r q -> (o r) q"),
                             max_rows[:, cq, :]).then_inc(max_stored, 16)
                sp.wait_ge(max_stored, j * 16 * NC + 16 * (NC + cq + 1))
                sp.dma_start(qs[STACK:STACK + 2, bass.ds(buf, 1), :, cq * CH:(cq + 1) * CH],
                             max_dram[bass.ds(j, 1), cq].rearrange("o (a g i) q -> a o g (i q)", a=2, g=HQ)
                             ).then_inc(max_loaded[cq % 2], 16)

            def normalise(j):
                sp.wait_ge(ctx_moved, j * NC + 1)
                sp.dma_start(den_dram[bass.ds(j, 1)].rearrange("o g t -> (o g) t"),
                             ctx2[D:P:32, bass.ds(j * S, S)]).then_inc(den_out, 16)
                sp.wait_ge(den_out, j * 16 + 16)
                sp.dma_start(dens[:], den_dram[bass.ds(j, 1)].rearrange("o g (a b) -> (o g a) b", b=HQ * S // P)
                             ).then_inc(den_in, 16)
                sp.wait_ge(rden_made, j + 1)
                sp.dma_start(rden_dram[bass.ds(j, 1)].rearrange("o g (a b) -> (o g a) b", b=HQ * S // P),
                             rdens[:]).then_inc(rden_out, 16)
                sp.wait_ge(rden_out, j * 16 + 16)
                sp.wait_ge(scaled, j + 1)
                for g in range(HQ):
                    sp.dma_start(rrows[32 * g:32 * g + 32, :],
                                 rden_dram[bass.ds(j, 1), g, :].to_broadcast([32, S])).then_inc(rden_in, 16)

            def body(j, ahead):
                maxima(j, j % 2, 1)
                if ahead:
                    sp.wait_ge(pv_done, j * NG + RING)
                    stage(j + 1, (j + 1) % 2)
                normalise(j)
                maxima(j, j % 2, 2)
                maxima(j, j % 2, 3)
                if ahead:
                    maxima(j + 1, (j + 1) % 2, 0)

            stage(0, 0)
            maxima(0, 0, 0)
            with sp.Fori(0, NQ - 1) as j:
                body(j, True)
            body(NQ - 1, False)
            normalise(NQ)

        @block.tensor
        def _(pe):
            def first_unit(j, buf, u, alone):
                kind, cq = UNITS[u][:2]
                bank = first_bank(u, alone)
                if alone:
                    if u >= ALONE:
                        pe.wait_ge(a_free, u - ALONE + 1 + PAIRED)
                elif kind == "turn":
                    wait_apart(pe, a_free, j * NU + first_free(u), ticks)
                else:
                    pe.wait_ge(a_free, j * NU + first_free(u))
                if kind == "turn":
                    wait_apart(pe, neg_ready, j * NC + cq + 1, ticks)
                    pe.transpose(ps[0:2 * RC, bank, 0:P // 2].bitcast(BF16),
                                 max_parts[:, cq].rearrange("p a r -> p (a r)"), c["identb"][:]).then_inc(a_scored, 1)
                    return
                _, _, g, i, kc = UNITS[u]
                diagonal = kc == cq
                w = P * (i + 1) if diagonal else CH
                ins = pe.matmul(ps[:, bank, 0:w], qs2[0:KROWS, bass.ds(buf * QB + g * S + cq * CH + i * P, P)],
                                ks2[0:KROWS, bass.ds(buf * QB + g * S + kc * CH, w)], start=True, stop=not diagonal)
                if diagonal:
                    ins = pe.matmul(ps[:, bank, w - P:w], c["identb"][:], c["future"][:], start=False, stop=True)
                ins.then_inc(a_scored, 1)

            def scores(j, buf, k, heads):
                cq, t = GROUPS[k]
                skip = max(0, t - TC * cq) * P
                for g in heads:
                    pe.wait_ge(exped, j * HQ * NG + HQ * k + g + 1)
                    pe.matmul(ps[:, B0 + g, skip:CH], ks2[0:KROWS, bass.ds(buf * QB + g * S + t * P, P)],
                              qs2[0:KROWS, bass.ds(buf * QB + g * S + cq * CH + skip, CH - skip)],
                              start=True, stop=True).then_inc(b_scored, 1)

            def product(j, k):
                cq, t = GROUPS[k]
                skip = max(0, t - TC * cq) * P
                pe.wait_ge(exped, j * HQ * NG + HQ * k + 2 * HQ)
                if k in DIAG:
                    pe.wait_ge(masked, j * len(DIAG) + DIAG.index(k) + 1)
                if t == 0:
                    pe.wait_ge(ctx_moved, j * NC + cq + 1)
                for g in range(HQ):
                    ins = pe.matmul(ps[32 * g:32 * g + 32, O0, skip:CH], vq[:, t, g, :],
                                    probs[:, k % RING, g, skip:CH], start=(t == 0), stop=(k == LAST[cq]),
                                    skip_group_check=True)
                ins.then_inc(pv_done, 1)

            def first_pass_alone():
                pe.wait_ge(staged, STAGED)
                for u in range(LEAD):
                    first_unit(0, 0, u, True)
                pe.wait_ge(a_free, LEAD + PAIRED)

            def both_passes(j, bufb, bufa, ahead):
                pe.wait_ge(v_placed, j + 1)
                entered = False
                for k in range(NG):
                    bufb, bufa = fresh(pe, bufb, 1), fresh(pe, bufa, 1)
                    share = [(n, u) for n, u in STEPS[k] if ahead or not n]

                    def some(n):
                        for on, u in share[:n]:
                            first_unit(j + on, bufa if on else bufb, u, False)
                        del share[:n]

                    if share and share[0][0] and not entered:
                        pe.wait_ge(staged, (j + 2) * STAGED)
                        entered = True
                    cq, t = GROUPS[k]
                    if t == 0:
                        pe.wait_ge(max_loaded[cq % 2], j * 8 * NC + 16 * (cq // 2 + 1))
                    for heads in ((0,), (1,), (2,), (3,)):
                        some(1)
                        scores(j, bufb, k, heads)
                    some(1)
                    if k:
                        product(j, k - 1)
                    some(len(share))
                product(j, NG - 1)

            first_pass_alone()
            with pe.Fori(0, NQ - 1) as j:
                both_passes(j, j % 2, (j + 1) % 2, True)
            both_passes(NQ - 1, (NQ - 1) % 2, None, False)

        @block.scalar
        def _(act):
            def body(j):
                for k, (cq, t) in enumerate(GROUPS):
                    skip = max(0, t - TC * cq) * P
                    act.wait_ge(pv_done, j * NG + k + 1)
                    for g in range(HQ):
                        act.wait_ge(b_scored, j * HQ * NG + HQ * k + g + 1)
                        act.activation(probs[:, k % RING, g, skip:CH], ps[:, B0 + g, skip:CH],
                                       ACT.Exp).then_inc(exped, 1)

            with act.Fori(0, NQ) as j:
                body(j)

        @block.gpsimd
        def _(pool):
            def mask(j, n):
                k = DIAG[n]
                cq, t = GROUPS[k]
                skip = (t - TC * cq) * P
                tri = probs[:, k % RING, :, skip:skip + P]
                wait_apart(pool, exped, j * HQ * NG + HQ * k + 2 * HQ, ticks_pool)
                pool.affine_select(out=tri, in_=tri, compare_op=ALU.is_ge, fill=0.0, base=0,
                                   pattern=[[0, HQ], [1, P]], channel_multiplier=-1).then_inc(masked, 1)

            def scale(j):
                pool.wait_ge(rden_in, j * 64 + 64)
                ctx = ctx2[:, bass.ds(j * S, S)]
                pool.tensor_tensor(ctx, ctx, rrows[:], ALU.mult).then_inc(scaled, 1)

            pool.memset(nothing[:, 0:1], 0.0).then_inc(scaled, 1)
            with pool.Fori(0, NQ) as j:
                for n in range(len(DIAG)):
                    mask(j, n)
                    if n == 3 * TC - 1:
                        scale(j)
            scale(NQ)

        @block.vector
        def _(dve):
            def place_values(j):
                dve.tensor_copy(vq[:, :, :, 0:D],
                                values[:].rearrange("p t (q d) -> p q t d", d=HQ * D)[:, bass.ds(j, 1)]
                                .rearrange("p o t (h d) -> p (o t) h d", h=HQ)).then_inc(v_placed, 1)

            def first_unit(j, alone, u):
                kind, cq = UNITS[u][:2]
                bank = first_bank(u, alone)
                dve.wait_ge(a_scored, j * NU + u + 1)
                if kind == "turn":
                    dve.wait_ge(max_stored, j * 16 * NC + 16 * (cq + 1))
                    dve.tensor_copy(max_rows[:, cq, :], ps[0:2 * RC, bank, 0:P // 2].bitcast(BF16)
                                    ).then_inc(rows_ready, 1)
                    dve.wait_ge(rows_ready, j * NC + cq + 1)
                    dve.memset(nothing[:, 1:2], 0.0).then_inc(a_free, 1)
                    return
                _, _, g, i, kc = UNITS[u]
                w = P * (i + 1) if kc == cq else CH
                dve.tensor_reduce(part_max[:, cq, g * TC + i, kc:kc + 1], ps[:, bank, 0:w], AX.X,
                                  ALU.max).then_inc(a_free, 1)
                if (g, i, kc) == (HQ - 1, TC - 1, cq):
                    dve.wait_ge(a_free, j * NU + u + 1 + PAIRED)
                    dve.tensor_reduce(neg_max[:, cq, :], part_max[:, cq], AX.X, ALU.max, negate=True
                                      ).then_inc(chain, 1)
                    dve.wait_ge(chain, j * 2 * NC + 2 * cq + 1)
                    dve.tensor_copy(max_parts[:, cq, 0, :], neg_max[:, cq, :]).then_inc(chain, 1)
                    dve.wait_ge(chain, j * 2 * NC + 2 * cq + 2)
                    dve.tensor_tensor(max_parts[:, cq, 1, :], neg_max[:, cq, :], max_parts[:, cq, 0, :],
                                      ALU.subtract).then_inc(neg_ready, 1)

            def move_context(j, cq):
                dve.wait_ge(pv_done, j * NG + LAST[cq] + 1 + RING)
                dve.tensor_copy(ctx2[:, bass.ds(j * S + S + cq * CH, CH)], ps[:, O0, :]
                                ).then_inc(ctx_moved, 1)

            def reciprocals(j):
                dve.wait_ge(den_in, j * 16 + 16)
                dve.reciprocal(rdens[:], dens[:]).then_inc(rden_made, 1)

            def body(j, ahead):
                for k in range(NG):
                    for cq in range(NC - 1):
                        if k == LAST[cq] + 2:
                            move_context(j, cq)
                    if k == 3:
                        reciprocals(j)
                    for n, u in STEPS[k]:
                        if ahead or not n:
                            first_unit(j + n, False, u)
                move_context(j, NC - 1)

            dve.memset(nothing[:, 2:3], 0.0).then_inc(a_free, PAIRED)
            dve.memset(nothing[:, 3:4], 0.0).then_inc(exped, HQ)
            dve.memset(nothing[:, 4:5], 0.0).then_inc(pv_done, RING)
            dve.memset(nothing[:, 5:6], 0.0).then_inc(ctx_moved, 1)
            dve.memset(nothing[:, 6:7], 0.0).then_inc(max_stored, 16 * NC)
            place_values(0)
            for u in range(LEAD):
                first_unit(0, True, u)
            with dve.Fori(0, NQ - 1) as j:
                body(j, True)
                place_values(j + 1)
            body(NQ - 1, False)
            reciprocals(NQ)


def project_context(nc, core, ps, tag, ctxu, wo, base, out):
    done, chain = core.sem(f"{tag}_done"), core.sem(f"{tag}_read")
    with nc.Block() as block:
        @block.tensor
        def _(pe):
            for n in range(NC):
                for i in range(TC):
                    t = n * TC + i
                    for q in range(NQ):
                        ins = pe.matmul(ps[:, n, i * P:(i + 1) * P], ctxu[:, 1 + q, t * P:(t + 1) * P], wo[:, q, :],
                                        start=(q == 0), stop=(q == NQ - 1))
                ins.then_inc(done, 1)

        @block.vector
        def _(dve):
            for n in range(NC):
                dve.wait_ge(done, n + 1)
                sl = slice(n * TC, (n + 1) * TC)
                dve.tensor_tensor(out[:, sl, :], ps[:, n, :].rearrange("p (a b) -> p a b", a=TC), base[:, sl, :],
                                  ALU.add).then_inc(chain, 1)


def ffn0_weights(nc, core, ps, ident, w_fc, w_proj, fbT, v, uT, gate, fcT, projT):
    G = F0 // P
    sums = core.sb("f0_sums", [P, G + 1])
    scale = core.sb("f0_scale", [P, G + 1])
    half = core.sb("f0_half", [P, 2, G + 1])
    tern = core.sb("f0_tern", [P, 2, F0])
    low = core.sb("f0_low", [P, 2, F0])
    m1 = core.sb("f0_m1", [RANK, P])
    chain, made, small = core.sem("f0_chain"), core.sem("f0_made"), core.sem("f0_small")
    turned, m1_moved, lowrank = core.sem("f0_turned"), core.sem("f0_m1_moved"), core.sem("f0_lowrank")
    wide = [w_fc[:].rearrange("p a b -> p (a b)"), w_proj[:]]
    with nc.Block() as block:
        @block.vector
        def _(dve):
            ch = Chain(dve, chain)
            ch.then(dve.tensor_reduce(sums[:, 0:G], w_fc[:], AX.X, ALU.add, apply_absolute_value=True))
            ch.then(dve.tensor_reduce(sums[:, G:G + 1], w_proj[:], AX.X, ALU.add, apply_absolute_value=True))
            ch.then(dve.tensor_scalar(scale[:, 0:G], sums[:, 0:G], 1.0 / P, 1e-5, ALU.mult, ALU.max))
            ch.then(dve.tensor_scalar(scale[:, G:], sums[:, G:], 1.0 / F0, 1e-5, ALU.mult, ALU.max))
            ch.then(dve.tensor_scalar(half[:, 0, :], scale[:], 0.5, None, ALU.mult))
            ch.then(dve.tensor_scalar(half[:, 1, :], scale[:], -0.5, None, ALU.mult))
            for x in range(2):
                for g in range(G):
                    s = g if x == 0 else G
                    sl = slice(g * P, (g + 1) * P)
                    w = wide[x][:, sl]
                    ch.then(dve.tensor_scalar(tern[:, x, sl], w, half[:, 0, s:s + 1], None, ALU.is_gt))
                    ch.then(dve.tensor_scalar(low[:, x, sl], w, half[:, 1, s:s + 1], None, ALU.is_lt))
                    ch.then(dve.tensor_tensor(tern[:, x, sl], tern[:, x, sl], low[:, x, sl], ALU.subtract))
                    ch.then(dve.tensor_tensor(tern[:, x, sl], tern[:, x, sl], w, ALU.subtract))
                    ch.then(dve.tensor_tensor(tern[:, x, sl], tern[:, x, sl], w, ALU.add))
                    dve.tensor_scalar(tern[:, x, sl], tern[:, x, sl], scale[:, s:s + 1], None,
                                      ALU.mult).then_inc(made, 1)
            dve.wait_ge(small, 1)
            dve.tensor_copy(m1[:], ps[0:RANK, 2, 0:P]).then_inc(m1_moved, 1)
            dve.wait_ge(turned, 1)
            dve.tensor_copy(projT[:].rearrange("p a b -> p (a b)"), ps[:, 1, :])
            ch.then(dve.tensor_copy(fcT[:], ps[:, 0, :]))
            dve.wait_ge(lowrank, 1)
            ch.then(dve.scalar_tensor_tensor(out=fcT[:], in0=ps[:, 3, :], scalar=gate[:, 0:1], in1=fcT[:],
                                             op0=ALU.mult, op1=ALU.add))

        @block.tensor
        def _(pe):
            pe.matmul(ps[0:RANK, 2, 0:P], fbT[:], v[:], start=True, stop=True).then_inc(small, 1)
            for x in range(2):
                for g in range(G):
                    pe.wait_ge(made, x * G + g + 1)
                    ins = pe.transpose(ps[:, x, g * P:(g + 1) * P], tern[:, x, g * P:(g + 1) * P], ident[:])
            ins.then_inc(turned, 1)
            pe.wait_ge(m1_moved, 1)
            pe.matmul(ps[:, 3, :], m1[:], uT[:], start=True, stop=True).then_inc(lowrank, 1)


def ffn0(nc, core, ps, cols, fcT, projT, acc):
    G = F0 // P
    relu = core.sb("ffn0_relu", [P, 2, G, CH])
    up, relued, squared, down, added = (core.sem(f"ffn0_{n}") for n in ("up", "relued", "squared", "down", "added"))
    with nc.Block() as block:
        @block.tensor
        def _(pe):
            for n in range(NC + 1):
                if n < NC:
                    for g in range(G):
                        if n:
                            pe.wait_ge(relued, (n - 1) * G + g + 1)
                        pe.matmul(ps[:, g, :], fcT[:, g * P:(g + 1) * P], cols[:, n * CH:(n + 1) * CH],
                                  start=True, stop=True).then_inc(up, 1)
                if n:
                    m = n - 1
                    pe.wait_ge(squared, n)
                    if m >= 2:
                        pe.wait_ge(added, m - 1)
                    for i in range(TC):
                        for g in range(G):
                            ins = pe.matmul(ps[:, 4 + m % 2, i * P:(i + 1) * P], relu[:, m % 2, g, i * P:(i + 1) * P],
                                            projT[:, g, :], start=(g == 0), stop=(g == G - 1))
                    ins.then_inc(down, 1)

        @block.scalar
        def _(act):
            for n in range(NC):
                if n >= 2:
                    act.wait_ge(down, n - 1)
                for g in range(G):
                    act.wait_ge(up, n * G + g + 1)
                    act.activation(relu[:, n % 2, g, :], ps[:, g, :], ACT.Relu).then_inc(relued, 1)

        @block.vector
        def _(dve):
            for n in range(NC + 1):
                if n < NC:
                    dve.wait_ge(relued, (n + 1) * G)
                    dve.tensor_tensor(relu[:, n % 2], relu[:, n % 2], relu[:, n % 2], ALU.mult).then_inc(squared, 1)
                if n:
                    m = n - 1
                    sl = slice(m * TC, (m + 1) * TC)
                    dve.wait_ge(down, n)
                    dve.tensor_tensor(acc[:, sl, :], ps[:, 4 + m % 2, :].rearrange("p (a b) -> p a b", a=TC),
                                      acc[:, sl, :], ALU.add).then_inc(added, 1)


def linear_attention(nc, core, ps, ident, qk, values, wo, blocks, acc):
    ktok = core.sb("la_ktok", [P, T, P])
    ones = core.sb("la_ones", [P, 1])
    vk = core.sb("la_vk", [P, P])
    kden = core.sb("la_kden", [P, P])
    ksum = core.sb("la_ksum", [P, 1])
    den = core.sb("la_den", [P, S])
    rden = core.sb("la_rden", [P, S])
    att = core.sb("la_att", [P, S])
    names = ("turned", "moved", "summed", "chain", "weights", "applied", "normed", "projected", "ones", "added")
    turned, moved, summed, chain, weights, applied, normed, projected, ones_made, added = (core.sem(f"la_{n}") for n in names)
    with nc.Block() as block:
        @block.tensor
        def _(pe):
            for t in range(T):
                ins = pe.transpose(ps[:, t // TC, (t % TC) * P:(t % TC + 1) * P], qk[:, 1, t * P:(t + 1) * P], ident[:])
                if t % TC == TC - 1:
                    ins.then_inc(turned, 1)
            pe.wait_ge(ones_made, 1)
            pe.wait_ge(moved, NC)
            for t in range(T):
                pe.matmul(ps[:, 4, 0:P], ktok[:, t, :], values[:, t, :], start=(t == 0), stop=(t == T - 1))
            for t in range(T):
                ins = pe.matmul(ps[:, 5, 0:1], ktok[:, t, :], ones[:], start=(t == 0), stop=(t == T - 1))
            ins.then_inc(summed, 1)
            pe.wait_ge(weights, 1)
            for n in range(NC):
                if n >= 1:
                    pe.wait_ge(normed, n)
                pe.matmul(ps[:, 6, :], kden[:], qk[:, 0, n * CH:(n + 1) * CH], start=True, stop=True)
                pe.matmul(ps[:, 7, :], vk[:], qk[:, 0, n * CH:(n + 1) * CH], start=True, stop=True).then_inc(applied, 1)
            for n in range(NC):
                pe.wait_ge(normed, n + 1)
                for i in range(TC):
                    t = n * TC + i
                    ins = pe.matmul(ps[:, n, i * P:(i + 1) * P], att[:, t * P:(t + 1) * P], wo[:], start=True, stop=True)
                ins.then_inc(projected, 1)

        @block.scalar
        def _(act):
            for n in range(NC):
                act.wait_ge(turned, n + 1)
                act.copy(ktok[:, n * TC:(n + 1) * TC, :],
                         ps[:, n, :].rearrange("p (a b) -> p a b", a=TC)).then_inc(moved, 1)

        @block.vector
        def _(dve):
            ch = Chain(dve, chain)
            dve.memset(ones[:], 1.0).then_inc(ones_made, 1)
            dve.wait_ge(summed, 1)
            ch.then(dve.tensor_copy(ksum[:], ps[:, 5, 0:1]))
            ch.then(dve.tensor_tensor(vk[:], ps[:, 4, 0:P], blocks[:], ALU.mult))
            dve.tensor_scalar(kden[:], blocks[:], ksum[:, 0:1], None, ALU.mult).then_inc(weights, 1)
            for n in range(NC):
                sl = slice(n * CH, (n + 1) * CH)
                dve.wait_ge(applied, n + 1)
                ch.then(dve.tensor_scalar(den[:, sl], ps[:, 6, :], 1e-6, None, ALU.add))
                ch.then(dve.reciprocal(rden[:, sl], den[:, sl]))
                dve.tensor_tensor(att[:, sl], ps[:, 7, :], rden[:, sl], ALU.mult).then_inc(normed, 1)
            for n in range(NC):
                sl = slice(n * TC, (n + 1) * TC)
                dve.wait_ge(projected, n + 1)
                dve.tensor_tensor(acc[:, sl, :], ps[:, n, :].rearrange("p (a b) -> p a b", a=TC), acc[:, sl, :],
                                  ALU.add).then_inc(added, 1)


def route(nc, core, ps, cols, w_router, order, combine):
    shape = [P, T, E]
    logits, left, pick, first, second, ex = (core.sb(f"rt_{n}", shape) for n in
                                             ("logits", "left", "pick", "first", "second", "ex"))
    best = core.sb("rt_best", [P, T])
    rank = core.sb("rt_rank", [P, T])
    best2 = core.sb("rt_best2", [P, T])
    tot = core.sb("rt_tot", [P, T])
    scored, chain, shifted, exped = core.sem("rt_scored"), core.sem("rt_chain"), core.sem("rt_shifted"), core.sem("rt_exped")

    def wide(x):
        return x[:].rearrange("p (t o) -> p t o", o=1).to_broadcast(shape)

    with nc.Block() as block:
        @block.tensor
        def _(pe):
            for t in range(T):
                ins = pe.matmul(ps[:, 0, t * E:(t + 1) * E], cols[:, t * P:(t + 1) * P], w_router[:], start=True, stop=True)
            ins.then_inc(scored, 1)

        @block.vector
        def _(dve):
            ch = Chain(dve, chain)

            def one_hot(values, top, out):
                ch.then(dve.tensor_reduce(top[:], values[:], AX.X, ALU.max))
                ch.then(dve.tensor_tensor(pick[:], values[:], wide(top), ALU.is_equal))
                ch.then(dve.tensor_tensor(pick[:], pick[:], order[:], ALU.mult))
                ch.then(dve.tensor_reduce(rank[:], pick[:], AX.X, ALU.max))
                ch.then(dve.tensor_tensor(out[:], order[:], wide(rank), ALU.is_equal))

            dve.wait_ge(scored, 1)
            ch.then(dve.tensor_copy(logits[:], ps[:, 0, 0:T * E].rearrange("p (t e) -> p t e", e=E)))
            one_hot(logits, best, first)
            ch.then(dve.scalar_tensor_tensor(out=left[:], in0=first[:], scalar=FLOOR, in1=logits[:],
                                             op0=ALU.mult, op1=ALU.add))
            one_hot(left, best2, second)
            dve.tensor_tensor(ex[:], logits[:], wide(best), ALU.subtract).then_inc(shifted, 1)
            ch.then(dve.tensor_tensor(first[:], first[:], second[:], ALU.add))
            dve.wait_ge(exped, 1)
            ch.then(dve.tensor_tensor(ex[:], ex[:], first[:], ALU.mult))
            ch.then(dve.tensor_reduce(tot[:], ex[:], AX.X, ALU.add))
            ch.then(dve.reciprocal(tot[:], tot[:]))
            ch.then(dve.tensor_tensor(combine[:], ex[:], wide(tot), ALU.mult))

        @block.scalar
        def _(act):
            act.wait_ge(shifted, 1)
            act.activation(ex[:], ex[:], ACT.Exp).then_inc(exped, 1)


def experts(nc, core, ps, cols, wg, wu, wd, combine, acc):
    silu = core.sb("moe_silu", [P, 2, CH])
    act_ = core.sb("moe_act", [P, 2, HC, CH])
    names = ("gu", "silued", "mixed", "down", "added")
    gu, silued, mixed, down, added = (core.sem(f"moe_{n}") for n in names)
    W_UNIT = NC * HC
    wcur = core.sb("moe_wcur", [P, 2, 2 * HID + HC * P])
    w_placed = [core.sem(f"moe_w_placed{b}") for b in range(2)]
    none = core.sb("moe_none", [P, 8])
    combine_by_expert = core.sb("moe_combine", [P, E, T])
    placed = core.sem("moe_placed")
    with nc.Block() as block:
        def weights(b):
            return wcur[:, b, 0:HID], wcur[:, b, HID:2 * HID], wcur[:, b, 2 * HID:]

        @block.tensor
        def _(pe):
            def expert(e, half):
                wgn, wun, _ = weights(half)
                pe.wait_ge(w_placed[half], e * 24 + 48)
                for n in range(NC):
                    for h in range(HC):
                        u = half * W_UNIT + n * HC + h
                        b = 2 * (u % 2)
                        pe.wait_ge(mixed, e * W_UNIT + u + 1)
                        pe.matmul(ps[:, b, :], wgn[:, h * P:(h + 1) * P], cols[:, n * CH:(n + 1) * CH],
                                  start=True, stop=True)
                        pe.matmul(ps[:, b + 1, :], wun[:, h * P:(h + 1) * P], cols[:, n * CH:(n + 1) * CH],
                                  start=True, stop=True).then_inc(gu, 1)
                    if n:
                        down_product(e, half, n - 1)
                down_product(e, half, NC - 1)

            def down_product(e, half, n):
                d = half * NC + n
                pe.wait_ge(mixed, e * W_UNIT + (d + 1) * HC + 2)
                pe.wait_ge(added, e * NC + d + 1)
                _, _, wdn = weights(half)
                for i in range(TC):
                    for h in range(HC):
                        ins = pe.matmul(ps[:, 4 + n % 2, i * P:(i + 1) * P], act_[:, n % 2, h, i * P:(i + 1) * P],
                                        wdn[:, h * P:(h + 1) * P], start=(h == 0), stop=(h == HC - 1))
                ins.then_inc(down, 1)

            with pe.Fori(0, E // 2) as pair:
                e = pair * 2
                for half in range(2):
                    expert(e, half)

        @block.sync
        def _(sp):
            with sp.Fori(0, E // 2) as pair:
                e = pair * 2
                for half in range(2):
                    sp.wait_ge(down, e * NC + NC * (half + 1))
                    wgn, wun, wdn = weights(half)
                    one = bass.ds(e + half, 1)
                    sp.dma_start(wgn, wg[one].rearrange("o d h -> (o d) h")).then_inc(w_placed[half], 16)
                    sp.dma_start(wun, wu[one].rearrange("o d h -> (o d) h")).then_inc(w_placed[half], 16)
                    sp.dma_start(wdn.rearrange("p (c d) -> p c d", c=HC),
                                 wd[one].rearrange("o (c p) d -> p (o c) d", p=P)).then_inc(w_placed[half], 16)

        @block.scalar
        def _(act):
            with act.Fori(0, E // 2) as pair:
                e = pair * 2
                for u in range(2 * W_UNIT):
                    act.wait_ge(gu, e * W_UNIT + u + 1)
                    act.wait_ge(mixed, e * W_UNIT + u + 1)
                    act.activation(silu[:, u % 2, :], ps[:, 2 * (u % 2), :], ACT.Silu).then_inc(silued, 1)

        @block.vector
        def _(dve):
            def add(e, half, n):
                d = half * NC + n
                dve.wait_ge(down, e * NC + d + 1 + 2 * NC)
                for i in range(TC):
                    t = n * TC + i
                    ins = dve.scalar_tensor_tensor(out=acc[:, t, :], in0=ps[:, 4 + n % 2, i * P:(i + 1) * P],
                                                   scalar=combine2[:, bass.ds(e * T + half * T + t, 1)],
                                                   in1=acc[:, t, :], op0=ALU.mult, op1=ALU.add)
                ins.then_inc(added, 1)

            combine2 = combine_by_expert[:].rearrange("p e t -> p (e t)")
            dve.memset(none[:, 0:1], 0.0).then_inc(mixed, 2)
            dve.memset(none[:, 1:2], 0.0).then_inc(added, 2)
            dve.memset(none[:, 2:3], 0.0).then_inc(down, 2 * NC)
            dve.tensor_copy(combine_by_expert[:], combine[:].rearrange("p t e -> p e t")).then_inc(placed, 1)
            dve.wait_ge(placed, 1)
            with dve.Fori(0, E // 2) as pair:
                e = pair * 2
                for half in range(2):
                    for n in range(NC):
                        for h in range(HC):
                            u = half * W_UNIT + n * HC + h
                            dve.wait_ge(silued, e * W_UNIT + u + 1)
                            if h == 0:
                                dve.wait_ge(down, e * NC + half * NC + n + 1 + 2 * NC - 2)
                            dve.tensor_tensor(act_[:, n % 2, h, :], ps[:, 2 * (u % 2) + 1, :], silu[:, u % 2, :],
                                              ALU.mult).then_inc(mixed, 1)
                        if n:
                            add(e, half, n - 1)
                    add(e, half, NC - 1)



def build(nc, a, out):
    with ExitStack() as outer:
        core = Core(nc, outer)
        ps = outer.enter_context(nc.psum_tensor("psum", [P, 8, CH], F32))
        c = {"ident": core.sb("ident", [P, P]), "identb": core.sb("identb", [P, P], BF16),
             "future": core.sb("future", [P, P], BF16),
             "qs": core.sb("qs", [P, 2, HQ, S], BF16), "ks": core.sb("ks", [P, 2, HQ, S], BF16)}
        ident = c["ident"]
        x = core.sb("x", [P, T, P])
        xn = core.sb("xn", [P, T, P])
        cols = core.sb("cols", [P, S])
        values = core.sb("values", [P, T, P])
        parts_dram = core.dram("parts", (2, 3, P, S), BF16)
        scratch = [[core.dram(f"maxima{n}", (NQ, NC, 2 * HQ * TC, P), BF16), core.dram(f"sums{n}", (NQ + 1, HQ, S), F32),
                    core.dram(f"rsums{n}", (NQ + 1, HQ, S), F32)] for n in range(2)]

        def tokens(ap):
            return ap.rearrange("(t p) d -> p t d", p=P)

        def quad_rows(wo, dst):
            return [(dst[32 * g:32 * g + D, :, :], wo.rearrange("(q g d) n -> g d q n", q=NQ, g=HQ)[g])
                    for g in range(HQ)]

        def zero(tag, tensors):
            z = core.sem(f"{tag}_zero")
            with nc.Block() as block:
                @block.vector
                def _(dve):
                    for t in tensors:
                        dve.memset(t[:], 0.0).then_inc(z, 1)

        with ExitStack() as ctx0:
            w0 = Core(nc, ctx0)
            wo = w0.sb("wo0", [P, NQ, P])
            bout = w0.sb("bout", [P, P])
            zero("z0", [wo])
            constants(nc, core, c)
            with ExitStack() as early:
                e0 = Core(nc, early)
                wqkv, bias, bias_v = e0.sb("wqkv", [P, 3 * P]), e0.sb("bias", [P, 2]), e0.sb("bias_v", [P, P])
                w_fc, w_proj = e0.sb("w_fc", [P, F0 // P, P]), e0.sb("w_proj", [P, F0])
                fbT, v, uT, gate = e0.sb("fbT", [RANK, RANK]), e0.sb("v", [RANK, P]), e0.sb("uT", [RANK, F0]), e0.sb("gate", [P, 1])
                fcT, projT = e0.sb("fcT", [P, F0]), e0.sb("projT", [P, F0 // P, P])
                load(nc, core, "l0", [
                    (x[:], tokens(a["x"])), (wqkv[:], a["Wqkv"]),
                    (bias[:], a["bqk"]), (bias_v[:], a["bv"].partition_broadcast(P)),
                    (bout[:], a["bout"].partition_broadcast(P)),
                    (w_fc[:], a["w_fc"].rearrange("(g p) d -> p g d", p=P)), (w_proj[:], a["w_proj"]),
                    (fbT[:], a["fast_bT"]), (v[:], a["v"]), (uT[:], a["uT"]), (gate[:], a["gate"].partition_broadcast(P)),
                    *quad_rows(a["Wout"], wo)])
                norm_transpose(nc, e0, ps, ident, "n0", x, xn, cols)
                with ExitStack() as proj:
                    qkv_plain(nc, Core(nc, proj), ps, "p0", cols, wqkv, bias, bias_v, values, parts_dram)
                ffn0_weights(nc, e0, ps, ident, w_fc, w_proj, fbT, v, uT, gate, fcT, projT)
                b = core.sem("bout_added")
                with nc.Block() as block:
                    @block.vector
                    def _(dve):
                        for t in range(T):
                            dve.tensor_tensor(x[:, t, :], x[:, t, :], bout[:], ALU.add).then_inc(b, 1)
                ffn0(nc, e0, ps, cols, fcT, projT, x)
            ctxu = w0.sb("ctx0", [P, NQ + 1, S])
            with ExitStack() as att:
                attention(nc, Core(nc, att), ps, "a0", parts_dram, values, c, ctxu, scratch[0])
            project_context(nc, w0, ps, "o0", ctxu, wo, x, x)

        hid = core.sb("hid", [P, T, P])
        with ExitStack() as ctx1:
            w1 = Core(nc, ctx1)
            wo = w1.sb("wo1", [P, NQ, P])
            zero("z1", [wo])
            with ExitStack() as early:
                e1 = Core(nc, early)
                wl = e1.sb("wl", [P, 6, P])
                wf = e1.sb("wf", [P, 5, P])
                g1 = e1.sb("g1", [P, P])
                cos, sin = e1.sb("cos", [P, S]), e1.sb("sin", [P, S])
                blocks = e1.sb("blocks", [P, P])
                load(nc, w1, "l1", [
                    *[(wl[:, i, :], a[n]) for i, n in enumerate(("Wq", "Wq_turned", "Wk", "Wk_turned", "Wv", "Wo"))],
                    *[(wf[:, i, :], a[n]) for i, n in enumerate(("wq", "wq_turned", "wk", "wk_turned", "wv"))],
                    (g1[:], a["g1"].partition_broadcast(P)), (blocks[:], a["blocks"]),
                    (cos[:], a["cos_pairs"]), (sin[:], a["sin_pairs"]), *quad_rows(a["wo"], wo)])
                norm_transpose(nc, e1, ps, ident, "n1", x, xn, cols)
                with ExitStack() as lin:
                    l1 = Core(nc, lin)
                    qk = l1.sb("la_qk", [P, 2, S])
                    qkv_rope(nc, l1, ps, "pl", cols, *(wl[:, i, :] for i in range(5)), cos, sin, values, "relu", 1.0, out=qk)
                    linear_attention(nc, l1, ps, ident, qk, values, wl[:, 5, :], blocks, x)
                load(nc, w1, "l2", [(cos[:], a["cos_halves"]), (sin[:], a["sin_halves"])])
                norm_transpose(nc, e1, ps, ident, "n2", xn, hid, cols, rms_gain=g1, eps=1e-6)
                qkv_rope(nc, e1, ps, "pf", cols, *(wf[:, i, :] for i in range(5)), cos, sin, values, "split", SM_SCALE,
                         parts_dram=parts_dram)
            ctxu = w1.sb("ctx1", [P, NQ + 1, S])
            with ExitStack() as att:
                attention(nc, Core(nc, att), ps, "a1", parts_dram, values, c, ctxu, scratch[1])
            project_context(nc, w1, ps, "o1", ctxu, wo, xn, hid)

        with ExitStack() as ctx2:
            w2 = Core(nc, ctx2)
            w_router, g2 = w2.sb("w_router", [P, E]), w2.sb("g2", [P, P])
            order, combine = w2.sb("order", [P, T, E]), w2.sb("combine", [P, T, E])
            s = w2.sem("hid_added")
            load(nc, w2, "l3", [
                (w_router[:], a["w_router"]),
                (g2[:], a["g2"].partition_broadcast(P)), (order[:], a["order"].partition_broadcast(P))])
            norm_transpose(nc, w2, ps, ident, "n3", hid, xn, cols, rms_gain=g2, eps=1e-6)
            with nc.Block() as block:
                @block.vector
                def _(dve):
                    dve.tensor_tensor(x[:], x[:], hid[:], ALU.add).then_inc(s, 1)
            route(nc, w2, ps, cols, w_router, order, combine)
            experts(nc, w2, ps, cols, a["wg"], a["wu"], a["wd"], combine, x)
            stored = w2.sem("out_stored")
            with nc.Block() as block:
                @block.sync
                def _(sp):
                    sp.dma_start(tokens(out), x[:]).then_inc(stored, 16)
                    sp.wait_ge(stored, 16)


def shape_tables():
    t = np.arange(S, dtype=np.float32)
    f = (1.0 / 10000.0 ** (np.arange(0, D, 2, dtype=np.float32) / D)).astype(np.float32)
    ang = np.einsum("i,j->ij", t, f)
    cos, sin = np.cos(ang).T, np.sin(ang).T
    head = np.arange(P) % D
    sign_pairs = np.where(head % 2, 1.0, -1.0)[:, None].astype(np.float32)
    sign_halves = np.where(head >= D // 2, 1.0, -1.0)[:, None].astype(np.float32)
    return {"cos_pairs": cos[head // 2], "sin_pairs": sin[head // 2] * sign_pairs,
            "cos_halves": cos[head % (D // 2)], "sin_halves": sin[head % (D // 2)] * sign_halves,
            "blocks": (np.arange(P)[:, None] // D == np.arange(P)[None] // D).astype(np.float32),
            "order": np.tile(E - np.arange(E, dtype=np.float32), (T, 1))}


def kernel(**inputs):
    import concourse.bacc as _bacc
    from concourse.bass_utils import run_bass_kernel_spmd as _run

    i = {k: np.asarray(v) for k, v in inputs.items()}
    head = np.arange(P)
    pairs = head ^ 1
    halves = head ^ (D // 2)
    arrays = {
        "x": i["L0_attn_x"][0], "Wqkv": i["L0_attn_Wqkv"], "bqk": i["L0_attn_bqkv"][:2 * P].reshape(2, P).T,
        "bv": i["L0_attn_bqkv"][2 * P:], "Wout": i["L0_attn_Wout"],
        "bout": i["L0_attn_bout"], "fast_bT": i["L0_ffn_fast_b"].T, "w_fc": i["L0_ffn_w_fc"],
        "w_proj": i["L0_ffn_w_proj"], "uT": i["L0_ffn_u"].T, "v": i["L0_ffn_v"], "gate": i["L0_ffn_gate"].reshape(1),
        "Wq": i["L1_attn_Wq"], "Wq_turned": i["L1_attn_Wq"][:, pairs], "Wk": i["L1_attn_Wk"],
        "Wk_turned": i["L1_attn_Wk"][:, pairs], "Wv": i["L1_attn_Wv"], "Wo": i["L1_attn_Wo"],
        "wq": i["L1_ffn_wq"], "wq_turned": i["L1_ffn_wq"][:, halves], "wk": i["L1_ffn_wk"],
        "wk_turned": i["L1_ffn_wk"][:, halves], "wv": i["L1_ffn_wv"], "wo": i["L1_ffn_wo"],
        "w_router": i["L1_ffn_w_router"], "wg": i["L1_ffn_wg"], "wu": i["L1_ffn_wu"], "wd": i["L1_ffn_wd"],
        "g1": i["L1_ffn_g1"], "g2": i["L1_ffn_g2"], **shape_tables(),
    }
    nc = _bacc.Bacc("TRN2", target_bir_lowering=False, num_devices=1)
    feed, aps = {}, {}
    for name, arr in arrays.items():
        arr = np.ascontiguousarray(arr)
        feed[f"in_{name}"] = arr
        aps[name] = nc.dram_tensor(f"in_{name}", arr.shape, mybir.dt.from_np(arr.dtype), kind="ExternalInput").ap()
    out = nc.dram_tensor("out", (S, P), F32, kind="ExternalOutput").ap()
    build(nc, aps, out)
    r = _run(nc, [feed], core_ids=[0])
    return r.results[0]["out"].reshape(1, S, P)
```

```python
from contextlib import ExitStack

import numpy as np

import concourse.bass as bass
from concourse import mybir

P = 128
S = 2048
T = S // P
H, D = 16, 8
HQ = 4
NQ = H // HQ
CH = 512
NC = S // CH
TC = CH // P
E = 8
HID = 384
HC = HID // P
F0 = 512
RANK = 16
STACK = 8 * D
KROWS = 96
Q_PARTS = (0, 1, 2, 0, 1, 2, 0, 1)
K_PARTS = (0, 0, 0, 1, 1, 1, 2, 2)
SM_SCALE = float(1.0 / np.sqrt(D))

F32 = mybir.dt.float32
F32R = mybir.dt.float32r
BF16 = mybir.dt.bfloat16
ALU = mybir.AluOpType
ACT = mybir.ActivationFunctionType
AX = mybir.AxisListType
PAIR_OF_ONES = float(np.array([0x3F803F80], np.uint32).view(np.float32)[0])
FLOOR = -3.0e38
MASKED = -1.0e30

GROUPS = [(c, t) for c in range(NC) for t in range(TC * (c + 1))]
NG = len(GROUPS)
DIAG = [k for k, (c, t) in enumerate(GROUPS) if t >= TC * c]
LAST = [max(k for k, (c, t) in enumerate(GROUPS) if c == cc) for cc in range(NC)]
ALONE, PAIRED = 6, 3
RING = 4


def first_pass_order():
    order, late = [], []
    for cq in range(NC):
        for n, (g, i, kc) in enumerate((g, i, kc) for g in range(HQ) for i in range(TC) for kc in range(cq + 1)):
            if n == 4:
                order += late
            order.append(("max", cq, g, i, kc))
        late = [("turn", cq)]
    return order + late


UNITS = first_pass_order()
NU = len(UNITS)
LEAD = 80
LEAD_FIRST = 40
RATIO = 4.6
RATIO_FIRST = 6.5
LAG = 2
SLACK = 2
READ = 58


def unit_columns(u):
    if UNITS[u][0] == "turn":
        return P + READ
    _, cq, _, i, kc = UNITS[u]
    return (P * (i + 1) if kc == cq else CH) + READ


def group_columns(k):
    cq, t = GROUPS[k]
    return CH - max(0, t - TC * cq) * P


def first_pass_steps(lead, ratio):
    steps, u, k, owed = [[] for _ in range(NG)], lead, 0, 0.0
    due = [(UNITS.index(("turn", cq)), GROUPS.index((cq, 0)) - SLACK) for cq in range(1, NC)]
    while u < NU:
        pace = ratio
        for turn, step in due:
            if u <= turn:
                left = sum(group_columns(n) for n in range(k, max(step, k + 1)))
                pace = max(pace, (sum(unit_columns(n) for n in range(u, turn + 1)) - owed) / left)
        owed -= pace * group_columns(k)
        while u < NU and owed < 0 and not (u == NU - 1 and steps[k]):
            steps[k].append((0, u))
            owed += unit_columns(u)
            u += 1
        k += 1
    total = sum(unit_columns(n) for n in range(LEAD))
    left = sum(group_columns(n) for n in range(k, NG - 1))
    done, passed = 0.0, group_columns(k)
    for u in range(LEAD):
        while done > total * passed / left and k < NG - 2:
            k += 1
            passed += group_columns(k)
        steps[k].append((1, u))
        done += unit_columns(u)
    return steps


STEPS_FIRST, STEPS = first_pass_steps(LEAD_FIRST, RATIO_FIRST), first_pass_steps(LEAD, RATIO)
STAGED = 16 * (len(Q_PARTS) + len(K_PARTS) + 1)
assert NG % RING == 0


def first_bank(u, alone):
    return u % (ALONE if alone else PAIRED)


def first_free(u):
    return u + 1 + (1 if u < NU % PAIRED else 0)


class Chain:

    def __init__(self, eng, sem):
        self.eng, self.sem, self.n = eng, sem, 0

    def then(self, ins):
        self.n += 1
        ins.then_inc(self.sem, 1)
        self.eng.wait_ge(self.sem, self.n)


class Core:

    def __init__(self, nc, ctx):
        self.nc, self.ctx = nc, ctx

    def sb(self, name, shape, dt=F32):
        return self.ctx.enter_context(self.nc.sbuf_tensor(name, shape, dt))

    def sem(self, name):
        return self.ctx.enter_context(self.nc.semaphore(name))

    def dram(self, name, shape, dt):
        return self.nc.dram_tensor(name, shape, dt, kind="Internal").ap()


def fresh(eng, value, most):
    if value is None or isinstance(value, int):
        return value
    with eng.register() as reg:
        eng.reg_mov(reg, value)
        return eng.snap(reg, min_val=0, max_val=most)


def wait_apart(eng, sem, value, ticks):
    eng.wait_ge(sem, value)
    eng.sem_inc(ticks, 1)


def stage_parts(sp, stack, which, x, parts_dram, j, buf, staged):
    columns = bass.ds(buf * HQ * S, HQ * S)
    for r, part in enumerate(which):
        sp.dma_start(stack[r * D:(r + 1) * D, columns].rearrange("d (h t) -> d h t", h=HQ),
                     parts_dram[x, part, bass.ds(j * HQ * D, HQ * D), :].rearrange("(h d) t -> d h t", h=HQ)
                     ).then_inc(staged, 16)


def clear_maxima(sp, stack, buf, staged):
    columns = bass.ds(buf * HQ * S, HQ * S)
    sp.dma_start(stack[STACK:STACK + 2, columns], stack[STACK + 2:STACK + 4, columns]).then_inc(staged, 16)


def store_and_stage_first(sp, c, parts, parts_dram, split, each, stored, staged):
    for x, (name, which) in enumerate((("qs", Q_PARTS), ("ks", K_PARTS))):
        sp.wait_ge(split, each * (x + 1))
        sp.dma_start(parts_dram[x].rearrange("a p t -> p a t"), parts[:, x]).then_inc(stored, 16)
        sp.wait_ge(stored, 16 * (x + 1))
        stage_parts(sp, c[name][:].rearrange("p a h t -> p (a h t)"), which, x, parts_dram, 0, 0, staged)
    clear_maxima(sp, c["qs"][:].rearrange("p a h t -> p (a h t)"), 0, staged)


def split_parts(dve, ch, src, parts, rest):
    ch.then(dve.tensor_copy(parts[:, 0, :], src))
    ch.then(dve.tensor_tensor(rest, src, parts[:, 0, :], ALU.subtract))
    ch.then(dve.tensor_copy(parts[:, 1, :], rest))
    ch.then(dve.tensor_tensor(rest, rest, parts[:, 1, :], ALU.subtract))
    return dve.tensor_copy(parts[:, 2, :], rest)


def layer0_front(nc, core, ps, c, others, weights, wo, wo_rows, wqkv, bias, bias_v, bout, w_fc, w_proj, fbT, v, uT, gate,
                 x, xn, cols, values, parts_dram, staged):
    ident = c["ident"]
    G = F0 // P
    st, mv = core.sb("n0_st", [P, T, 6]), core.sb("n0_mv", [P, T, 2])
    var, root, rstd = core.sb("n0_var", [P, T]), core.sb("n0_root", [P, T]), core.sb("n0_rstd", [P, T])
    sums = core.sb("f0_sums", [P, G + 1])
    scale = core.sb("f0_scale", [P, G + 1])
    half = core.sb("f0_half", [P, 2, G + 1])
    tern = core.sb("f0_tern", [P, 2, G, P])
    low = core.sb("f0_low", [P, 2, G, P])
    m1 = core.sb("f0_m1", [RANK, P])
    fcT, projT = core.sb("fcT", [P, F0]), core.sb("projT", [P, G, P])
    flat = core.sb("p0_qk", [P, 2, S])
    rest = core.sb("p0_rest", [P, S])
    parts = core.sb("p0_parts", [P, 2, 3, S], BF16)
    biask = core.sb("p0_biask", [P, 1])
    relu = core.sb("ffn0_relu", [P, 2, G, CH])
    w_landed, x_landed, landed, wo_zeroed, const_made, rows_set = (
        core.sem(f"l0_{n}") for n in ("w_landed", "x_landed", "landed", "wo_zeroed", "const_made", "rows_set"))
    chain, var_ready, root_ready, tok_ready, transposed, cols_moved = (
        core.sem(f"n0_{n}") for n in ("chain", "var", "root", "tok", "transposed", "cols"))
    tern_made, small, turned, m1_moved, lowrank, fc_made = (
        core.sem(f"f0_{n}") for n in ("made", "small", "turned", "m1_moved", "lowrank", "fc_made"))
    mm, moved, v_ready, v_moved, kb, split, stored = (
        core.sem(f"p0_{n}") for n in ("mm", "moved", "v_ready", "v_moved", "kb", "split", "stored"))
    up, relued, squared, down, added, biased = (
        core.sem(f"ffn0_{n}") for n in ("up", "relued", "squared", "down", "added", "biased"))
    w = [w_fc[:], w_proj[:].rearrange("p (g d) -> p g d", g=G)]
    rest_of = others[1:]
    WEIGHTS, OTHERS = 16 * len(weights), 16 * (len(rest_of) + len(wo_rows))

    def wide(one):
        return one.rearrange("p (g o) -> p g o", o=1).to_broadcast([P, G, P])

    with nc.Block() as block:
        @block.sync
        def _(sp):
            sp.dma_start(*others[0]).then_inc(x_landed, 16)
            for dst, src in weights[0::2]:
                sp.dma_start(dst, src).then_inc(w_landed, 16)
            for dst, src in rest_of[0::2]:
                sp.dma_start(dst, src).then_inc(landed, 16)
            sp.wait_ge(wo_zeroed, 1)
            for dst, src in wo_rows:
                sp.dma_start(dst, src).then_inc(landed, 16)
            sp.wait_ge(rows_set, 2)
            store_and_stage_first(sp, c, parts, parts_dram, split, 1, stored, staged)

        @block.scalar
        def _(act):
            for dst, src in rest_of[1::2]:
                act.dma_start(dst, src).then_inc(landed, 16)
            for dst, src in weights[1::2]:
                act.dma_start(dst, src).then_inc(w_landed, 16)
            act.wait_ge(var_ready, 1)
            act.activation(root[:], var[:], ACT.Sqrt).then_inc(root_ready, 1)
            for n in range(NC):
                act.wait_ge(transposed, n + 1)
                act.copy(cols[:, n * CH:(n + 1) * CH], ps[:, n, :]).then_inc(cols_moved, 1)
            act.wait_ge(kb, 1)
            for y in range(2):
                for n in range(NC):
                    act.wait_ge(mm, y * NC + n + 1)
                    act.activation(flat[:, y, n * CH:(n + 1) * CH], ps[:, n, :], ACT.Identity,
                                   bias=(biask[:] if y else bias[:, 0:1]),
                                   scale=(SM_SCALE if y else 1.0)).then_inc(moved, 1)
            for n in range(NC):
                if n >= 2:
                    act.wait_ge(down, n - 1)
                for g in range(G):
                    act.wait_ge(up, n * G + g + 1)
                    act.activation(relu[:, n % 2, g, :], ps[:, g, :], ACT.Relu).then_inc(relued, 1)

        @block.gpsimd
        def _(pool):
            ch = Chain(pool, const_made)
            ch.then(pool.memset(ident[:], 0.0))
            ch.then(pool.affine_select(out=ident[:], in_=ident[:], compare_op=ALU.not_equal, fill=1.0,
                                       base=0, pattern=[[-1, P]], channel_multiplier=1))
            pool.memset(wo[:], 0.0).then_inc(wo_zeroed, 1)
            ch.then(pool.memset(c["identb"][:], 0.0))
            ch.then(pool.memset(c["future"][:], 0.0))
            ch.then(pool.affine_select(out=c["identb"][:], in_=c["identb"][:], compare_op=ALU.not_equal, fill=1.0,
                                       base=0, pattern=[[-1, P]], channel_multiplier=1))
            ch.then(pool.affine_select(out=c["future"][:], in_=c["future"][:], compare_op=ALU.is_ge, fill=MASKED,
                                       base=0, pattern=[[-1, P]], channel_multiplier=1))
            for name, word in (("qs", 0.0), ("ks", PAIR_OF_ONES)):
                pool.memset(c[name][STACK:KROWS].rearrange("p a h t -> p (a h t)").bitcast(F32), word).then_inc(rows_set, 1)

        @block.vector
        def _(dve):
            ch = Chain(dve, chain)
            dve.wait_ge(x_landed, 16)
            for t in range(T):
                last = dve.bn_stats(st[:, t, :], x[:, t, :])
            ch.then(last)
            for t in range(T):
                last = dve.bn_aggr(mv[:, t, :], st[:, t, :])
            ch.then(last)
            dve.tensor_scalar(var[:], mv[:, :, 1], 1e-5, None, ALU.add).then_inc(var_ready, 1)
            dve.wait_ge(root_ready, 1)
            ch.then(dve.reciprocal(rstd[:], root[:]))
            for t in range(T):
                dve.tensor_scalar(xn[:, t, :], x[:, t, :], mv[:, t, 0:1], rstd[:, t:t + 1],
                                  ALU.subtract, ALU.mult).then_inc(tok_ready, 1)
            dve.wait_ge(landed, OTHERS)
            dve.tensor_scalar(biask[:], bias[:, 1:2], SM_SCALE, None, ALU.mult).then_inc(kb, 1)
            dve.wait_ge(small, 1)
            dve.tensor_copy(m1[:], ps[0:RANK, 7, 0:P]).then_inc(m1_moved, 1)
            dve.wait_ge(w_landed, WEIGHTS)
            dve.tensor_reduce(sums[:, 0:G], w_fc[:], AX.X, ALU.add, apply_absolute_value=True)
            ch.then(dve.tensor_reduce(sums[:, G:G + 1], w_proj[:], AX.X, ALU.add, apply_absolute_value=True))
            dve.tensor_scalar(scale[:, 0:G], sums[:, 0:G], 1.0 / P, 1e-5, ALU.mult, ALU.max)
            ch.then(dve.tensor_scalar(scale[:, G:], sums[:, G:], 1.0 / F0, 1e-5, ALU.mult, ALU.max))
            dve.tensor_scalar(half[:, 0, :], scale[:], 0.5, None, ALU.mult)
            ch.then(dve.tensor_scalar(half[:, 1, :], scale[:], -0.5, None, ALU.mult))
            dve.tensor_tensor(tern[:, 0], w[0], wide(half[:, 0, 0:G]), ALU.is_gt)
            dve.tensor_tensor(low[:, 0], w[0], wide(half[:, 1, 0:G]), ALU.is_lt)
            dve.tensor_scalar(tern[:, 1], w[1], half[:, 0, G:G + 1], None, ALU.is_gt)
            ch.then(dve.tensor_scalar(low[:, 1], w[1], half[:, 1, G:G + 1], None, ALU.is_lt))
            for y in range(2):
                last = dve.tensor_tensor(tern[:, y], tern[:, y], low[:, y], ALU.subtract)
            ch.then(last)
            for op in (ALU.subtract, ALU.add):
                for y in range(2):
                    last = dve.tensor_tensor(tern[:, y], tern[:, y], w[y], op)
                ch.then(last)
            dve.tensor_tensor(tern[:, 0], tern[:, 0], wide(scale[:, 0:G]), ALU.mult).then_inc(tern_made, 1)
            dve.tensor_scalar(tern[:, 1], tern[:, 1], scale[:, G:G + 1], None, ALU.mult).then_inc(tern_made, 1)
            for n in range(NC):
                dve.wait_ge(v_ready, n + 1)
                dve.tensor_tensor(values[:, n * TC:(n + 1) * TC, :],
                                  ps[:, 4 + n, :].rearrange("p (a b) -> p a b", a=TC),
                                  bias_v[:].rearrange("p (o b) -> p o b", o=1).to_broadcast([P, TC, P]), ALU.add
                                  ).then_inc(v_moved, 1)
            dve.wait_ge(turned, 2)
            ch.then(dve.tensor_copy(fcT[:], ps[:, 6, :]))
            dve.wait_ge(lowrank, 1)
            dve.scalar_tensor_tensor(out=fcT[:], in0=ps[:, 5, :], scalar=gate[:, 0:1], in1=fcT[:],
                                     op0=ALU.mult, op1=ALU.add).then_inc(fc_made, 1)
            dve.tensor_copy(projT[:].rearrange("p a b -> p (a b)"), ps[:, 7, :]).then_inc(fc_made, 1)
            dve.wait_ge(moved, NC)
            split_parts(dve, ch, flat[:, 0, :], parts[:, 0], rest[:]).then_inc(split, 1)
            dve.tensor_tensor(x[:], x[:], bout[:].rearrange("p (o b) -> p o b", o=1).to_broadcast([P, T, P]),
                              ALU.add).then_inc(biased, 1)
            dve.wait_ge(biased, 1)
            for n in range(NC + 1):
                if n < NC:
                    dve.wait_ge(relued, (n + 1) * G)
                    dve.tensor_tensor(relu[:, n % 2], relu[:, n % 2], relu[:, n % 2], ALU.mult).then_inc(squared, 1)
                if n == 0:
                    dve.wait_ge(moved, 2 * NC)
                    dve.wait_ge(split, 1)
                    split_parts(dve, ch, flat[:, 1, :], parts[:, 1], rest[:]).then_inc(split, 1)
                if n:
                    m = n - 1
                    sl = slice(m * TC, (m + 1) * TC)
                    dve.wait_ge(down, n)
                    dve.tensor_tensor(x[:, sl, :], ps[:, 4 + m % 2, :].rearrange("p (a b) -> p a b", a=TC),
                                      x[:, sl, :], ALU.add).then_inc(added, 1)

        @block.tensor
        def _(pe):
            pe.wait_ge(const_made, 2)
            for t in range(T):
                pe.wait_ge(tok_ready, t + 1)
                ins = pe.transpose(ps[:, t // TC, (t % TC) * P:(t % TC + 1) * P], xn[:, t, :], ident[:])
                if t % TC == TC - 1:
                    ins.then_inc(transposed, 1)
            pe.wait_ge(w_landed, WEIGHTS)
            pe.matmul(ps[0:RANK, 7, 0:P], fbT[:], v[:], start=True, stop=True).then_inc(small, 1)
            pe.wait_ge(landed, OTHERS)
            for y in range(2):
                for n in range(NC):
                    if y:
                        pe.wait_ge(moved, n + 1)
                    else:
                        pe.wait_ge(cols_moved, n + 1)
                    pe.matmul(ps[:, n, :], wqkv[:, y * P:(y + 1) * P], cols[:, n * CH:(n + 1) * CH],
                              start=True, stop=True).then_inc(mm, 1)
            pe.wait_ge(m1_moved, 1)
            for n in range(NC):
                for t in range(n * TC, (n + 1) * TC):
                    ins = pe.matmul(ps[:, 4 + n, (t % TC) * P:(t % TC + 1) * P], cols[:, t * P:(t + 1) * P],
                                    wqkv[:, 2 * P:3 * P], start=True, stop=True)
                ins.then_inc(v_ready, 1)
            pe.wait_ge(v_moved, NC)
            for y in range(2):
                pe.wait_ge(tern_made, y + 1)
                for g in range(G):
                    ins = pe.transpose(ps[:, 6 + y, g * P:(g + 1) * P], tern[:, y, g, :], ident[:])
                ins.then_inc(turned, 1)
            pe.matmul(ps[:, 5, :], m1[:], uT[:], start=True, stop=True).then_inc(lowrank, 1)
            for n in range(NC + 1):
                if n < NC:
                    for g in range(G):
                        if n:
                            pe.wait_ge(relued, (n - 1) * G + g + 1)
                        else:
                            pe.wait_ge(moved, NC + g + 1)
                            pe.wait_ge(fc_made, 1)
                        pe.matmul(ps[:, g, :], fcT[:, g * P:(g + 1) * P], cols[:, n * CH:(n + 1) * CH],
                                  start=True, stop=True).then_inc(up, 1)
                if n:
                    m = n - 1
                    pe.wait_ge(squared, n)
                    if m >= 2:
                        pe.wait_ge(added, m - 1)
                    else:
                        pe.wait_ge(fc_made, 2)
                    for i in range(TC):
                        for g in range(G):
                            ins = pe.matmul(ps[:, 4 + m % 2, i * P:(i + 1) * P], relu[:, m % 2, g, i * P:(i + 1) * P],
                                            projT[:, g, :], start=(g == 0), stop=(g == G - 1))
                    ins.then_inc(down, 1)


def attention(nc, core, ps, tag, parts_dram, values, c, ctxu, scratch, wo, base, out, staged):
    qs, ks = c["qs"], c["ks"]
    probs = core.sb(f"{tag}_probs", [P, RING, HQ, CH])
    vq = core.sb(f"{tag}_vq", [P, T, HQ, 32])
    RC = HQ * TC
    part_max = core.sb(f"{tag}_pmax", [P, NC, RC, NC])
    neg_max = core.sb(f"{tag}_nmax", [P, NC, RC])
    max_parts = core.sb(f"{tag}_mparts", [P, NC, 2, RC], BF16)
    max_rows = core.sb(f"{tag}_mrows", [2 * RC, NC, P], BF16)
    dens = core.sb(f"{tag}_dens", [P, HQ * S // P])
    rdens = core.sb(f"{tag}_rdens", [P, HQ * S // P])
    rrows = core.sb(f"{tag}_rrows", [P, S])
    nothing = core.sb(f"{tag}_nothing", [P, 8])
    qs2 = qs[:].rearrange("p a h t -> p (a h t)")
    ks2 = ks[:].rearrange("p a h t -> p (a h t)")
    ctx2 = ctxu[:].rearrange("p a t -> p (a t)")
    QB = HQ * S
    max_dram, den_dram, rden_dram = scratch

    prepared, ticks, ticks_pool = core.sem(f"{tag}_prepared"), core.sem(f"{tag}_ticks"), core.sem(f"{tag}_ticks_pool")
    chain_start = core.sem(f"{tag}_chain_start")
    v_placed = core.sem(f"{tag}_v_placed")
    a_scored = core.sem(f"{tag}_a_scored")
    a_free = core.sem(f"{tag}_a_free")
    neg_ready = core.sem(f"{tag}_neg_ready")
    chain = core.sem(f"{tag}_chain")
    rows_ready = core.sem(f"{tag}_rows_ready")
    max_stored = core.sem(f"{tag}_max_stored")
    max_loaded = [core.sem(f"{tag}_max_loaded{n}") for n in range(2)]
    b_scored = core.sem(f"{tag}_b_scored")
    exped = core.sem(f"{tag}_exped")
    masked = core.sem(f"{tag}_masked")
    pv_done = core.sem(f"{tag}_pv_done")
    ctx_moved = core.sem(f"{tag}_ctx_moved")
    den_out, den_in = core.sem(f"{tag}_den_out"), core.sem(f"{tag}_den_in")
    rden_made, rden_out = core.sem(f"{tag}_rden_made"), core.sem(f"{tag}_rden_out")
    rden_in, scaled = core.sem(f"{tag}_rden_in"), core.sem(f"{tag}_scaled")
    last_scaled, projected = core.sem(f"{tag}_last_scaled"), core.sem(f"{tag}_projected")
    B0, O0 = 3, 7

    with nc.Block() as block:
        @block.sync
        def _(sp):
            def maxima(j, buf, cq):
                sp.wait_ge(rows_ready, j * NC + cq + 1)
                sp.dma_start(max_dram[bass.ds(j, 1), cq].rearrange("o r q -> (o r) q"),
                             max_rows[:, cq, :]).then_inc(max_stored, 16)
                sp.wait_ge(max_stored, j * 16 * NC + 16 * (NC + cq + 1))
                sp.dma_start(qs[STACK:STACK + 2, bass.ds(buf, 1), :, cq * CH:(cq + 1) * CH],
                             max_dram[bass.ds(j, 1), cq].rearrange("o (a g i) q -> a o g (i q)", a=2, g=HQ)
                             ).then_inc(max_loaded[cq % 2], 16)

            def normalise(j):
                sp.wait_ge(ctx_moved, j * NC + 1)
                sp.dma_start(den_dram[bass.ds(j, 1)].rearrange("o g t -> (o g) t"),
                             ctx2[D:P:32, bass.ds(j * S, S)]).then_inc(den_out, 16)
                sp.wait_ge(den_out, j * 16 + 16)
                sp.dma_start(dens[:], den_dram[bass.ds(j, 1)].rearrange("o g (a b) -> (o g a) b", b=HQ * S // P)
                             ).then_inc(den_in, 16)
                sp.wait_ge(rden_made, j + 1)
                sp.dma_start(rden_dram[bass.ds(j, 1)].rearrange("o g (a b) -> (o g a) b", b=HQ * S // P),
                             rdens[:]).then_inc(rden_out, 16)
                sp.wait_ge(rden_out, j * 16 + 16)
                sp.wait_ge(scaled, j + 1)
                for g in range(HQ):
                    sp.dma_start(rrows[32 * g:32 * g + 32, :],
                                 rden_dram[bass.ds(j, 1), g, :].to_broadcast([32, S])).then_inc(rden_in, 16)

            def body(j, ahead):
                maxima(j, j % 2, 1)
                normalise(j)
                maxima(j, j % 2, 2)
                if ahead:
                    sp.wait_ge(pv_done, j * NG + RING)
                    stage_parts(sp, qs2, Q_PARTS, 0, parts_dram, j + 1, (j + 1) % 2, staged)
                    stage_parts(sp, ks2, K_PARTS, 1, parts_dram, j + 1, (j + 1) % 2, staged)
                    clear_maxima(sp, qs2, (j + 1) % 2, staged)
                maxima(j, j % 2, 3)
                if ahead:
                    maxima(j + 1, (j + 1) % 2, 0)

            maxima(0, 0, 0)
            sp.wait_ge(prepared, 3)
            body(0, True)
            with sp.Fori(1, NQ - 1) as j:
                body(j, True)
            body(NQ - 1, False)
            normalise(NQ)

        @block.tensor
        def _(pe):
            def first_unit(j, buf, u, alone):
                kind, cq = UNITS[u][:2]
                bank = first_bank(u, alone)
                if alone:
                    if u >= ALONE:
                        pe.wait_ge(a_free, u - ALONE + 1 + PAIRED)
                elif kind == "turn":
                    wait_apart(pe, a_free, j * NU + first_free(u), ticks)
                else:
                    pe.wait_ge(a_free, j * NU + first_free(u))
                if kind == "turn":
                    wait_apart(pe, neg_ready, j * NC + cq + 1, ticks)
                    pe.transpose(ps[0:2 * RC, bank, 0:P // 2].bitcast(BF16),
                                 max_parts[:, cq].rearrange("p a r -> p (a r)"), c["identb"][:]).then_inc(a_scored, 1)
                    return
                _, _, g, i, kc = UNITS[u]
                diagonal = kc == cq
                w = P * (i + 1) if diagonal else CH
                ins = pe.matmul(ps[:, bank, 0:w], qs2[0:KROWS, bass.ds(buf * QB + g * S + cq * CH + i * P, P)],
                                ks2[0:KROWS, bass.ds(buf * QB + g * S + kc * CH, w)], start=True, stop=not diagonal)
                if diagonal:
                    ins = pe.matmul(ps[:, bank, w - P:w], c["identb"][:], c["future"][:], start=False, stop=True)
                ins.then_inc(a_scored, 1)

            def scores(j, buf, k, heads):
                cq, t = GROUPS[k]
                skip = max(0, t - TC * cq) * P
                for g in heads:
                    pe.wait_ge(exped, j * HQ * NG + HQ * k + g + 1)
                    pe.matmul(ps[:, B0 + g, skip:CH], ks2[0:KROWS, bass.ds(buf * QB + g * S + t * P, P)],
                              qs2[0:KROWS, bass.ds(buf * QB + g * S + cq * CH + skip, CH - skip)],
                              start=True, stop=True).then_inc(b_scored, 1)

            def product(j, k):
                cq, t = GROUPS[k]
                skip = max(0, t - TC * cq) * P
                pe.wait_ge(exped, j * HQ * NG + HQ * k + 2 * HQ)
                if k in DIAG:
                    pe.wait_ge(masked, j * len(DIAG) + DIAG.index(k) + 1)
                if t == 0:
                    pe.wait_ge(ctx_moved, j * NC + cq + 1)
                for g in range(HQ):
                    ins = pe.matmul(ps[32 * g:32 * g + 32, O0, skip:CH], vq[:, t, g, :],
                                    probs[:, k % RING, g, skip:CH], start=(t == 0), stop=(k == LAST[cq]),
                                    skip_group_check=True)
                ins.then_inc(pv_done, 1)

            def first_pass_alone():
                pe.wait_ge(staged, STAGED)
                for u in range(LEAD_FIRST):
                    first_unit(0, 0, u, True)
                pe.wait_ge(a_free, LEAD_FIRST + PAIRED)

            def both_passes(j, bufb, bufa, ahead, steps):
                entered = False
                for k in range(NG):
                    bufb, bufa = fresh(pe, bufb, 1), fresh(pe, bufa, 1)
                    share = [(n, u) for n, u in steps[k] if ahead or not n]

                    def some(n):
                        for on, u in share[:n]:
                            first_unit(j + on, bufa if on else bufb, u, False)
                        del share[:n]

                    if share and share[0][0] and not entered:
                        pe.wait_ge(staged, (j + 2) * STAGED)
                        entered = True
                    cq, t = GROUPS[k]
                    if t == 0:
                        pe.wait_ge(max_loaded[cq % 2], j * 8 * NC + 16 * (cq // 2 + 1))
                    for heads in ((0,), (1,), (2,), (3,)):
                        some(1)
                        scores(j, bufb, k, heads)
                    some(1)
                    if k == LAG:
                        pe.wait_ge(v_placed, j + 1)
                    if k >= LAG:
                        product(j, k - LAG)
                    some(len(share))
                for k in range(NG - LAG, NG):
                    product(j, k)

            def project(q, n):
                for i in range(TC):
                    t = n * TC + i
                    ins = pe.matmul(ps[:, n, i * P:(i + 1) * P], ctxu[:, 1 + q, t * P:(t + 1) * P], wo[:, q, :],
                                    start=(q == 0 and i == 0), stop=(q == NQ - 1), skip_group_check=True)
                return ins

            first_pass_alone()
            both_passes(0, 0, 1, True, STEPS_FIRST)
            with pe.Fori(1, NQ - 1) as j:
                both_passes(j, j % 2, (j + 1) % 2, True, STEPS)
            both_passes(NQ - 1, (NQ - 1) % 2, None, False, STEPS)
            pe.wait_ge(a_free, NQ * NU + PAIRED)
            pe.wait_ge(exped, NQ * NG * HQ + HQ)
            pe.wait_ge(scaled, NQ + 1)
            for q in range(NQ - 1):
                for n in range(NC):
                    project(q, n)
            for n in range(NC):
                pe.wait_ge(last_scaled, n + 1)
                project(NQ - 1, n).then_inc(projected, 1)

        @block.scalar
        def _(act):
            def body(j):
                for k, (cq, t) in enumerate(GROUPS):
                    skip = max(0, t - TC * cq) * P
                    act.wait_ge(pv_done, j * NG + k + 1)
                    for g in range(HQ):
                        act.wait_ge(b_scored, j * HQ * NG + HQ * k + g + 1)
                        act.activation(probs[:, k % RING, g, skip:CH], ps[:, B0 + g, skip:CH],
                                       ACT.Exp).then_inc(exped, 1)

            with act.Fori(0, NQ) as j:
                body(j)

        @block.gpsimd
        def _(pool):
            def mask(j, n):
                k = DIAG[n]
                cq, t = GROUPS[k]
                skip = (t - TC * cq) * P
                tri = probs[:, k % RING, :, skip:skip + P]
                wait_apart(pool, exped, j * HQ * NG + HQ * k + 2 * HQ, ticks_pool)
                pool.affine_select(out=tri, in_=tri, compare_op=ALU.is_ge, fill=0.0, base=0,
                                   pattern=[[0, HQ], [1, P]], channel_multiplier=-1).then_inc(masked, 1)

            def scale(j):
                pool.wait_ge(rden_in, j * 64 + 64)
                ctx = ctx2[:, bass.ds(j * S, S)]
                pool.tensor_tensor(ctx, ctx, rrows[:], ALU.mult).then_inc(scaled, 1)

            pool.memset(vq[:], 0.0).then_inc(prepared, 1)
            pool.wait_ge(prepared, 1)
            pool.memset(vq[:, :, :, D:D + 1], 1.0).then_inc(prepared, 1)
            pool.memset(ctxu[:, 0, :], 1.0).then_inc(prepared, 1)
            pool.wait_ge(prepared, 3)
            pool.memset(nothing[:, 0:1], 0.0).then_inc(scaled, 1)
            with pool.Fori(0, NQ) as j:
                for n in range(len(DIAG)):
                    mask(j, n)
                    if n == 3 * TC - 1:
                        scale(j)

        @block.vector
        def _(dve):
            def place_values(j):
                dve.tensor_copy(vq[:, :, :, 0:D],
                                values[:].rearrange("p t (q d) -> p q t d", d=HQ * D)[:, bass.ds(j, 1)]
                                .rearrange("p o t (h d) -> p (o t) h d", h=HQ)).then_inc(v_placed, 1)

            def first_unit(j, alone, u):
                kind, cq = UNITS[u][:2]
                bank = first_bank(u, alone)
                dve.wait_ge(a_scored, j * NU + u + 1)
                if kind == "turn":
                    dve.wait_ge(max_stored, j * 16 * NC + 16 * (cq + 1))
                    dve.tensor_copy(max_rows[:, cq, :], ps[0:2 * RC, bank, 0:P // 2].bitcast(BF16)
                                    ).then_inc(rows_ready, 1)
                    dve.wait_ge(rows_ready, j * NC + cq + 1)
                    dve.memset(nothing[:, 1:2], 0.0).then_inc(a_free, 1)
                    return
                _, _, g, i, kc = UNITS[u]
                w = P * (i + 1) if kc == cq else CH
                dve.tensor_reduce(part_max[:, cq, g * TC + i, kc:kc + 1], ps[:, bank, 0:w], AX.X,
                                  ALU.max).then_inc(a_free, 1)
                if (g, i, kc) == (HQ - 1, TC - 1, cq):
                    dve.wait_ge(a_free, j * NU + u + 1 + PAIRED)
                    dve.tensor_reduce(neg_max[:, cq, :], part_max[:, cq], AX.X, ALU.max, negate=True
                                      ).then_inc(chain, 1)
                    dve.wait_ge(chain, j * 2 * NC + 2 * cq + 1)
                    dve.tensor_copy(max_parts[:, cq, 0, :], neg_max[:, cq, :]).then_inc(chain, 1)
                    dve.wait_ge(chain, j * 2 * NC + 2 * cq + 2)
                    dve.tensor_tensor(max_parts[:, cq, 1, :], neg_max[:, cq, :], max_parts[:, cq, 0, :],
                                      ALU.subtract).then_inc(neg_ready, 1)

            def move_context(j, cq):
                dve.wait_ge(pv_done, j * NG + LAST[cq] + 1 + RING)
                dve.tensor_copy(ctx2[:, bass.ds(j * S + S + cq * CH, CH)], ps[:, O0, :]
                                ).then_inc(ctx_moved, 1)

            def reciprocals(j):
                dve.wait_ge(den_in, j * 16 + 16)
                dve.reciprocal(rdens[:], dens[:]).then_inc(rden_made, 1)

            def body(j, ahead, steps):
                for k in range(NG):
                    for cq in range(NC - 1):
                        if k == LAST[cq] + LAG + 1:
                            move_context(j, cq)
                    if k == 7:
                        reciprocals(j)
                    for n, u in steps[k]:
                        if ahead or not n:
                            first_unit(j + n, False, u)
                move_context(j, NC - 1)

            dve.memset(part_max[:], FLOOR).then_inc(chain_start, 1)
            dve.wait_ge(chain_start, 1)
            dve.memset(nothing[:, 2:3], 0.0).then_inc(a_free, PAIRED)
            dve.memset(nothing[:, 3:4], 0.0).then_inc(exped, HQ)
            dve.memset(nothing[:, 4:5], 0.0).then_inc(pv_done, RING)
            dve.memset(nothing[:, 5:6], 0.0).then_inc(ctx_moved, 1)
            dve.memset(nothing[:, 6:7], 0.0).then_inc(max_stored, 16 * NC)
            for u in range(LEAD_FIRST):
                first_unit(0, True, u)
            dve.wait_ge(prepared, 2)
            place_values(0)
            body(0, True, STEPS_FIRST)
            place_values(1)
            with dve.Fori(1, NQ - 1) as j:
                body(j, True, STEPS)
                place_values(j + 1)
            body(NQ - 1, False, STEPS)
            reciprocals(NQ)
            dve.wait_ge(rden_in, (NQ + 1) * 64)
            for n in range(NC):
                x = slice(n * CH, (n + 1) * CH)
                dve.tensor_tensor(ctxu[:, NQ, x], ctxu[:, NQ, x], rrows[:, x], ALU.mult).then_inc(last_scaled, 1)
            for n in range(NC):
                sl = slice(n * TC, (n + 1) * TC)
                dve.wait_ge(projected, n + 1)
                dve.tensor_tensor(out[:, sl, :], ps[:, n, :].rearrange("p (a b) -> p a b", a=TC), base[:, sl, :],
                                  ALU.add).then_inc(chain, 1)


def layer1_front(nc, core, ps, c, sooner, later, second_tables, wo_heads, wo_rows, wl, wf, tables, by_token, g1, blocks, heads,
                 x, xn, hid, cols, values, parts_dram, staged):
    ident = c["ident"]
    st, mv = core.sb("n1_st", [P, T, 6]), core.sb("n1_mv", [P, 2, T, 2])
    var, root, rstd = core.sb("n1_var", [P, 2, T]), core.sb("n1_root", [P, 2, T]), core.sb("n1_rstd", [P, 2, T])
    q_lin = core.sb("q_lin", [P, S])
    k_lin = core.sb("k_lin", [P, T, P])
    v_lin = core.sb("v_lin", [P, T, P + 1])
    TURNS, RESTS = 3, 4
    flat, turn = core.sb("flat", [P, TURNS, CH]), core.sb("turn", [P, TURNS, CH])
    rest = core.sb("rest", [P, RESTS, CH])
    parts = core.sb("parts1", [P, 2, 3, S], BF16)
    ksum, kv = core.sb("ksum", [P, 1]), core.sb("kv", [P, P + H])
    den = core.sb("den", [P, T, H])
    names = ("sooner", "later", "tables", "wo_zeroed", "ones", "chain", "var", "root", "tok", "transposed", "moved",
             "projected", "rotated", "added", "relued", "kv_projected", "v_lin_moved", "v_projected", "v_moved",
             "part0", "part1", "part2", "rested", "rested2", "stored",
             "summed", "kv_made", "applied", "normed", "turned", "ctx_moved", "out_projected", "out_added")
    (sooner_in, later_in, tables_in, wo_zeroed, ones_made, chain, var_ready, root_ready, tok_ready, transposed, moved,
     projected, rotated, added, relued, kv_projected, v_lin_moved, v_projected, v_moved,
     part0, part1, part2, rested, rested2, stored,
     summed, kv_made, applied, normed, turned, ctx_moved, out_projected, out_added) = (core.sem(f"f1_{n}") for n in names)
    SOONER, LATER, TABLES = 16 * len(sooner), 16 * (len(later) + len(wo_rows)), 16 * len(second_tables)
    NU2 = 2 * NC
    halves = ps[:].rearrange("p b (a w) -> p (b a) w", a=2)

    def chunk(n):
        return slice(n * CH, (n + 1) * CH)

    def tiles(n):
        return slice(n * TC, (n + 1) * TC)

    def pair(u):
        return 4 + 2 * (u % 2)

    def quad(n):
        return 4 * (n % 2)

    with nc.Block() as block:
        @block.sync
        def _(sp):
            for dst, src in sooner:
                sp.dma_start(dst, src).then_inc(sooner_in, 16)
            for dst, src in later:
                sp.dma_start(dst, src).then_inc(later_in, 16)
            sp.wait_ge(wo_zeroed, 1)
            for dst, src in wo_rows:
                sp.dma_start(dst, src).then_inc(later_in, 16)
            sp.wait_ge(rotated, 2 * NC)
            for dst, src in second_tables:
                sp.dma_start(dst, src).then_inc(tables_in, 16)
            store_and_stage_first(sp, c, parts, parts_dram, part2, NC, stored, staged)
            sp.wait_ge(later_in, LATER)
            sp.wait_ge(tables_in, TABLES)

        @block.tensor
        def _(pe):
            def transposes(y, tok, first_bank):
                for t in range(T):
                    pe.wait_ge(tok_ready, y * T + t + 1)
                    ins = pe.transpose(ps[:, first_bank + t // TC, (t % TC) * P:(t % TC + 1) * P], tok[:, t, :], ident[:])
                    if t % TC == TC - 1:
                        ins.then_inc(transposed, 1)

            def project(u, w, wt, x):
                for y, ww in enumerate((w, wt)):
                    ins = pe.matmul(ps[:, pair(u) + y, :], ww, cols[:, x], start=True, stop=True)
                ins.then_inc(projected, 1)

            transposes(0, xn, 0)
            pe.wait_ge(sooner_in, SOONER)
            for n in range(NC):
                pe.wait_ge(moved, n + 1)
                if n >= 2:
                    pe.wait_ge(rotated, 2 * (n - 1))
                project(n, wl[:, 0, :], wl[:, 1, :], chunk(n))
            for n in range(NC):
                if n == 1:
                    pe.wait_ge(rotated, 2 * NC)
                if n >= 2:
                    pe.wait_ge(rotated, 2 * (NC + n - 1))
                    pe.wait_ge(v_lin_moved, n - 1)
                for i in range(TC):
                    t = n * TC + i
                    ins = pe.matmul(ps[:, quad(n) + i, 0:3 * P], cols[:, t * P:(t + 1) * P],
                                    wl[:, 2:5, :].rearrange("p a b -> p (a b)"), start=True, stop=True)
                ins.then_inc(kv_projected, 1)
            pe.wait_ge(rotated, 2 * (2 * NC - 1))
            pe.wait_ge(v_lin_moved, NC - 1)
            transposes(1, hid, 0)
            pe.wait_ge(later_in, LATER)
            pe.wait_ge(v_lin_moved, NC)
            for u in range(NU2):
                if u < NC:
                    pe.wait_ge(moved, NC + u + 1)
                pe.wait_ge(rotated, 2 * (2 * NC + max(0, u - 1)))
                y = 2 * (u // NC)
                project(u, wf[:, y, :], wf[:, y + 1, :], chunk(u % NC))
            for n in range(NC):
                for t in range(n * TC, (n + 1) * TC):
                    ins = pe.matmul(ps[:, n, (t % TC) * P:(t % TC + 1) * P], cols[:, t * P:(t + 1) * P], wf[:, 4, :],
                                    start=True, stop=True)
                ins.then_inc(v_projected, 1)

            pe.wait_ge(relued, 2 * NC)
            pe.wait_ge(ones_made, 1)
            pe.wait_ge(rotated, 2 * (2 * NC + NU2))
            for t in range(T):
                ins = pe.matmul(ps[:, 4, 0:P + 1], k_lin[:, t, :], v_lin[:, t, :], start=(t == 0), stop=(t == T - 1))
            ins.then_inc(summed, 1)
            pe.wait_ge(v_moved, NC)
            pe.wait_ge(kv_made, 1)
            for t in range(T):
                ins = pe.matmul(halves[:, t, 0:P + H], q_lin[:, t * P:(t + 1) * P], kv[:], start=True, stop=True)
                if t % TC == TC - 1:
                    ins.then_inc(applied, 1)
            for n in range(NC + 1):
                if n < NC:
                    pe.wait_ge(normed, n + 1)
                    for i in range(TC):
                        ins = pe.transpose(ps[:, 2 * n, i * P:(i + 1) * P], k_lin[:, n * TC + i, :], ident[:])
                    ins.then_inc(turned, 1)
                if n:
                    pe.wait_ge(ctx_moved, n)
                    for i in range(TC):
                        t = (n - 1) * TC + i
                        ins = pe.matmul(ps[:, 2 * n - 1, i * P:(i + 1) * P], cols[:, t * P:(t + 1) * P], wl[:, 5, :],
                                        start=True, stop=True)
                    ins.then_inc(out_projected, 1)

        @block.scalar
        def _(act):
            def columns(y):
                for n in range(NC):
                    act.wait_ge(transposed, y * NC + n + 1)
                    act.copy(cols[:, chunk(n)], ps[:, n, :]).then_inc(moved, 1)

            act.wait_ge(var_ready, 1)
            act.activation(root[:, 0], var[:, 0], ACT.Sqrt).then_inc(root_ready, 1)
            columns(0)
            act.wait_ge(var_ready, 2)
            act.activation(root[:, 1], var[:, 1], ACT.Sqrt).then_inc(root_ready, 1)
            for n in range(NC):
                act.wait_ge(added, n + 1)
                act.activation(q_lin[:, chunk(n)], q_lin[:, chunk(n)], ACT.Relu).then_inc(relued, 1)
            for first in (0, 2):
                for n in (first, first + 1):
                    act.wait_ge(kv_projected, n + 1)
                    act.copy(v_lin[:, tiles(n), 0:P], ps[:, quad(n):quad(n) + TC, 2 * P:3 * P]).then_inc(v_lin_moved, 1)
                for n in (first, first + 1):
                    act.wait_ge(added, NC + n + 1)
                    act.activation(k_lin[:, tiles(n), :], k_lin[:, tiles(n), :], ACT.Relu).then_inc(relued, 1)
            columns(1)
            for u in range(NU2 + 2):
                if u < NU2:
                    act.wait_ge(added, 2 * NC + u + 1)
                    act.copy(parts[:, u // NC, 0, chunk(u % NC)], flat[:, u % TURNS, :]).then_inc(part0, 1)
                if 1 <= u <= NU2:
                    act.wait_ge(rested, u)
                    act.copy(parts[:, (u - 1) // NC, 1, chunk((u - 1) % NC)], rest[:, (u - 1) % RESTS, :]).then_inc(part1, 1)
                if u >= 2:
                    act.wait_ge(rested2, u - 1)
                    act.copy(parts[:, (u - 2) // NC, 2, chunk((u - 2) % NC)], rest[:, (u - 2) % RESTS, :]).then_inc(part2, 1)
            for n in range(NC):
                act.wait_ge(v_projected, n + 1)
                act.copy(values[:, tiles(n), :], ps[:, n, :].rearrange("p (a b) -> p a b", a=TC)).then_inc(v_moved, 1)
            for n in range(NC):
                act.wait_ge(turned, n + 1)
                act.copy(cols[:, chunk(n)], ps[:, 2 * n, :]).then_inc(ctx_moved, 1)

        @block.gpsimd
        def _(pool):
            pool.memset(wo_heads[:], 0.0).then_inc(wo_zeroed, 1)
            pool.memset(v_lin[:, :, P:P + 1], 1.0).then_inc(ones_made, 1)

            def add_turned(m, out):
                pool.wait_ge(rotated, 2 * (m + 1))
                pool.tensor_tensor(out, out, turn[:, m % TURNS, :], ALU.add).then_inc(added, 1)

            for n in range(NC):
                add_turned(n, q_lin[:, chunk(n)])
            for n in range(NC):
                add_turned(NC + n, k_lin[:, tiles(n), :].rearrange("p a b -> p (a b)"))
            for u in range(NU2 + 2):
                if u < NU2:
                    add_turned(2 * NC + u, flat[:, u % TURNS, :])
                if u >= 2:
                    v = u - 2
                    pool.wait_ge(part1, v + 1)
                    pool.tensor_tensor(rest[:, v % RESTS, :], rest[:, v % RESTS, :], parts[:, v // NC, 1, chunk(v % NC)],
                                       ALU.subtract).then_inc(rested2, 1)

        @block.vector
        def _(dve):
            ch = Chain(dve, chain)

            def statistics(y, src):
                for t in range(T):
                    last = dve.bn_stats(st[:, t, :], src[:, t, :])
                ch.then(last)
                for t in range(T):
                    last = dve.bn_aggr(mv[:, y, t, :], st[:, t, :])
                ch.then(last)

            def rotate(m, out, plain, turned_form, cos, sin, scale):
                if m >= TURNS:
                    dve.wait_ge(added, m - TURNS + 1)
                t = turn[:, m % TURNS, :]
                if len(out.shape) == 4:
                    t = t.rearrange("p (a h d) -> p a h d", a=TC, h=H)
                for dst, src, table in ((out, plain, cos), (t, turned_form, sin)):
                    if scale is None:
                        dve.tensor_tensor(dst, src, table, ALU.mult).then_inc(rotated, 1)
                    else:
                        dve.scalar_tensor_tensor(out=dst, in0=src, scalar=scale, in1=table, op0=ALU.mult, op1=ALU.mult
                                                 ).then_inc(rotated, 1)

            def rotate_k(n):
                dve.wait_ge(v_lin_moved, n + 1)
                four = slice(quad(n), quad(n) + TC)
                plain, turned_form = (ps[:, four, y * P:(y + 1) * P].rearrange("p a (h d) -> p a h d", h=H) for y in range(2))
                cos, sin = (by_token[:, y, tiles(n)].rearrange("p a (o d) -> p a o d", o=1).to_broadcast([P, TC, H, D])
                            for y in range(2))
                rotate(NC + n, k_lin[:, tiles(n), :].rearrange("p a (h d) -> p a h d", h=H), plain, turned_form, cos, sin, None)

            statistics(0, x)
            dve.tensor_scalar(var[:, 0], mv[:, 0, :, 1], 1e-5, None, ALU.add).then_inc(var_ready, 1)
            dve.wait_ge(root_ready, 1)
            ch.then(dve.reciprocal(rstd[:, 0], root[:, 0]))
            for t in range(T):
                dve.tensor_scalar(xn[:, t, :], x[:, t, :], mv[:, 0, t, 0:1], rstd[:, 0, t:t + 1],
                                  ALU.subtract, ALU.mult).then_inc(tok_ready, 1)
            dve.wait_ge(tok_ready, T)
            statistics(1, xn)
            ch.then(dve.tensor_tensor(var[:, 1], mv[:, 1, :, 0], mv[:, 1, :, 0], ALU.mult))
            dve.scalar_tensor_tensor(out=var[:, 1], in0=mv[:, 1, :, 1], scalar=1e-6, in1=var[:, 1],
                                     op0=ALU.add, op1=ALU.add).then_inc(var_ready, 1)
            dve.wait_ge(sooner_in, SOONER)
            for n in range(NC):
                dve.wait_ge(projected, n + 1)
                rotate(n, q_lin[:, chunk(n)], ps[:, pair(n), :], ps[:, pair(n) + 1, :],
                       tables[:, 0, chunk(n)], tables[:, 1, chunk(n)], None)
            for n in (0, 1):
                rotate_k(n)
            dve.wait_ge(root_ready, 2)
            ch.then(dve.reciprocal(rstd[:, 1], root[:, 1]))
            for t in range(T):
                dve.scalar_tensor_tensor(out=hid[:, t, :], in0=xn[:, t, :], scalar=rstd[:, 1, t:t + 1],
                                         in1=g1[:], op0=ALU.mult, op1=ALU.mult).then_inc(tok_ready, 1)
            for n in (2, 3):
                rotate_k(n)
            dve.wait_ge(tables_in, TABLES)
            for u in range(NU2 + 1):
                if u < NU2:
                    dve.wait_ge(projected, NC + u + 1)
                    if u >= TURNS:
                        dve.wait_ge(rested, u - TURNS + 1)
                    rotate(2 * NC + u, flat[:, u % TURNS, :], ps[:, pair(u), :], ps[:, pair(u) + 1, :],
                           tables[:, 0, chunk(u % NC)], tables[:, 1, chunk(u % NC)], SM_SCALE if u >= NC else None)
                if u:
                    v = u - 1
                    dve.wait_ge(part0, v + 1)
                    if v >= RESTS:
                        dve.wait_ge(part2, v - RESTS + 1)
                    dve.tensor_tensor(rest[:, v % RESTS, :], flat[:, v % TURNS, :], parts[:, v // NC, 0, chunk(v % NC)],
                                      ALU.subtract).then_inc(rested, 1)
            dve.wait_ge(summed, 1)
            dve.wait_ge(later_in, LATER)
            ch.then(dve.tensor_copy(ksum[:], ps[:, 4, P:P + 1]))
            ch.then(dve.tensor_tensor(kv[:, 0:P], ps[:, 4, 0:P], blocks[:], ALU.mult))
            dve.tensor_scalar(kv[:, P:], heads[:], ksum[:, 0:1], None, ALU.mult).then_inc(kv_made, 1)
            for n in range(NC):
                dve.wait_ge(applied, n + 1)
                ch.then(dve.tensor_scalar(den[:, tiles(n)], halves[:, tiles(n), P:P + H], 1e-6, None, ALU.add))
                ch.then(dve.reciprocal(den[:, tiles(n)], den[:, tiles(n)]))
                dve.tensor_tensor(k_lin[:, tiles(n), :].rearrange("p a (h d) -> p a h d", h=H),
                                  halves[:, tiles(n), 0:P].rearrange("p a (h d) -> p a h d", h=H),
                                  den[:, tiles(n)].rearrange("p a (h o) -> p a h o", o=1).to_broadcast([P, TC, H, D]),
                                  ALU.mult).then_inc(normed, 1)
            for n in range(NC):
                dve.wait_ge(out_projected, n + 1)
                dve.tensor_tensor(x[:, tiles(n), :], ps[:, 2 * n + 1, :].rearrange("p (a b) -> p a b", a=TC),
                                  x[:, tiles(n), :], ALU.add).then_inc(out_added, 1)


def experts(nc, core, ps, ident, small, hid, normed, cols, w_router, g2, order, wg, wu, wd, rows_dram, acc, out):
    W = 2 * HID + HC * P
    UE = NC * HC
    G = 3
    raw = core.sb("moe_raw", [P, 2, W])
    w_high, w_low = core.sb("moe_w_high", [P, 2, W], F32R), core.sb("moe_w_low", [P, 2, W], F32R)
    c_high, c_low = core.sb("moe_c_high", [P, S], F32R), core.sb("moe_c_low", [P, S], F32R)
    spread = core.sb("moe_spread", [P, 2, S])
    silu, hidden = core.sb("moe_silu", [P, G, CH]), core.sb("moe_hidden", [P, G, CH])
    h_high, h_low = core.sb("moe_h_high", [P, 2, HC, CH], F32R), core.sb("moe_h_low", [P, 2, HC, CH], F32R)
    weighted = core.sb("moe_weighted", [P, 2, CH])
    total = core.sb("moe_total", [P, S])
    st, mv = core.sb("n3_st", [P, T, 6]), core.sb("n3_mv", [P, T, 2])
    var, root, rstd = core.sb("n3_var", [P, T]), core.sb("n3_root", [P, T]), core.sb("n3_rstd", [P, T])
    shape = [P, T, E]
    logits, left, pick, picked, second, ex, combine = (core.sb(f"rt_{n}", shape) for n in (
        "logits", "left", "pick", "picked", "second", "ex", "combine"))
    best, best2, rank, tot = (core.sb(f"rt_{n}", [P, T]) for n in ("best", "best2", "rank", "tot"))
    small_in, chain, var_ready, root_ready, tok_ready, transposed, moved, high_moved, c_low_made = (
        core.sem(f"n3_{n}") for n in ("small", "chain", "var", "root", "tok", "transposed", "moved", "high", "low"))
    scored, shifted, exped, combined, hid_added = (
        core.sem(f"rt_{n}") for n in ("scored", "shifted", "exped", "combined", "hid_added"))
    rows = core.sb("moe_rows", [E, S])
    nothing = core.sb("moe_nothing", [P, 8])
    names = ("turned", "rows_made", "rows_stored", "split", "gated", "silued", "mixed", "high_made", "low_made",
             "down", "weigh", "added", "back", "stored", "c_split", "final")
    (turned, rows_made, rows_stored, split, gated, silued, mixed, high_made, low_made,
     down, weigh, added, back, stored, c_split, final) = (core.sem(f"moe_{n}") for n in names)
    placed = [core.sem(f"moe_placed{b}") for b in range(2)]
    spread_in = [core.sem(f"moe_spread_in{b}") for b in range(2)]
    D0 = 6
    SMALL = 16 * len(small)

    def wide(x):
        return x[:].rearrange("p (t o) -> p t o", o=1).to_broadcast(shape)

    def three(pe, bank, high, low, x_high, x_low, first, last):
        pe.matmul(bank, high, x_high, start=first, stop=False)
        pe.matmul(bank, high, x_low, start=False, stop=False)
        return pe.matmul(bank, low, x_high, start=False, stop=last)

    with nc.Block() as block:
        @block.sync
        def _(sp):
            def expert(n, b):
                one = bass.ds(n, 1)
                sp.dma_start(raw[:, b, 0:HID], wg[one].rearrange("o d h -> (o d) h")).then_inc(placed[b], 16)
                sp.dma_start(raw[:, b, HID:2 * HID], wu[one].rearrange("o d h -> (o d) h")).then_inc(placed[b], 16)
                sp.dma_start(raw[:, b, 2 * HID:].rearrange("p (c d) -> p c d", c=HC),
                             wd[one].rearrange("o (c p) d -> p (o c) d", p=P)).then_inc(placed[b], 16)
                return one

            def spread_row(one, b):
                sp.dma_start(spread[:, b, :], rows_dram[one].to_broadcast([P, S])).then_inc(spread_in[b], 16)

            for dst, src in small:
                sp.dma_start(dst, src).then_inc(small_in, 16)
            one = expert(0, 0)
            for n in range(NC):
                sp.wait_ge(rows_made, n + 1)
            sp.dma_start(rows_dram, rows[:]).then_inc(rows_stored, 16)
            sp.wait_ge(rows_stored, 16)
            spread_row(one, 0)
            with sp.Fori(0, E // 2) as pair:
                e = pair * 2
                for half in range(2):
                    sp.wait_ge(split, e + half + 1)
                    one = expert((e + half + 1) % E, 1 - half)
                    sp.wait_ge(added, e * NC + half * NC + 2)
                    spread_row(one, 1 - half)
            for n in range(NC):
                sp.wait_ge(final, n + 1)
                sp.dma_start(out[n * CH:(n + 1) * CH, :].rearrange("(t p) d -> p t d", p=P),
                             acc[:, n * TC:(n + 1) * TC, :]).then_inc(stored, 16)
            sp.wait_ge(stored, 16 * NC)
            sp.wait_ge(spread_in[0], 16 * (E // 2 + 1))

        @block.tensor
        def _(pe):
            for t in range(T):
                pe.wait_ge(tok_ready, t + 1)
                ins = pe.transpose(ps[:, t // TC, (t % TC) * P:(t % TC + 1) * P], normed[:, t, :], ident[:])
                if t % TC == TC - 1:
                    ins.then_inc(transposed, 1)
            pe.wait_ge(small_in, SMALL)
            for t in range(T):
                pe.wait_ge(moved, t // TC + 1)
                ins = pe.matmul(ps[:, 4, t * E:(t + 1) * E], cols[:, t * P:(t + 1) * P], w_router[:], start=True, stop=True)
            ins.then_inc(scored, 1)
            pe.wait_ge(high_moved, NC)
            pe.wait_ge(combined, 1)
            for t in range(T):
                ins = pe.transpose(ps[0:E, t // TC, (t % TC) * P:(t % TC + 1) * P], combine[:, t, :], ident[:])
                if t % TC == TC - 1:
                    ins.then_inc(turned, 1)
            pe.wait_ge(rows_made, NC)
            pe.wait_ge(c_low_made, NC)

            def down_product(e, d):
                half, n = d // NC, d % NC
                pe.wait_ge(low_made, e * UE + HC * (d + 1) + G)
                pe.wait_ge(added, e * NC + d + 1)
                for h in range(HC):
                    w = slice(2 * HID + h * P, 2 * HID + (h + 1) * P)
                    ins = three(pe, ps[:, D0 + n % 2, :], w_high[:, half, w], w_low[:, half, w],
                                h_high[:, n % 2, h, :], h_low[:, n % 2, h, :], h == 0, h == HC - 1)
                ins.then_inc(down, 1)

            with pe.Fori(0, E // 2) as pair:
                e = pair * 2
                for half in range(2):
                    pe.wait_ge(split, e + half + 1)
                    for n in range(NC):
                        x = slice(n * CH, (n + 1) * CH)
                        for h in range(HC):
                            u = half * UE + n * HC + h
                            pe.wait_ge(mixed, e * UE + u + 1)
                            for y in range(2):
                                w = slice(y * HID + h * P, y * HID + (h + 1) * P)
                                ins = three(pe, ps[:, 2 * (u % G) + y, :], w_high[:, half, w], w_low[:, half, w],
                                            c_high[:, x], c_low[:, x], True, True)
                            ins.then_inc(gated, 1)
                        if half * NC + n:
                            down_product(e, half * NC + n - 1)
                down_product(e, 2 * NC - 1)
            pe.wait_ge(added, E * NC + 2)
            for t in range(T):
                ins = pe.transpose(ps[:, t // TC, (t % TC) * P:(t % TC + 1) * P], total[:, t * P:(t + 1) * P], ident[:])
                if t % TC == TC - 1:
                    ins.then_inc(back, 1)

        @block.scalar
        def _(act):
            act.wait_ge(var_ready, 1)
            act.activation(root[:], var[:], ACT.Sqrt).then_inc(root_ready, 1)
            for n in range(NC):
                x = slice(n * CH, (n + 1) * CH)
                act.wait_ge(transposed, n + 1)
                act.copy(cols[:, x], ps[:, n, :]).then_inc(moved, 1)
                act.copy(c_high[:, x], ps[:, n, :]).then_inc(high_moved, 1)
            act.wait_ge(shifted, 1)
            act.activation(ex[:], ex[:], ACT.Exp).then_inc(exped, 1)
            for n in range(NC):
                act.wait_ge(turned, n + 1)
                act.copy(rows[:, n * CH:(n + 1) * CH], ps[0:E, n, :]).then_inc(rows_made, 1)

            def high(e, u):
                d = u // HC
                act.wait_ge(mixed, e * UE + u + 1 + G)
                if u % HC == 0:
                    act.wait_ge(down, e * NC + d - 1 + 2 * NC)
                act.copy(h_high[:, d % 2, u % HC, :], hidden[:, u % G, :]).then_inc(high_made, 1)

            with act.Fori(0, E // 2) as pair:
                e = pair * 2
                for u in range(2 * UE):
                    act.wait_ge(gated, e * UE + u + 1)
                    act.wait_ge(mixed, e * UE + u + 1)
                    act.activation(silu[:, u % G, :], ps[:, 2 * (u % G), :], ACT.Silu).then_inc(silued, 1)
                    if u:
                        high(e, u - 1)
                high(e, 2 * UE - 1)

        @block.gpsimd
        def _(pool):
            for n in range(NC):
                x = slice(n * CH, (n + 1) * CH)
                pool.wait_ge(high_moved, n + 1)
                pool.tensor_tensor(c_low[:, x], cols[:, x], c_high[:, x].bitcast(F32), ALU.subtract).then_inc(c_low_made, 1)
            pool.tensor_tensor(acc[:], acc[:], hid[:], ALU.add).then_inc(hid_added, 1)
            with pool.Fori(0, E // 2) as pair:
                e = pair * 2
                for u in range(2 * UE):
                    h_part = (slice(None), (u // HC) % 2, u % HC)
                    pool.wait_ge(high_made, e * UE + u + 1)
                    pool.tensor_tensor(h_low[h_part], hidden[:, u % G, :], h_high[h_part].bitcast(F32),
                                       ALU.subtract).then_inc(low_made, 1)

        @block.vector
        def _(dve):
            def split_weights(count, b):
                dve.tensor_copy(w_high[:, b, :], raw[:, b, :]).then_inc(weigh, 1)
                dve.wait_ge(weigh, count)
                dve.tensor_tensor(w_low[:, b, :], raw[:, b, :], w_high[:, b, :].bitcast(F32),
                                  ALU.subtract).then_inc(split, 1)

            def add(e, d):
                half, n = d // NC, d % NC
                x = slice(n * CH, (n + 1) * CH)
                dve.wait_ge(down, e * NC + d + 1 + 2 * NC)
                dve.tensor_tensor(weighted[:, n % 2, :], ps[:, D0 + n % 2, :], spread[:, half, x],
                                  ALU.mult).then_inc(c_split, 1)
                dve.wait_ge(c_split, e * NC + d + 2)
                dve.tensor_tensor(total[:, x], total[:, x], weighted[:, n % 2, :], ALU.add).then_inc(added, 1)

            def one_hot(scores, top, out):
                ch.then(dve.tensor_reduce(top[:], scores[:], AX.X, ALU.max))
                ch.then(dve.tensor_tensor(pick[:], scores[:], wide(top), ALU.is_equal))
                ch.then(dve.tensor_tensor(pick[:], pick[:], order[:], ALU.mult))
                ch.then(dve.tensor_reduce(rank[:], pick[:], AX.X, ALU.max))
                ch.then(dve.tensor_tensor(out[:], order[:], wide(rank), ALU.is_equal))

            ch = Chain(dve, chain)
            for t in range(T):
                last = dve.bn_stats(st[:, t, :], hid[:, t, :])
            ch.then(last)
            for t in range(T):
                last = dve.bn_aggr(mv[:, t, :], st[:, t, :])
            ch.then(last)
            ch.then(dve.tensor_tensor(var[:], mv[:, :, 0], mv[:, :, 0], ALU.mult))
            dve.scalar_tensor_tensor(out=var[:], in0=mv[:, :, 1], scalar=1e-6, in1=var[:],
                                     op0=ALU.add, op1=ALU.add).then_inc(var_ready, 1)
            dve.wait_ge(small_in, SMALL)
            dve.wait_ge(root_ready, 1)
            ch.then(dve.reciprocal(rstd[:], root[:]))
            for t in range(T):
                dve.scalar_tensor_tensor(out=normed[:, t, :], in0=hid[:, t, :], scalar=rstd[:, t:t + 1],
                                         in1=g2[:], op0=ALU.mult, op1=ALU.mult).then_inc(tok_ready, 1)
            dve.wait_ge(placed[0], 48)
            split_weights(1, 0)
            dve.wait_ge(scored, 1)
            ch.then(dve.tensor_copy(logits[:], ps[:, 4, 0:T * E].rearrange("p (t e) -> p t e", e=E)))
            one_hot(logits, best, picked)
            dve.tensor_tensor(ex[:], logits[:], wide(best), ALU.subtract).then_inc(shifted, 1)
            ch.then(dve.scalar_tensor_tensor(out=left[:], in0=picked[:], scalar=FLOOR, in1=logits[:],
                                             op0=ALU.mult, op1=ALU.add))
            one_hot(left, best2, second)
            ch.then(dve.tensor_tensor(picked[:], picked[:], second[:], ALU.add))
            dve.wait_ge(exped, 1)
            ch.then(dve.tensor_tensor(ex[:], ex[:], picked[:], ALU.mult))
            ch.then(dve.tensor_reduce(tot[:], ex[:], AX.X, ALU.add))
            ch.then(dve.reciprocal(tot[:], tot[:]))
            dve.tensor_tensor(combine[:], ex[:], wide(tot), ALU.mult).then_inc(combined, 1)

            dve.memset(total[:], 0.0).then_inc(c_split, 1)
            dve.memset(nothing[:, 0:1], 0.0).then_inc(mixed, G)
            dve.memset(nothing[:, 1:2], 0.0).then_inc(added, 2)
            dve.memset(nothing[:, 2:3], 0.0).then_inc(down, 2 * NC)
            dve.memset(nothing[:, 3:4], 0.0).then_inc(low_made, G)
            with dve.Fori(0, E // 2) as pair:
                e = pair * 2
                for half in range(2):
                    for n in range(NC):
                        for h in range(HC):
                            u = half * UE + n * HC + h
                            dve.wait_ge(silued, e * UE + u + 1)
                            dve.wait_ge(low_made, e * UE + u + 1)
                            dve.tensor_tensor(hidden[:, u % G, :], ps[:, 2 * (u % G) + 1, :], silu[:, u % G, :],
                                              ALU.mult).then_inc(mixed, 1)
                        if n == 1:
                            dve.wait_ge(spread_in[half], pair * 16 + 16)
                        if half * NC + n:
                            add(e, half * NC + n - 1)
                        if n == 1:
                            dve.wait_ge(placed[1 - half], pair * 48 + 48 * (half + 1))
                            split_weights(e + half + 2, 1 - half)
                add(e, 2 * NC - 1)
            dve.wait_ge(hid_added, 1)
            for n in range(NC):
                t = slice(n * TC, (n + 1) * TC)
                dve.wait_ge(back, n + 1)
                dve.tensor_tensor(acc[:, t, :], ps[:, n, :].rearrange("p (a b) -> p a b", a=TC), acc[:, t, :],
                                  ALU.add).then_inc(final, 1)


def build(nc, a, out):
    with ExitStack() as outer:
        core = Core(nc, outer)
        ps = outer.enter_context(nc.psum_tensor("psum", [P, 8, CH], F32))
        c = {"ident": core.sb("ident", [P, P]), "identb": core.sb("identb", [P, P], BF16),
             "future": core.sb("future", [P, P], BF16)}
        ident = c["ident"]
        x = core.sb("x", [P, T, P])
        xn = core.sb("xn", [P, T, P])
        cols = core.sb("cols", [P, S])
        values = core.sb("values", [P, T, P])
        hid = core.sb("hid", [P, T, P])
        attending = outer.enter_context(ExitStack())
        stacks = Core(nc, attending)
        c["qs"], c["ks"] = stacks.sb("qs", [P, 2, HQ, S], BF16), stacks.sb("ks", [P, 2, HQ, S], BF16)
        staged0, staged1 = core.sem("staged0"), core.sem("staged1")
        parts_dram = core.dram("parts", (2, 3, P, S), BF16)
        scratch = [[core.dram(f"maxima{n}", (NQ, NC, 2 * HQ * TC, P), BF16), core.dram(f"sums{n}", (NQ + 1, HQ, S), F32),
                    core.dram(f"rsums{n}", (NQ + 1, HQ, S), F32)] for n in range(2)]

        rows_dram = core.dram("combine_rows", (E, S), F32)

        def tokens(ap):
            return ap.rearrange("(t p) d -> p t d", p=P)

        def quad_rows(wo, dst):
            return [(dst[32 * g:32 * g + D, :, :], wo.rearrange("(q g d) n -> g d q n", q=NQ, g=HQ)[g])
                    for g in range(HQ)]

        with ExitStack() as ctx0:
            w0 = Core(nc, ctx0)
            wo = w0.sb("wo0", [P, NQ, P])
            bout = w0.sb("bout", [P, P])
            with ExitStack() as early:
                e0 = Core(nc, early)
                wqkv, bias, bias_v = e0.sb("wqkv", [P, 3 * P]), e0.sb("bias", [P, 2]), e0.sb("bias_v", [P, P])
                w_fc, w_proj = e0.sb("w_fc", [P, F0 // P, P]), e0.sb("w_proj", [P, F0])
                fbT, v, uT, gate = e0.sb("fbT", [RANK, RANK]), e0.sb("v", [RANK, P]), e0.sb("uT", [RANK, F0]), e0.sb("gate", [P, 1])
                weights = [(w_fc[:], a["w_fc"].rearrange("(g p) d -> p g d", p=P)), (w_proj[:], a["w_proj"]),
                           (fbT[:], a["fast_bT"]), (v[:], a["v"]), (uT[:], a["uT"]),
                           (gate[:], a["gate"].partition_broadcast(P))]
                others = [(x[:], tokens(a["x"])), (wqkv[:], a["Wqkv"]), (bias[:], a["bqk"]),
                          (bias_v[:], a["bv"].partition_broadcast(P)), (bout[:], a["bout"].partition_broadcast(P))]
                layer0_front(nc, e0, ps, c, others, weights, wo, quad_rows(a["Wout"], wo), wqkv, bias, bias_v, bout,
                             w_fc, w_proj, fbT, v, uT, gate, x, xn, cols, values, parts_dram, staged0)
            ctxu = w0.sb("ctx0", [P, NQ + 1, S])
            with ExitStack() as att:
                attention(nc, Core(nc, att), ps, "a0", parts_dram, values, c, ctxu, scratch[0], wo, x, x, staged0)

        with ExitStack() as ctx1:
            w1 = Core(nc, ctx1)
            wo = w1.sb("wo1", [P, NQ, P])
            with ExitStack() as early:
                e1 = Core(nc, early)
                wl, wf = e1.sb("wl", [P, 6, P]), e1.sb("wf", [P, 5, P])
                g1, blocks, heads = e1.sb("g1", [P, P]), e1.sb("blocks", [P, P]), e1.sb("heads", [P, H])
                tables = e1.sb("tables", [P, 2, S])
                by_token = e1.sb("by_token", [P, 2, T, D])
                sooner = [
                    *[(wl[:, i, :], a[n]) for i, n in enumerate(("Wq", "Wq_turned", "Wk", "Wk_turned", "Wv", "Wo"))],
                    (tables[:, 0, :], a["cos_pairs"]), (tables[:, 1, :], a["sin_pairs"]),
                    (by_token[:, 0], a["cos_tokens"].rearrange("(t p) d -> p t d", p=P)),
                    (by_token[:, 1], a["sin_tokens"].rearrange("(t p) d -> p t d", p=P)),
                    (g1[:], a["g1"].partition_broadcast(P))]
                later = [
                    *[(wf[:, i, :], a[n]) for i, n in enumerate(("wq", "wq_turned", "wk", "wk_turned", "wv"))],
                    (blocks[:], a["blocks"]), (heads[:], a["heads"])]
                second_tables = [(tables[:, 0, :], a["cos_halves"]), (tables[:, 1, :], a["sin_halves"])]
                layer1_front(nc, e1, ps, c, sooner, later, second_tables, wo, quad_rows(a["wo"], wo), wl, wf, tables, by_token,
                             g1, blocks, heads, x, xn, hid, cols, values, parts_dram, staged1)
            ctxu = w1.sb("ctx1", [P, NQ + 1, S])
            with ExitStack() as att:
                attention(nc, Core(nc, att), ps, "a1", parts_dram, values, c, ctxu, scratch[1], wo, xn, hid, staged1)

        attending.close()
        with ExitStack() as ctx2:
            w2 = Core(nc, ctx2)
            w_router, g2, order = w2.sb("w_router", [P, E]), w2.sb("g2", [P, P]), w2.sb("order", [P, T, E])
            small = [(w_router[:], a["w_router"]), (g2[:], a["g2"].partition_broadcast(P)),
                     (order[:], a["order"].partition_broadcast(P))]
            experts(nc, w2, ps, ident, small, hid, xn, cols, w_router, g2, order, a["wg"], a["wu"], a["wd"],
                    rows_dram, x, out)


def shape_tables():
    t = np.arange(S, dtype=np.float32)
    f = (1.0 / 10000.0 ** (np.arange(0, D, 2, dtype=np.float32) / D)).astype(np.float32)
    ang = np.einsum("i,j->ij", t, f)
    cos, sin = np.cos(ang).T, np.sin(ang).T
    head = np.arange(P) % D
    sign_pairs = np.where(head % 2, 1.0, -1.0)[:, None].astype(np.float32)
    sign_halves = np.where(head >= D // 2, 1.0, -1.0)[:, None].astype(np.float32)
    return {"cos_pairs": cos[head // 2], "sin_pairs": sin[head // 2] * sign_pairs,
            "cos_halves": cos[head % (D // 2)], "sin_halves": sin[head % (D // 2)] * sign_halves,
            "cos_tokens": cos.T[:, np.arange(D) // 2],
            "sin_tokens": sin.T[:, np.arange(D) // 2] * np.where(np.arange(D) % 2, 1.0, -1.0).astype(np.float32),
            "heads": (np.arange(P)[:, None] // D == np.arange(H)[None]).astype(np.float32),
            "blocks": (np.arange(P)[:, None] // D == np.arange(P)[None] // D).astype(np.float32),
            "order": np.tile(E - np.arange(E, dtype=np.float32), (T, 1))}


def kernel(**inputs):
    import concourse.bacc as _bacc
    from concourse.bass_utils import run_bass_kernel_spmd as _run

    i = {k: np.asarray(v) for k, v in inputs.items()}
    head = np.arange(P)
    pairs = head ^ 1
    halves = head ^ (D // 2)
    arrays = {
        "x": i["L0_attn_x"][0], "Wqkv": i["L0_attn_Wqkv"], "bqk": i["L0_attn_bqkv"][:2 * P].reshape(2, P).T,
        "bv": i["L0_attn_bqkv"][2 * P:], "Wout": i["L0_attn_Wout"],
        "bout": i["L0_attn_bout"], "fast_bT": i["L0_ffn_fast_b"].T, "w_fc": i["L0_ffn_w_fc"],
        "w_proj": i["L0_ffn_w_proj"], "uT": i["L0_ffn_u"].T, "v": i["L0_ffn_v"], "gate": i["L0_ffn_gate"].reshape(1),
        "Wq": i["L1_attn_Wq"], "Wq_turned": i["L1_attn_Wq"][:, pairs], "Wk": i["L1_attn_Wk"],
        "Wk_turned": i["L1_attn_Wk"][:, pairs], "Wv": i["L1_attn_Wv"], "Wo": i["L1_attn_Wo"],
        "wq": i["L1_ffn_wq"], "wq_turned": i["L1_ffn_wq"][:, halves], "wk": i["L1_ffn_wk"],
        "wk_turned": i["L1_ffn_wk"][:, halves], "wv": i["L1_ffn_wv"], "wo": i["L1_ffn_wo"],
        "w_router": i["L1_ffn_w_router"], "wg": i["L1_ffn_wg"], "wu": i["L1_ffn_wu"], "wd": i["L1_ffn_wd"],
        "g1": i["L1_ffn_g1"], "g2": i["L1_ffn_g2"], **shape_tables(),
    }
    nc = _bacc.Bacc("TRN2", target_bir_lowering=False, num_devices=1)
    feed, aps = {}, {}
    for name, arr in arrays.items():
        arr = np.ascontiguousarray(arr)
        feed[f"in_{name}"] = arr
        aps[name] = nc.dram_tensor(f"in_{name}", arr.shape, mybir.dt.from_np(arr.dtype), kind="ExternalInput").ap()
    out = nc.dram_tensor("out", (S, P), F32, kind="ExternalOutput").ap()
    build(nc, aps, out)
    r = _run(nc, [feed], core_ids=[0])
    return r.results[0]["out"].reshape(1, S, P)
```
